# Optimizing a Trainium2 kernel written in Bass

```python
import numpy as np
import jax
import jax.numpy as jnp

def _softmax(x, axis=-1):
    return jax.nn.softmax(x, axis=axis)

def _gelu(x):
    return jax.nn.gelu(x, approximate=True)

def _silu(x):
    return jax.nn.silu(x)

def _sigmoid(x):
    return jax.nn.sigmoid(x)

def _layernorm(x, axis=-1, eps=1e-05):
    m = jnp.mean(x, axis=axis, keepdims=True)
    v = jnp.var(x, axis=axis, keepdims=True)
    return (x - m) / jnp.sqrt(v + eps)

def _scatter_add(tgt, idx, src, axis=0):
    return tgt.at[idx].add(src)

def _segment_sum(src, seg, n):
    return jax.ops.segment_sum(src, seg, n)
kernel_name = 'mk_sandwich_d2_jaxref_r8_1597f1'

def setup_inputs(seed: int=0):
    np.random.seed(seed)
    _w = jnp.asarray

    def _L0_attn_setup():
        import jax, jax.numpy as jnp
        import numpy as np
        HID = 256
        H = 16
        QLR = 192
        KVLR = 64
        DN = 128
        DR = 64
        DV = 128
        DQ = DN + DR
        B = 2
        S = 256
        THETA = 10000.0
        EPS = 1e-06

        def rms_norm(x, w, eps=EPS):
            x32 = x.astype(jnp.float32)
            var = jnp.mean(x32 * x32, axis=-1, keepdims=True)
            return (w * (x32 * jax.lax.rsqrt(var + eps))).astype(x.dtype)

        def rotate_half(x):
            x1, x2 = jnp.split(x, 2, axis=-1)
            return jnp.concatenate((-x2, x1), axis=-1)

        def rope_tables(seq_len, dim, base=THETA):
            inv_freq = 1.0 / base ** (jnp.arange(0, dim, 2, dtype=jnp.float32) / dim)
            t = jnp.arange(seq_len, dtype=jnp.float32)
            freqs = jnp.outer(t, inv_freq)
            emb = jnp.concatenate((freqs, freqs), -1)
            return (jnp.cos(emb), jnp.sin(emb))
        key = jax.random.key(seed)
        ks = jax.random.split(key, 8)
        sd = lambda fan_in: 1.0 / np.sqrt(fan_in)
        return {'hidden_states': jax.random.normal(ks[0], (B, S, HID), jnp.float32), 'w_qa': jax.random.normal(ks[1], (QLR, HID), jnp.float32) * sd(HID), 'q_a_ln_w': jnp.ones((QLR,), jnp.float32), 'w_qb': jax.random.normal(ks[2], (H * DQ, QLR), jnp.float32) * sd(QLR), 'w_kva': jax.random.normal(ks[3], (KVLR + DR, HID), jnp.float32) * sd(HID), 'kv_a_ln_w': jnp.ones((KVLR,), jnp.float32), 'w_kvb': jax.random.normal(ks[4], (H * (DN + DV), KVLR), jnp.float32) * sd(KVLR), 'w_o': jax.random.normal(ks[5], (HID, H * DV), jnp.float32) * sd(H * DV)}
    _L0_attn_in = _L0_attn_setup()

    def _L0_ffn_setup():
        import jax, jax.numpy as jnp
        import numpy as np
        N_EXPERTS = 8
        TOP_K = 2
        N_GROUP = 4
        TOPK_GROUP = 2
        ROUTED_SCALE = 1.0

        def _group_limited_topk(scores):
            T, N = scores.shape
            E = N // N_GROUP
            group_scores = scores.reshape(T, N_GROUP, E).max(axis=-1)
            _, gidx = jax.lax.top_k(group_scores, TOPK_GROUP)
            gmask = jax.nn.one_hot(gidx, N_GROUP, dtype=scores.dtype).sum(1)
            smask = jnp.repeat(gmask, E, axis=1)
            masked = jnp.where(smask > 0, scores, jnp.zeros((), scores.dtype))
            topk_w, topk_i = jax.lax.top_k(masked, TOP_K)
            return (topk_w, topk_i)
        key = jax.random.key(seed)
        ks = jax.random.split(key, 8)
        B, S, H, F, FS, N = (2, 128, 256, 176, 352, N_EXPERTS)
        std = jnp.float32(0.02)
        return {'hidden_states': jax.random.normal(ks[0], (B, S, H), jnp.float32), 'gate_weight': jax.random.normal(ks[1], (N, H), jnp.float32) * std, 'gate_w': jax.random.normal(ks[2], (N, F, H), jnp.float32) * std, 'up_w': jax.random.normal(ks[3], (N, F, H), jnp.float32) * std, 'down_w': jax.random.normal(ks[4], (N, H, F), jnp.float32) * std, 'sh_gate_w': jax.random.normal(ks[5], (FS, H), jnp.float32) * std, 'sh_up_w': jax.random.normal(ks[6], (FS, H), jnp.float32) * std, 'sh_down_w': jax.random.normal(ks[7], (H, FS), jnp.float32) * std}
    _L0_ffn_in = _L0_ffn_setup()

    def _L1_attn_setup():
        import jax, jax.numpy as jnp
        import numpy as np
        C = 8.0

        def _linear_scan(alpha, xbeta):

            def combine(e1, e2):
                a1, b1 = e1
                a2, b2 = e2
                return (a2 * a1, a2 * b1 + b2)
            _, h = jax.lax.associative_scan(combine, (alpha, xbeta), axis=1)
            return h
        dim = 256
        B, T = (4, 512)
        key = jax.random.key(seed)
        k_x, k_wi, k_wg = jax.random.split(key, 3)
        std = dim ** (-0.5)
        x = jax.random.normal(k_x, (B, T, dim), dtype=jnp.float32)
        W_in = jax.random.normal(k_wi, (dim, dim), dtype=jnp.float32) * std
        b_in = jnp.zeros((dim,), dtype=jnp.float32)
        W_gate = jax.random.normal(k_wg, (dim, dim), dtype=jnp.float32) * std
        b_gate = jnp.zeros((dim,), dtype=jnp.float32)
        forget_lambda = jnp.linspace(-4.323, -9.0, dim, dtype=jnp.float32)
        return {'x': x, 'W_in': W_in, 'b_in': b_in, 'W_gate': W_gate, 'b_gate': b_gate, 'forget_lambda': forget_lambda}
    _L1_attn_in = _L1_attn_setup()

    def _L1_ffn_setup():
        import jax, jax.numpy as jnp
        import numpy as np
        DIM = 256
        HID = 704
        ZERO_POINT = 128.0

        def _qlinear(x, wq, scale):
            W = (wq.astype(jnp.float32) - ZERO_POINT) * scale[:, None]
            return jnp.einsum('bsd,hd->bsh', x, W)
        key = jax.random.key(seed)
        ks = jax.random.split(key, 7)
        B, S = (4, 256)
        sg = jax.random.uniform(ks[1], (HID,)) * (0.02 / np.sqrt(DIM)) + 0.0001
        su = jax.random.uniform(ks[3], (HID,)) * (0.02 / np.sqrt(DIM)) + 0.0001
        sd = jax.random.uniform(ks[5], (DIM,)) * (0.02 / np.sqrt(HID)) + 0.0001
        return {'x': jax.random.normal(ks[0], (B, S, DIM), dtype=jnp.float32), 'wq_gate': jax.random.randint(ks[2], (HID, DIM), 0, 32, dtype=jnp.int32), 's_gate': sg, 'wq_up': jax.random.randint(ks[4], (HID, DIM), 0, 32, dtype=jnp.int32), 's_up': su, 'wq_down': jax.random.randint(ks[6], (DIM, HID), 0, 32, dtype=jnp.int32), 's_down': sd}
    _L1_ffn_in = _L1_ffn_setup()
    _d = {'L0_attn_hidden_states': _L0_attn_in['hidden_states'], 'L0_attn_w_qa': _L0_attn_in['w_qa'], 'L0_attn_q_a_ln_w': _L0_attn_in['q_a_ln_w'], 'L0_attn_w_qb': _L0_attn_in['w_qb'], 'L0_attn_w_kva': _L0_attn_in['w_kva'], 'L0_attn_kv_a_ln_w': _L0_attn_in['kv_a_ln_w'], 'L0_attn_w_kvb': _L0_attn_in['w_kvb'], 'L0_attn_w_o': _L0_attn_in['w_o'], 'L0_ffn_gate_weight': _L0_ffn_in['gate_weight'], 'L0_ffn_gate_w': _L0_ffn_in['gate_w'], 'L0_ffn_up_w': _L0_ffn_in['up_w'], 'L0_ffn_down_w': _L0_ffn_in['down_w'], 'L0_ffn_sh_gate_w': _L0_ffn_in['sh_gate_w'], 'L0_ffn_sh_up_w': _L0_ffn_in['sh_up_w'], 'L0_ffn_sh_down_w': _L0_ffn_in['sh_down_w'], 'L1_attn_W_in': _L1_attn_in['W_in'], 'L1_attn_b_in': _L1_attn_in['b_in'], 'L1_attn_W_gate': _L1_attn_in['W_gate'], 'L1_attn_b_gate': _L1_attn_in['b_gate'], 'L1_attn_forget_lambda': _L1_attn_in['forget_lambda'], 'L1_ffn_wq_gate': _L1_ffn_in['wq_gate'], 'L1_ffn_s_gate': _L1_ffn_in['s_gate'], 'L1_ffn_wq_up': _L1_ffn_in['wq_up'], 'L1_ffn_s_up': _L1_ffn_in['s_up'], 'L1_ffn_wq_down': _L1_ffn_in['wq_down'], 'L1_ffn_s_down': _L1_ffn_in['s_down']}
    _x0 = _d['L0_attn_hidden_states']
    _d['L0_attn_hidden_states'] = jax.random.normal(jax.random.fold_in(jax.random.key(seed), 1), (1, 2048, 256), dtype=_x0.dtype)
    del _x0
    return _d

def reference(L0_attn_hidden_states, L0_attn_w_qa, L0_attn_q_a_ln_w, L0_attn_w_qb, L0_attn_w_kva, L0_attn_kv_a_ln_w, L0_attn_w_kvb, L0_attn_w_o, L0_ffn_gate_weight, L0_ffn_gate_w, L0_ffn_up_w, L0_ffn_down_w, L0_ffn_sh_gate_w, L0_ffn_sh_up_w, L0_ffn_sh_down_w, L1_attn_W_in, L1_attn_b_in, L1_attn_W_gate, L1_attn_b_gate, L1_attn_forget_lambda, L1_ffn_wq_gate, L1_ffn_s_gate, L1_ffn_wq_up, L1_ffn_s_up, L1_ffn_wq_down, L1_ffn_s_down):

    def _L0_attn_ref(hidden_states, w_qa, q_a_ln_w, w_qb, w_kva, kv_a_ln_w, w_kvb, w_o):
        import jax, jax.numpy as jnp
        import numpy as np
        HID = 256
        H = 16
        QLR = 192
        KVLR = 64
        DN = 128
        DR = 64
        DV = 128
        DQ = DN + DR
        B = 2
        S = 256
        THETA = 10000.0
        EPS = 1e-06

        def rms_norm(x, w, eps=EPS):
            x32 = x.astype(jnp.float32)
            var = jnp.mean(x32 * x32, axis=-1, keepdims=True)
            return (w * (x32 * jax.lax.rsqrt(var + eps))).astype(x.dtype)

        def rotate_half(x):
            x1, x2 = jnp.split(x, 2, axis=-1)
            return jnp.concatenate((-x2, x1), axis=-1)

        def rope_tables(seq_len, dim, base=THETA):
            inv_freq = 1.0 / base ** (jnp.arange(0, dim, 2, dtype=jnp.float32) / dim)
            t = jnp.arange(seq_len, dtype=jnp.float32)
            freqs = jnp.outer(t, inv_freq)
            emb = jnp.concatenate((freqs, freqs), -1)
            return (jnp.cos(emb), jnp.sin(emb))
        b, s, _ = hidden_states.shape
        scale = DQ ** (-0.5)
        cos, sin = rope_tables(s, DR)
        cq = rms_norm(hidden_states @ w_qa.T, q_a_ln_w)
        q = (cq @ w_qb.T).reshape(b, s, H, DQ).transpose(0, 2, 1, 3)
        q_nope, q_pe = (q[..., :DN], q[..., DN:])
        q_pe = q_pe * cos + rotate_half(q_pe) * sin
        ckv = hidden_states @ w_kva.T
        k_pe = ckv[..., KVLR:].reshape(b, s, 1, DR).transpose(0, 2, 1, 3)
        k_pe = k_pe * cos + rotate_half(k_pe) * sin
        ckv_l = rms_norm(ckv[..., :KVLR], kv_a_ln_w)
        kv = (ckv_l @ w_kvb.T).reshape(b, s, H, DN + DV).transpose(0, 2, 1, 3)
        k_nope, v = (kv[..., :DN], kv[..., DN:])
        q_full = jnp.concatenate([q_nope, q_pe], axis=-1)
        k_full = jnp.concatenate([k_nope, jnp.broadcast_to(k_pe, (b, H, s, DR))], axis=-1)
        scores = jnp.einsum('bhqd,bhkd->bhqk', q_full, k_full) * scale
        causal = jnp.triu(jnp.ones((s, s), dtype=bool), k=1)
        scores = jnp.where(causal, -jnp.inf, scores)
        attn = jax.nn.softmax(scores.astype(jnp.float32), axis=-1).astype(q_full.dtype)
        out = jnp.einsum('bhqk,bhkd->bhqd', attn, v)
        out = out.transpose(0, 2, 1, 3).reshape(b, s, H * DV)
        return out @ w_o.T

    def _L0_ffn_ref(hidden_states, gate_weight, gate_w, up_w, down_w, sh_gate_w, sh_up_w, sh_down_w):
        import jax, jax.numpy as jnp
        import numpy as np
        N_EXPERTS = 8
        TOP_K = 2
        N_GROUP = 4
        TOPK_GROUP = 2
        ROUTED_SCALE = 1.0

        def _group_limited_topk(scores):
            T, N = scores.shape
            E = N // N_GROUP
            group_scores = scores.reshape(T, N_GROUP, E).max(axis=-1)
            _, gidx = jax.lax.top_k(group_scores, TOPK_GROUP)
            gmask = jax.nn.one_hot(gidx, N_GROUP, dtype=scores.dtype).sum(1)
            smask = jnp.repeat(gmask, E, axis=1)
            masked = jnp.where(smask > 0, scores, jnp.zeros((), scores.dtype))
            topk_w, topk_i = jax.lax.top_k(masked, TOP_K)
            return (topk_w, topk_i)
        B, S, H = hidden_states.shape
        h = hidden_states.reshape(-1, H)
        logits = h.astype(jnp.float32) @ gate_weight.astype(jnp.float32).T
        scores = jax.nn.softmax(logits, axis=-1)
        topk_w, topk_i = _group_limited_topk(scores)
        topk_w = (topk_w * ROUTED_SCALE).astype(h.dtype)
        wmat = (jax.nn.one_hot(topk_i, N_EXPERTS, dtype=topk_w.dtype) * topk_w[..., None]).sum(axis=1)
        g = jnp.einsum('th,nfh->ntf', h, gate_w)
        u = jnp.einsum('th,nfh->ntf', h, up_w)
        e = jnp.einsum('ntf,nhf->nth', jax.nn.silu(g) * u, down_w)
        routed = jnp.einsum('nth,tn->th', e, wmat)
        sg = h @ sh_gate_w.T
        su = h @ sh_up_w.T
        shared = jax.nn.silu(sg) * su @ sh_down_w.T
        return (routed + shared).reshape(B, S, H)

    def _L1_attn_ref(x, W_in, b_in, W_gate, b_gate, forget_lambda):
        import jax, jax.numpy as jnp
        import numpy as np
        C = 8.0

        def _linear_scan(alpha, xbeta):

            def combine(e1, e2):
                a1, b1 = e1
                a2, b2 = e2
                return (a2 * a1, a2 * b1 + b2)
            _, h = jax.lax.associative_scan(combine, (alpha, xbeta), axis=1)
            return h
        input_gate = jnp.einsum('btd,ed->bte', x, W_in) + b_in
        recurrence_gate = jnp.einsum('btd,ed->bte', x, W_gate) + b_gate
        alpha = jnp.exp(-C * jax.nn.softplus(forget_lambda) * jax.nn.sigmoid(recurrence_gate))
        beta = jnp.sqrt(1.0 - alpha ** 2 + 1e-06)
        xbeta = beta * jax.nn.sigmoid(input_gate) * x
        return _linear_scan(alpha, xbeta)

    def _L1_ffn_ref(x, wq_gate, s_gate, wq_up, s_up, wq_down, s_down):
        import jax, jax.numpy as jnp
        import numpy as np
        DIM = 256
        HID = 704
        ZERO_POINT = 128.0

        def _qlinear(x, wq, scale):
            W = (wq.astype(jnp.float32) - ZERO_POINT) * scale[:, None]
            return jnp.einsum('bsd,hd->bsh', x, W)
        gate = _qlinear(x, wq_gate, s_gate)
        gate = jax.nn.silu(gate)
        up = _qlinear(x, wq_up, s_up)
        return _qlinear(gate * up, wq_down, s_down)
    x = L0_attn_hidden_states
    x = x + _layernorm(_L0_attn_ref(_layernorm(x, axis=-1), L0_attn_w_qa, L0_attn_q_a_ln_w, L0_attn_w_qb, L0_attn_w_kva, L0_attn_kv_a_ln_w, L0_attn_w_kvb, L0_attn_w_o), axis=-1)
    x = x + _layernorm(_L0_ffn_ref(_layernorm(x, axis=-1), L0_ffn_gate_weight, L0_ffn_gate_w, L0_ffn_up_w, L0_ffn_down_w, L0_ffn_sh_gate_w, L0_ffn_sh_up_w, L0_ffn_sh_down_w), axis=-1)
    x = x + _layernorm(_L1_attn_ref(_layernorm(x, axis=-1), L1_attn_W_in, L1_attn_b_in, L1_attn_W_gate, L1_attn_b_gate, L1_attn_forget_lambda), axis=-1)
    x = x + _layernorm(_L1_ffn_ref(_layernorm(x, axis=-1), L1_ffn_wq_gate, L1_ffn_s_gate, L1_ffn_wq_up, L1_ffn_s_up, L1_ffn_wq_down, L1_ffn_s_down), axis=-1)
    return x

_drawn_inputs = setup_inputs


def setup_inputs(seed=0):
    import zlib

    import numpy as np

    out = dict(_drawn_inputs(seed))
    spreads = {'L0_attn_q_a_ln_w': (1.0, 0.2),
     'L0_attn_kv_a_ln_w': (1.0, 0.2),
     'L1_attn_b_in': (0.0, 0.413),
     'L1_attn_b_gate': (0.0, 0.8)}
    factors = {}
    for name, (base, spread) in spreads.items():
        noise = np.random.default_rng([zlib.crc32(name.encode()), seed]).standard_normal(out[name].shape)
        drawn = base * np.exp(spread * noise) if base else spread * noise
        out[name] = jnp.asarray(drawn.astype(out[name].dtype))
    for name, factor in factors.items():
        out[name] = (out[name] * factor).astype(out[name].dtype)
    return out
```

```python
from contextlib import ExitStack

import numpy as np
import concourse.bass as bass
from concourse import mybir

F32 = mybir.dt.float32
F32R = mybir.dt.float32r
BF16 = mybir.dt.bfloat16
F16 = mybir.dt.float16
I32 = mybir.dt.int32
ALU = mybir.AluOpType
ACT = mybir.ActivationFunctionType
AX = mybir.AxisListType

P = 128
T = 2048
D = 256
KD = D // P
NT = T // P
BT = 512
NB = T // BT
TPB = BT // P
H, QL, KVL, DN, DR, DV = 16, 192, 64, 128, 64, 128
DQ = KVL + DR
LAT = QL + KVL + DR
SCALE = float(DN + DR) ** -0.5
LN_EPS, RMS_EPS = 1e-5, 1e-6
MASKED = -1e30
NE, FE, FS = 8, 176, 352
FR = NE * FE
FM = FR + FS
NFM = -(-FM // P)
FQ = 704
NFQ = -(-FQ // P)
ZERO_POINT = 128.0
LRU_C = 8.0
LOG1P_TERMS = 9


class Chain:

    def __init__(self, eng, sem):
        self.eng, self.sem, self.n = eng, sem, 0

    def inc(self, ins):
        self.n += 1
        ins.then_inc(self.sem, 1)

    def wait(self):
        self.eng.wait_ge(self.sem, self.n)


def f(ap):
    return ap.bitcast(F32)


def build(nc, x, w_lat, w_qn, w_qpe, w_kn, w_v, w_o, q_ln, kv_ln, cos2, sin2, gw, wg, wu, wd, sel,
          l_in, l_gate, l_b, l_lam, qg, qu, qd, sg, su, sd, out):
    with ExitStack() as whole:
        sems = {}

        def sem(name):
            if name not in sems:
                sems[name] = whole.enter_context(nc.semaphore(name))
            return sems[name]

        used = {}

        def own(name):
            used[name] = used.get(name, 0) + 1
            return f"{name}_{used[name]}"

        def sb(ctx, name, shape, dt=F32):
            return ctx.enter_context(nc.sbuf_tensor(own(name), shape, dt))

        def ps(ctx, name, shape, dt=F32):
            return ctx.enter_context(nc.psum_tensor(own(name), shape, dt))

        def phase_end():
            nums = sorted(s.num for s in sems.values())
            nc.all_engine_barrier(sems_to_clear=range(nums[0], nums[-1] + 1))

        for name in ("dma_x", "dma_w", "dma_w2", "dma_w3", "dma_out", "gp", "dv", "ac", "a1", "a2", "a3", "a4", "p1", "p2", "p3", "p4", "p5",
                     "v1", "v2", "v3", "v4", "v5", "v6", "g1", "g2", "g3"):
            sem(name)

        X = sb(whole, "X", [P, NT, D])
        ident = sb(whole, "ident", [P, P])
        identb = sb(whole, "identb", [P, P], BF16)
        maskb = sb(whole, "maskb", [P, P], BF16)
        mhalf = sb(whole, "mhalf", [P, NT * 2])
        stats = sb(whole, "stats", [P, NT, 6])
        mv = sb(whole, "mv", [P, NT, 2])
        rs = sb(whole, "rs", [P, NT])
        nmr = sb(whole, "nmr", [P, NT])

        def pool_rsqrt(pool, ch, dst, src, eps, scale=1.0):
            ch.inc(pool.tensor_scalar(dst, src, scale, eps, ALU.mult, ALU.add))
            ch.wait()
            return pool.tensor_tensor(dst, dst, mhalf[:, 0:dst.shape[1]], ALU.pow)

        def add_normed(dve, ch, t, y, tmp, varied="v2", read="v5"):
            ch.inc(dve.bn_stats(stats[:, t, :], y))
            ch.wait()
            dve.bn_aggr(mv[:, t, :], stats[:, t, :]).then_inc(sem(varied), 1)
            dve.wait_ge(sem("g1"), t + 1)
            ch.inc(dve.scalar_tensor_tensor(out=nmr[:, t:t + 1], in0=mv[:, t, 0:1], scalar=-1.0, in1=rs[:, t:t + 1],
                                            op0=ALU.mult, op1=ALU.mult))
            ch.wait()
            dve.tensor_scalar(tmp, y, rs[:, t:t + 1], nmr[:, t:t + 1], ALU.mult, ALU.add).then_inc(sem(read), 1)
            dve.wait_ge(sem(read), t + 1)
            dve.tensor_tensor(X[:, t, :], X[:, t, :], tmp, ALU.add).then_inc(sem("v6"), 1)

        with ExitStack() as att:
            kT_hi = sb(att, "kT_hi", [P, T], F32R)
            kT_lo = sb(att, "kT_lo", [P, T], F32R)
            c_hi = sb(att, "c_hi", [P, NT, 66], F16)
            c_lo = sb(att, "c_lo", [P, NT, 66], F16)
            cqT0 = sb(att, "cqT0", [P, T])
            cqT1 = sb(att, "cqT1", [QL - P, T])
            Wq0 = sb(att, "Wq0", [P, H * DQ])
            Wq1 = sb(att, "Wq1", [QL - P, H * DQ])
            Wvo_hi = sb(att, "Wvo_hi", [P, H // 2, D], F32R)
            Wvo_lo = sb(att, "Wvo_lo", [P, H // 2, D], F32R)
            cs = sb(att, "cs", [P, NT, DR])
            sn = sb(att, "sn", [P, NT, DR])
            with ExitStack() as pre:
                wl = sb(pre, "wl", [P, KD, LAT])
                wqn = sb(pre, "wqn", [P, H, QL])
                wqp0 = sb(pre, "wqp0", [P, H, DR])
                wqp1 = sb(pre, "wqp1", [QL - P, H, DR])
                wk = sb(pre, "wk", [P, H, KVL])
                wv = sb(pre, "wv", [P, H, KVL])
                wo = sb(pre, "wo", [P, H, D])
                qln0 = sb(pre, "qln0", [P, 1])
                qln1 = sb(pre, "qln1", [QL - P, 1])
                kln = sb(pre, "kln", [P, KVL])
                xn = sb(pre, "xn", [P, 2, D])
                xnT = sb(pre, "xnT", [P, 2, KD, P])
                lat = sb(pre, "lat", [P, 2, LAT])
                latn = sb(pre, "latn", [P, 2, LAT])
                junk = sb(pre, "junk", [P, QL])
                ss = sb(pre, "ss", [P, NT, 2])
                rr = sb(pre, "rr", [P, NT, 2])
                rt = sb(pre, "rt", [P, 2, DR])
                pt = [ps(pre, f"pt{b}", [P, 512]) for b in range(2)]
                pl = [ps(pre, f"pl{b}", [P, 512]) for b in range(2)]
                pk = [ps(pre, f"pk{b}", [P, 512]) for b in range(2)]
                pa = [ps(pre, f"pa{b}", [P, 512]) for b in range(2)]
                with nc.Block() as block:

                    @block.sync
                    def _(sp):
                        for g in range(4):
                            sp.dma_start(X[:, 4 * g:4 * g + 4, :], x[:, 4 * g:4 * g + 4, :]).then_inc(sem("dma_x"), 16)
                        sp.dma_start(wl[:], w_lat).then_inc(sem("dma_w"), 16)
                        sp.dma_start(cs[:], cos2).then_inc(sem("dma_w2"), 16)
                        sp.dma_start(sn[:], sin2).then_inc(sem("dma_w2"), 16)

                    @block.scalar
                    def _(act):
                        w3 = sem("dma_w3")
                        act.dma_start(kln[:], kv_ln.partition_broadcast(P)).then_inc(w3, 16)
                        act.dma_start(qln0[:], q_ln[0:P, :]).then_inc(w3, 16)
                        act.dma_start(qln1[:], q_ln[P:QL, :]).then_inc(w3, 16)
                        act.dma_start(wk[:], w_kn).then_inc(w3, 16)
                        act.dma_start(wqn[:], w_qn).then_inc(w3, 16)
                        act.dma_start(wqp0[:], w_qpe[0:P]).then_inc(w3, 16)
                        act.dma_start(wqp1[:], w_qpe[P:QL]).then_inc(w3, 16)
                        act.dma_start(wv[:], w_v).then_inc(w3, 16)
                        act.dma_start(wo[:], w_o).then_inc(w3, 16)
                        for t in range(NT):
                            b = t % 2
                            act.wait_ge(sem("p1"), t + 1)
                            if t >= 2:
                                act.wait_ge(sem("p2"), t - 1)
                            act.activation(xnT[:, b], pt[b][:, 0:D].rearrange("p (k n) -> p k n", k=KD), ACT.Copy).then_inc(sem("a1"), 1)
                            act.wait_ge(sem("p2"), t + 1)
                            if t:
                                act.wait_ge(sem("a2"), t)
                            act.activation(junk[:], pl[b][:, 0:QL], ACT.Square, accum_out=ss[:, t, 0:1]).then_inc(sem("ac"), 1)
                            act.wait_ge(sem("ac"), t + 1)
                            act.activation(junk[:, 0:KVL], pl[b][:, QL:QL + KVL], ACT.Square,
                                           accum_out=ss[:, t, 1:2]).then_inc(sem("a2"), 1)
                        for j in range(H // 2):
                            act.wait_ge(sem("p5"), j + 1)
                            act.activation(Wvo_hi[0:64, j], pa[j % 2][0:64, 0:D], ACT.Copy).then_inc(sem("a3"), 1)
                            act.activation(Wvo_hi[64:128, j], pa[j % 2][64:128, D:2 * D], ACT.Copy).then_inc(sem("a3"), 1)

                    @block.gpsimd
                    def _(pool):
                        ch = Chain(pool, sem("gp"))
                        pool.memset(mhalf[:], -0.5)
                        pool.memset(ident[:], 0.0)
                        ch.inc(pool.memset(identb[:], 0.0))
                        ch.inc(pool.memset(maskb[:], 0.0))
                        pool.memset(c_hi[:, :, 64:65], 1.0)
                        pool.memset(c_hi[:, :, 65:66], 0.0)
                        ch.inc(pool.memset(c_lo[:, :, 64:66], 0.0))
                        ch.wait()
                        ch.inc(pool.affine_select(out=ident[:], in_=ident[:], compare_op=ALU.not_equal, fill=1.0, base=0,
                                                  pattern=[[-1, P]], channel_multiplier=1))
                        ch.inc(pool.affine_select(out=identb[:], in_=identb[:], compare_op=ALU.not_equal, fill=1.0, base=0,
                                                  pattern=[[-1, P]], channel_multiplier=1))
                        ch.inc(pool.affine_select(out=maskb[:], in_=maskb[:], compare_op=ALU.is_ge, fill=MASKED, base=0,
                                                  pattern=[[-1, P]], channel_multiplier=1))
                        ch.wait()
                        pool.memset(rt[:], 0.0).then_inc(sem("g3"), 1)

                        def deviation(t):
                            pool.wait_ge(sem("v1"), t + 1)
                            pool_rsqrt(pool, ch, rs[:, t:t + 1], mv[:, t, 1:2], LN_EPS).then_inc(sem("g1"), 1)

                        deviation(0)
                        for t in range(NT):
                            if t + 1 < NT:
                                deviation(t + 1)
                            pool.wait_ge(sem("a2"), t + 1)
                            ch.inc(pool.tensor_scalar(rr[:, t, 0:1], ss[:, t, 0:1], 1.0 / QL, RMS_EPS, ALU.mult, ALU.add))
                            ch.inc(pool.tensor_scalar(rr[:, t, 1:2], ss[:, t, 1:2], 1.0 / KVL, RMS_EPS, ALU.mult, ALU.add))
                            ch.wait()
                            pool.tensor_tensor(rr[:, t, :], rr[:, t, :], mhalf[:, 0:2], ALU.pow).then_inc(sem("g2"), 1)

                    @block.vector
                    def _(dve):
                        ch = Chain(dve, sem("dv"))

                        def normed(t):
                            dve.wait_ge(sem("dma_x"), 64)
                            ch.inc(dve.bn_stats(stats[:, t, :], X[:, t, :]))
                            ch.wait()
                            dve.bn_aggr(mv[:, t, :], stats[:, t, :]).then_inc(sem("v1"), 1)
                            dve.wait_ge(sem("g1"), t + 1)
                            if t >= 2:
                                dve.wait_ge(sem("p1"), t - 1)
                            dve.tensor_scalar(xn[:, t % 2, :], X[:, t, :], mv[:, t, 0:1], rs[:, t:t + 1],
                                              ALU.subtract, ALU.mult).then_inc(sem("v2"), 1)

                        normed(0)
                        for t in range(NT):
                            b = t % 2
                            if t + 1 < NT:
                                normed(t + 1)
                            if t == 0:
                                dve.wait_ge(sem("dma_w2"), 32)
                            dve.wait_ge(sem("g2"), t + 1)
                            if t >= 2:
                                dve.wait_ge(sem("p3"), t - 1)
                            L, N = pl[b], latn[:, b]
                            dve.tensor_scalar(N[:, 0:QL], L[:, 0:QL], rr[:, t, 0:1], None, ALU.mult)
                            dve.tensor_scalar(N[:, QL:QL + KVL], L[:, QL:QL + KVL], rr[:, t, 1:2], None, ALU.mult)
                            ch.inc(dve.tensor_copy(lat[:, b, 0:DR], L[:, QL + KVL:LAT]))
                            ch.wait()
                            r, kp = rt[:, b], lat[:, b, 0:DR]
                            if t == 0:
                                dve.wait_ge(sem("g3"), 1)
                            dve.tensor_tensor(r[:, 0:32], kp[:, 32:64], sn[:, t, 0:32], ALU.mult)
                            ch.inc(dve.tensor_tensor(r[:, 32:64], kp[:, 0:32], sn[:, t, 32:64], ALU.mult))
                            ch.inc(dve.tensor_tensor(lat[:, b, DR:2 * DR], kp, cs[:, t, :], ALU.mult))
                            dve.tensor_copy(c_hi[:, t, 0:KVL], N[:, QL:QL + KVL]).then_inc(sem("dv"), 1)
                            ch.n += 1
                            ch.wait()
                            dve.tensor_tensor(N[:, QL + KVL:LAT], lat[:, b, DR:2 * DR], r, ALU.add).then_inc(sem("v3"), 1)
                            ch.inc(dve.tensor_tensor(c_lo[:, t, 0:KVL], N[:, QL:QL + KVL], c_hi[:, t, 0:KVL], ALU.subtract))
                            dve.wait_ge(sem("p3"), t + 1)
                            sl = slice(t * P, (t + 1) * P)
                            dve.tensor_copy(cqT0[:, sl], pk[b][:, 0:P]).then_inc(sem("v4"), 1)
                            dve.tensor_copy(cqT1[:, sl], pk[b][0:64, P:2 * P]).then_inc(sem("v4"), 1)
                            ch.inc(dve.tensor_copy(kT_hi[:, sl], pk[b][:, 2 * P:3 * P]))
                            ch.wait()
                            dve.tensor_tensor(kT_lo[:, sl], pk[b][:, 2 * P:3 * P], f(kT_hi[:, sl]), ALU.subtract).then_inc(sem("v4"), 1)
                        dve.wait_ge(sem("dma_w3"), 16 * 9)
                        for w in (wk, wv):
                            dve.tensor_tensor(w[:], w[:], kln[:].unsqueeze(1).to_broadcast([P, H, KVL]), ALU.mult).then_inc(sem("v5"), 1)
                        q0 = Wq0[:].rearrange("p (h d) -> p h d", h=H)
                        q1 = Wq1[:].rearrange("p (h d) -> p h d", h=H)
                        dve.tensor_scalar(q0[:, :, KVL:DQ], wqp0[:], qln0[:], None, ALU.mult)
                        dve.tensor_scalar(q1[:, :, KVL:DQ], wqp1[:], qln1[:], None, ALU.mult)
                        for g in range(2):
                            dve.wait_ge(sem("p4"), g + 1)
                            h8 = slice(8 * g, 8 * g + 8)
                            dve.tensor_scalar(q0[:, h8, 0:KVL], pt[g][:].rearrange("p (h d) -> p h d", h=8), qln0[:], None, ALU.mult)
                            dve.tensor_scalar(q1[:, h8, 0:KVL], pl[g][0:64, :].rearrange("p (h d) -> p h d", h=8), qln1[:], None, ALU.mult)
                        for j in range(H // 2):
                            dve.wait_ge(sem("a3"), 2 * j + 2)
                            dve.tensor_tensor(Wvo_lo[0:64, j], pa[j % 2][0:64, 0:D], f(Wvo_hi[0:64, j]), ALU.subtract)
                            dve.tensor_tensor(Wvo_lo[64:128, j], pa[j % 2][64:128, D:2 * D], f(Wvo_hi[64:128, j]),
                                              ALU.subtract).then_inc(sem("v6"), 1)

                    @block.tensor
                    def _(pe):
                        def transposed(t):
                            if t == 0:
                                pe.wait_ge(sem("g3"), 1)
                            pe.wait_ge(sem("v2"), t + 1)
                            if t >= 2:
                                pe.wait_ge(sem("a1"), t - 1)
                            for k in range(KD):
                                m = pe.transpose(pt[t % 2][:, k * P:(k + 1) * P], xn[:, t % 2, k * P:(k + 1) * P], ident[:])
                            m.then_inc(sem("p1"), 1)

                        transposed(0)
                        pe.wait_ge(sem("dma_w"), 16)
                        for t in range(NT):
                            b = t % 2
                            if t + 1 < NT:
                                transposed(t + 1)
                            pe.wait_ge(sem("a1"), t + 1)
                            if t >= 2:
                                pe.wait_ge(sem("v3"), t - 1)
                                pe.wait_ge(sem("a2"), t - 1)
                            for k in range(KD):
                                m = pe.matmul(pl[b][:, 0:LAT], xnT[:, b, k, :], wl[:, k, :], start=(k == 0), stop=(k == KD - 1))
                            m.then_inc(sem("p2"), 1)
                            pe.wait_ge(sem("v3"), t + 1)
                            if t >= 2:
                                pe.wait_ge(sem("v4"), 3 * (t - 1))
                            N = latn[:, b]
                            pe.transpose(pk[b][:, 0:P], N[:, 0:P], ident[:])
                            pe.transpose(pk[b][0:64, P:2 * P], N[:, P:QL], ident[:])
                            pe.transpose(pk[b][:, 2 * P:3 * P], N[:, QL:LAT], ident[:]).then_inc(sem("p3"), 1)
                        pe.wait_ge(sem("v5"), 2)
                        pe.wait_ge(sem("v4"), 3 * NT)
                        for g in range(2):
                            for j in range(8):
                                h = 8 * g + j
                                pe.matmul(pt[g][:, j * 64:(j + 1) * 64], wqn[:, h, 0:P], wk[:, h, :], start=True, stop=True)
                                m = pe.matmul(pl[g][0:64, j * 64:(j + 1) * 64], wqn[:, h, P:QL], wk[:, h, :], start=True, stop=True)
                            m.then_inc(sem("p4"), 1)
                        for j in range(H // 2):
                            if j >= 2:
                                pe.wait_ge(sem("v6"), j - 1)
                            pair = wv[:, 2 * j:2 * j + 2, :]
                            pe.matmul(pa[j % 2][:, 0:D], pair, wo[:, 2 * j, :], start=True, stop=True)
                            pe.matmul(pa[j % 2][:, D:2 * D], pair, wo[:, 2 * j + 1, :], start=True, stop=True).then_inc(sem("p5"), 1)

                phase_end()

            O = sb(att, "O", [P, NT, H * KVL])
            with ExitStack() as loop:
                qs = sb(loop, "qs", [P, 2, DQ])
                qr = sb(loop, "qr", [P, 2, DQ])
                qt = sb(loop, "qt", [P, 2, DR])
                qT_hi = sb(loop, "qT_hi", [P, 2, P], F32R)
                qT_lo = sb(loop, "qT_lo", [P, 2, P], F32R)
                pr = sb(loop, "pr", [P, 2, T])
                pT_hi = sb(loop, "pT_hi", [P, 3, BT], F16)
                pT_lo = sb(loop, "pT_lo", [P, 3, BT], F16)
                cmx = sb(loop, "cmx", [P, 2, 4])
                nmx = sb(loop, "nmx", [P, 2])
                rl = sb(loop, "rl", [P, 2])
                pS = [ps(loop, f"pS{b}", [P, BT]) for b in range(4)]
                pT = [ps(loop, f"pT{b}", [P, BT]) for b in range(2)]
                pO = ps(loop, "pO", [P, BT])
                pQ = ps(loop, "pQ", [P, BT])
                chunks = [[(c, min(4, i + 1 - 4 * c)) for c in range(i // 4 + 1)] for i in range(NT)]
                first = [sum(len(chunks[j]) for j in range(i)) for i in range(NT + 1)]

                with nc.Fori(0, H) as h:
                    with nc.Block() as block:

                        @block.tensor
                        def _(pe):
                            def project(i):
                                if i >= 1:
                                    pe.wait_ge(sem("a2"), i)
                                    pe.wait_ge(sem("v2"), i)
                                sl = slice(i * P, (i + 1) * P)
                                pe.matmul(pQ[:, 0:DQ], cqT0[:, sl], Wq0[:, bass.ds(h * DQ, DQ)], start=True, stop=False)
                                pe.matmul(pQ[:, 0:DQ], cqT1[:, sl], Wq1[:, bass.ds(h * DQ, DQ)],
                                          start=False, stop=True).then_inc(sem("p1"), 1)

                            def turn(i):
                                pe.wait_ge(sem("g1"), i + 1)
                                pe.transpose(pQ[:, P:2 * P], qr[:, i % 2, :], ident[:]).then_inc(sem("p2"), 1)

                            def scores(i, c, n):
                                at = first[i] + c
                                if c == 0:
                                    pe.wait_ge(sem("a2"), i + 1)
                                    pe.wait_ge(sem("v2"), i + 1)
                                if at >= 4:
                                    pe.wait_ge(sem("a3"), at - 3)
                                w = max(256, n * P)
                                o, ks = pS[at % 4][:, 0:w], slice(c * BT, c * BT + w)
                                last = c == len(chunks[i]) - 1
                                pe.matmul(o, qT_hi[:, i % 2], kT_hi[:, ks], start=True, stop=False)
                                pe.matmul(o, qT_hi[:, i % 2], kT_lo[:, ks], start=False, stop=False)
                                if last:
                                    pe.matmul(pS[at % 4][:, (n - 1) * P:n * P], identb[:], maskb[:], start=False, stop=False,
                                              skip_group_check=True)
                                pe.matmul(o, qT_lo[:, i % 2], kT_hi[:, ks], start=False, stop=True).then_inc(sem("p3"), 1)

                            def turn_probs(i, c, n):
                                at = first[i] + c
                                pe.wait_ge(sem("a3"), at + 1)
                                if at >= 2:
                                    pe.wait_ge(sem("a4"), at - 1)
                                    pe.wait_ge(sem("v4"), at - 1)
                                for k in range(n):
                                    m = pe.transpose(pT[at % 2][:, k * P:(k + 1) * P],
                                                     pr[:, i % 2, (4 * c + k) * P:(4 * c + k + 1) * P], ident[:])
                                m.then_inc(sem("p4"), 1)

                            def values(i, c, n):
                                at = first[i] + c
                                pe.wait_ge(sem("a4"), at + 1)
                                pe.wait_ge(sem("v4"), at + 1)
                                if c == 0 and i >= 1:
                                    pe.wait_ge(sem("v5"), i)
                                o = pO[:, 0:KVL + 1]
                                for k in range(n):
                                    ks = slice(k * P, (k + 1) * P)
                                    j = 4 * c + k
                                    last = j == i
                                    hi, lo = pT_hi[:, at % 3, ks], pT_lo[:, at % 3, ks]
                                    pe.matmul(o, hi, c_hi[:, j, 0:KVL + 1], start=(j == 0), stop=False)
                                    pe.matmul(o, hi, c_lo[:, j, 0:KVL + 1], start=False, stop=False)
                                    m = pe.matmul(o, lo, c_hi[:, j, 0:KVL + 1], start=False, stop=last)
                                m.then_inc(sem("p5"), 1)

                            project(0)
                            turn(0)
                            project(1)
                            turn(1)
                            project(2)
                            scores(0, *chunks[0][0])
                            late = None
                            for i in range(NT):
                                if i + 1 < NT:
                                    scores(i + 1, *chunks[i + 1][0])
                                if late:
                                    values(*late)
                                if i + 1 < NT:
                                    for c in chunks[i + 1][1:]:
                                        scores(i + 1, *c)
                                if i + 2 < NT:
                                    turn(i + 2)
                                for k, c in enumerate(chunks[i]):
                                    turn_probs(i, *c)
                                    if k:
                                        values(i, *chunks[i][k - 1])
                                if i + 3 < NT:
                                    project(i + 3)
                                late = (i, *chunks[i][-1])
                            values(*late)

                        @block.scalar
                        def _(act):
                            def q_out(i):
                                act.wait_ge(sem("p1"), i + 1)
                                if i >= 2:
                                    act.wait_ge(sem("g1"), i - 1)
                                act.activation(qs[:, i % 2], pQ[:, 0:DQ], ACT.Copy, scale=SCALE).then_inc(sem("a1"), 1)

                            def q_hi(i):
                                act.wait_ge(sem("p2"), i + 1)
                                act.activation(qT_hi[:, i % 2], pQ[:, P:2 * P], ACT.Copy).then_inc(sem("a2"), 1)

                            def exps(i, c, n):
                                if c == 0:
                                    act.wait_ge(sem("v3"), i + 1)
                                    if i >= 2:
                                        act.wait_ge(sem("p4"), first[i - 1])
                                at = first[i] + c
                                act.activation(pr[:, i % 2, c * BT:c * BT + n * P], pS[at % 4][:, 0:n * P], ACT.Exp,
                                               bias=nmx[:, i % 2:i % 2 + 1]).then_inc(sem("a3"), 1)

                            def p_hi(i, c, n):
                                at = first[i] + c
                                act.wait_ge(sem("p4"), at + 1)
                                if at >= 3:
                                    act.wait_ge(sem("p5"), at - 2)
                                act.activation(pT_hi[:, at % 3, 0:n * P], pT[at % 2][:, 0:n * P], ACT.Copy).then_inc(sem("a4"), 1)

                            q_out(0)
                            q_hi(0)
                            q_out(1)
                            q_hi(1)
                            q_out(2)
                            exps(0, *chunks[0][0])
                            for i in range(NT):
                                if i + 2 < NT:
                                    q_hi(i + 2)
                                his = [(p_hi, i, c) for c in chunks[i]]
                                exs = [(exps, i + 1, c) for c in chunks[i + 1]] if i + 1 < NT else []
                                order = his[:1]
                                for k in range(4):
                                    order += exs[k:k + 1] + his[k + 1:k + 2]
                                for step, j, c in order:
                                    step(j, *c)
                                if i + 3 < NT:
                                    q_out(i + 3)

                        @block.gpsimd
                        def _(pool):
                            ch = Chain(pool, sem("gp"))
                            for i in range(NT):
                                pool.wait_ge(sem("a1"), i + 1)
                                if i >= 2:
                                    pool.wait_ge(sem("p2"), i - 1)
                                q, r, o = qs[:, i % 2, KVL:DQ], qt[:, i % 2], qr[:, i % 2]
                                ch.inc(pool.tensor_tensor(r[:, 0:32], q[:, 32:64], sn[:, i, 0:32], ALU.mult))
                                ch.inc(pool.tensor_tensor(r[:, 32:64], q[:, 0:32], sn[:, i, 32:64], ALU.mult))
                                ch.inc(pool.tensor_tensor(o[:, KVL:DQ], q, cs[:, i, :], ALU.mult))
                                ch.inc(pool.tensor_copy(o[:, 0:KVL], qs[:, i % 2, 0:KVL]))
                                ch.wait()
                                pool.tensor_tensor(o[:, KVL:DQ], o[:, KVL:DQ], r, ALU.add).then_inc(sem("g1"), 1)

                        @block.vector
                        def _(dve):
                            ch = Chain(dve, sem("dv"))

                            def q_lo(i):
                                dve.wait_ge(sem("a2"), i + 1)
                                dve.tensor_tensor(qT_lo[:, i % 2], pQ[:, P:2 * P], f(qT_hi[:, i % 2]), ALU.subtract).then_inc(sem("v2"), 1)

                            def maxima(i):
                                one = len(chunks[i]) == 1
                                if i >= 2:
                                    dve.wait_ge(sem("a3"), first[i - 1])
                                for c, n in chunks[i]:
                                    at = first[i] + c
                                    dve.wait_ge(sem("p3"), at + 1)
                                    if one:
                                        dve.tensor_reduce(nmx[:, i % 2:i % 2 + 1], pS[at % 4][:, 0:n * P], AX.X, ALU.max,
                                                          negate=True).then_inc(sem("v3"), 1)
                                    else:
                                        ch.inc(dve.tensor_reduce(cmx[:, i % 2, c:c + 1], pS[at % 4][:, 0:n * P], AX.X, ALU.max))
                                if not one:
                                    ch.wait()
                                    dve.tensor_reduce(nmx[:, i % 2:i % 2 + 1], cmx[:, i % 2, 0:len(chunks[i])], AX.X, ALU.max,
                                                      negate=True).then_inc(sem("v3"), 1)

                            def p_lo(i, c, n):
                                at = first[i] + c
                                dve.wait_ge(sem("a4"), at + 1)
                                dve.tensor_tensor(pT_lo[:, at % 3, 0:n * P], pT[at % 2][:, 0:n * P], pT_hi[:, at % 3, 0:n * P],
                                                  ALU.subtract).then_inc(sem("v4"), 1)

                            def o_out(i):
                                dve.wait_ge(sem("p5"), first[i + 1])
                                ch.inc(dve.reciprocal(rl[:, i % 2:i % 2 + 1], pO[:, KVL:KVL + 1]))
                                ch.wait()
                                dve.tensor_scalar(O[:, i, bass.ds(h * KVL, KVL)], pO[:, 0:KVL], rl[:, i % 2:i % 2 + 1], None,
                                                  ALU.mult).then_inc(sem("v5"), 1)

                            q_lo(0)
                            q_lo(1)
                            maxima(0)
                            for i in range(NT):
                                if i + 1 < NT:
                                    maxima(i + 1)
                                if i >= 1:
                                    o_out(i - 1)
                                if i + 2 < NT:
                                    q_lo(i + 2)
                                for c in chunks[i]:
                                    p_lo(i, *c)
                            o_out(NT - 1)

                    phase_end()

            with ExitStack() as op:
                OT_hi = sb(op, "OT_hi", [P, 2, 8, P], F32R)
                OT_lo = sb(op, "OT_lo", [P, 2, 8, P], F32R)
                tmp = sb(op, "tmp", [P, 2, D])
                pt = [[ps(op, f"po{b}{k}", [P, 512]) for k in range(2)] for b in range(2)]
                py = [ps(op, f"py{b}", [P, 512]) for b in range(2)]
                with nc.Block() as block:

                    @block.tensor
                    def _(pe):
                        def turn(t):
                            for k in range(2):
                                if t >= 2:
                                    pe.wait_ge(sem("v1"), 2 * (t - 2) + k + 1)
                                for j in range(4):
                                    m = pe.transpose(pt[t % 2][k][:, j * P:(j + 1) * P], O[:, t, (4 * k + j) * P:(4 * k + j + 1) * P], ident[:])
                                m.then_inc(sem("p1"), 1)

                        turn(0)
                        for t in range(NT):
                            if t + 1 < NT:
                                turn(t + 1)
                            pe.wait_ge(sem("v1"), 2 * t + 2)
                            if t >= 2:
                                pe.wait_ge(sem("v5"), t - 1)
                            y = py[t % 2][:, 0:D]
                            n = 0
                            for j in range(8):
                                for a, w in ((OT_hi, Wvo_hi), (OT_hi, Wvo_lo), (OT_lo, Wvo_hi)):
                                    m = pe.matmul(y, a[:, t % 2, j], w[:, j], start=(n == 0), stop=(n == 23))
                                    n += 1
                            m.then_inc(sem("p2"), 1)

                    @block.scalar
                    def _(act):
                        for t in range(NT):
                            for k in range(2):
                                act.wait_ge(sem("p1"), 2 * t + k + 1)
                                if t >= 2:
                                    act.wait_ge(sem("p2"), t - 1)
                                act.activation(OT_hi[:, t % 2, 4 * k:4 * k + 4], pt[t % 2][k][:].rearrange("p (j n) -> p j n", j=4),
                                               ACT.Copy).then_inc(sem("a1"), 1)

                    @block.gpsimd
                    def _(pool):
                        ch = Chain(pool, sem("gp"))
                        for t in range(NT):
                            pool.wait_ge(sem("v2"), t + 1)
                            pool_rsqrt(pool, ch, rs[:, t:t + 1], mv[:, t, 1:2], LN_EPS).then_inc(sem("g1"), 1)

                    @block.vector
                    def _(dve):
                        ch = Chain(dve, sem("dv"))

                        def split(t):
                            for k in range(2):
                                dve.wait_ge(sem("a1"), 2 * t + k + 1)
                                dve.tensor_tensor(OT_lo[:, t % 2, 4 * k:4 * k + 4], pt[t % 2][k][:].rearrange("p (j n) -> p j n", j=4),
                                                  f(OT_hi[:, t % 2, 4 * k:4 * k + 4]), ALU.subtract).then_inc(sem("v1"), 1)

                        split(0)
                        for t in range(NT):
                            if t + 1 < NT:
                                split(t + 1)
                            dve.wait_ge(sem("p2"), t + 1)
                            add_normed(dve, ch, t, py[t % 2][:, 0:D], tmp[:, t % 2])

                phase_end()

        def turned_norm(xT_hi, xT_lo):
            with ExitStack() as c:
                xn = sb(c, "xn", [P, 4, D])
                pt = [ps(c, f"pt{b}", [P, 512]) for b in range(4)]
                with nc.Block() as block:

                    @block.vector
                    def _(dve):
                        ch = Chain(dve, sem("dv"))

                        def centred(t):
                            dve.wait_ge(sem("g1"), t + 1)
                            if t >= 4:
                                dve.wait_ge(sem("p1"), t - 3)
                            dve.tensor_scalar(xn[:, t % 4, :], X[:, t, :], mv[:, t, 0:1], rs[:, t:t + 1],
                                              ALU.subtract, ALU.mult).then_inc(sem("v2"), 1)

                        def low(t):
                            dve.wait_ge(sem("a1"), t + 1)
                            sl = slice(t * P, (t + 1) * P)
                            dve.tensor_tensor(xT_lo[:, :, sl], pt[t % 4][:, 0:D].rearrange("p (k n) -> p k n", k=KD),
                                              f(xT_hi[:, :, sl]), ALU.subtract).then_inc(sem("v3"), 1)

                        for t in range(NT + 4):
                            if t < NT:
                                ch.inc(dve.bn_stats(stats[:, t, :], X[:, t, :]))
                                ch.wait()
                                dve.bn_aggr(mv[:, t, :], stats[:, t, :]).then_inc(sem("v1"), 1)
                            if 2 <= t < NT + 2:
                                centred(t - 2)
                            if 4 <= t:
                                low(t - 4)

                    @block.gpsimd
                    def _(pool):
                        ch = Chain(pool, sem("gp"))
                        for t in range(NT):
                            pool.wait_ge(sem("v1"), t + 1)
                            pool_rsqrt(pool, ch, rs[:, t:t + 1], mv[:, t, 1:2], LN_EPS).then_inc(sem("g1"), 1)

                    @block.tensor
                    def _(pe):
                        for t in range(NT):
                            pe.wait_ge(sem("v2"), t + 1)
                            if t >= 4:
                                pe.wait_ge(sem("v3"), t - 3)
                            for k in range(KD):
                                m = pe.transpose(pt[t % 4][:, k * P:(k + 1) * P], xn[:, t % 4, k * P:(k + 1) * P], ident[:])
                            m.then_inc(sem("p1"), 1)

                    @block.scalar
                    def _(act):
                        for t in range(NT):
                            act.wait_ge(sem("p1"), t + 1)
                            act.activation(xT_hi[:, :, t * P:(t + 1) * P], pt[t % 4][:, 0:D].rearrange("p (k n) -> p k n", k=KD),
                                           ACT.Copy).then_inc(sem("a1"), 1)
                phase_end()

        def split_weights(parts):
            with ExitStack() as c:
                width = 1760
                raw = sb(c, "raw", [P, 2, width])
                with nc.Block() as block:

                    @block.sync
                    def _(sp):
                        for n, (src, hi, lo) in enumerate(parts):
                            if n >= 2:
                                sp.wait_ge(sem("v1"), n - 1)
                            rows, cols = hi.shape[0], hi.free_size()
                            dst = raw[0:rows, n % 2, 0:cols]
                            if len(src.shape) == 3:
                                dst = dst.rearrange("p (a b) -> p a b", a=src.shape[1])
                            sp.dma_start(dst, src).then_inc(sem("dma_w" if n % 2 == 0 else "dma_w2"), 16)

                    @block.scalar
                    def _(act):
                        for n, (src, hi, lo) in enumerate(parts):
                            act.wait_ge(sem("dma_w" if n % 2 == 0 else "dma_w2"), 16 * (n // 2 + 1))
                            rows, cols = hi.shape[0], hi.free_size()
                            r = raw[0:rows, n % 2, 0:cols]
                            if len(hi.shape) == 3:
                                r = r.rearrange("p (a b) -> p a b", a=hi.shape[1])
                            act.activation(hi, r, ACT.Copy).then_inc(sem("a1"), 1)

                    @block.vector
                    def _(dve):
                        for n, (src, hi, lo) in enumerate(parts):
                            dve.wait_ge(sem("a1"), n + 1)
                            rows, cols = hi.shape[0], hi.free_size()
                            r = raw[0:rows, n % 2, 0:cols]
                            if len(hi.shape) == 3:
                                r = r.rearrange("p (a b) -> p a b", a=hi.shape[1])
                            dve.tensor_tensor(lo, r, f(hi), ALU.subtract).then_inc(sem("v1"), 1)
                phase_end()

        def gated_ffn(xT, wg_, wu_, wd_, n_m, rows, n_routed=0, selb=None, wT=None, g_scale=None, u_scale=None, store=False):
            with ExitStack() as c:
                sgb = sb(c, "sgb", [P, 2, BT])
                hb = sb(c, "hb", [P, 2, BT])
                h_hi = sb(c, "h_hi", [P, 2, BT], F32R)
                h_lo = sb(c, "h_lo", [P, 2, BT], F32R)
                y = sb(c, "y", [P, TPB, D])
                tmp = sb(c, "tmp", [P, 2, D])
                pG = [ps(c, f"pG{b}", [P, BT]) for b in range(2)]
                pU = [ps(c, f"pU{b}", [P, BT]) for b in range(2)]
                pW = [ps(c, f"pW{b}", [P, BT]) for b in range(2)]
                pY = [ps(c, f"pY{b}", [P, 2, D]) for b in range(2)]
                N = NB * n_m

                def routed(n):
                    return n % n_m < n_routed

                def n_scaled(n):
                    return (n // n_m) * n_routed + min(n % n_m + 1, n_routed)

                with nc.Block() as block:

                    @block.tensor
                    def _(pe):
                        def up(n):
                            tb, m = divmod(n, n_m)
                            b, r, ts = n % 2, rows[m], slice(tb * BT, (tb + 1) * BT)
                            fs = slice(m * P, m * P + r)
                            if n >= 2:
                                pe.wait_ge(sem("a1"), n - 1)
                                pe.wait_ge(sem("v1"), n - 1)
                            for out_, w in ((pG[b], wg_), (pU[b], wu_)):
                                q = 0
                                for k in range(KD):
                                    for i, j in ((0, 0), (0, 1), (1, 0)):
                                        mm = pe.matmul(out_[0:r, :], w[i][:, k, fs], xT[j][:, k, ts], start=(q == 0), stop=(q == 5))
                                        q += 1
                            if routed(n):
                                if n_scaled(n) > 2:
                                    pe.wait_ge(sem("v2"), n_scaled(n) - 2)
                                mm = pe.matmul(pW[(n_scaled(n) - 1) % 2][0:r, :], selb[:, fs], wT[:, ts], start=True, stop=True)
                            mm.then_inc(sem("p1"), 1)

                        def down(n):
                            tb, m = divmod(n, n_m)
                            b, r = n % 2, rows[m]
                            pe.wait_ge(sem("a2"), n + 1)
                            pe.wait_ge(sem("v3"), n + 1)
                            if m == 0 and tb:
                                pe.wait_ge(sem("a3"), 2 * tb)
                            for q in range(TPB):
                                qs_ = slice(q * P, (q + 1) * P)
                                for j, (a, w) in enumerate(((h_hi, wd_[0]), (h_hi, wd_[1]), (h_lo, wd_[0]))):
                                    mm = pe.matmul(pY[q // 2][:, q % 2, :], a[0:r, b, qs_], w[0:r, m, :],
                                                   start=(m == 0 and q % 2 == 0 and j == 0), stop=(m == n_m - 1 and j == 2),
                                                   skip_group_check=True)
                            mm.then_inc(sem("p2"), 1)

                        up(0)
                        for n in range(N):
                            if n + 1 < N:
                                up(n + 1)
                            down(n)

                    @block.scalar
                    def _(act):
                        def silu(n):
                            b, m = n % 2, n % n_m
                            r = rows[m]
                            act.wait_ge(sem("p1"), n + 1)
                            if n >= 2:
                                act.wait_ge(sem("v1"), n - 1)
                            kw = {"scale": g_scale[0:r, m:m + 1]} if g_scale is not None else {}
                            act.activation(sgb[0:r, b], pG[b][0:r, :], ACT.Silu, **kw).then_inc(sem("a1"), 1)

                        silu(0)
                        for n in range(N):
                            if n + 1 < N:
                                silu(n + 1)
                            tb, m = divmod(n, n_m)
                            b, r = n % 2, rows[m]
                            if routed(n):
                                act.wait_ge(sem("v2"), n_scaled(n))
                            else:
                                act.wait_ge(sem("v1"), n + 1)
                            if n >= 2:
                                act.wait_ge(sem("p2"), n - 1)
                            act.activation(h_hi[0:r, b], hb[0:r, b], ACT.Copy).then_inc(sem("a2"), 1)
                            if m == n_m - 1:
                                act.wait_ge(sem("p2"), n + 1)
                                if tb:
                                    act.wait_ge(sem("v5"), TPB * tb)
                                for k in range(2):
                                    act.activation(y[:, 2 * k:2 * k + 2, :], pY[k][:], ACT.Copy).then_inc(sem("a3"), 1)

                    @block.gpsimd
                    def _(pool):
                        ch = Chain(pool, sem("gp"))
                        for t in range(NT):
                            pool.wait_ge(sem("v4"), t + 1)
                            pool_rsqrt(pool, ch, rs[:, t:t + 1], mv[:, t, 1:2], LN_EPS).then_inc(sem("g1"), 1)

                    @block.vector
                    def _(dve):
                        ch = Chain(dve, sem("dv"))

                        def hidden(n):
                            b, m = n % 2, n % n_m
                            r = rows[m]
                            dve.wait_ge(sem("a1"), n + 1)
                            if n >= 2:
                                dve.wait_ge(sem("a2"), n - 1)
                                dve.wait_ge(sem("v3"), n - 1)
                            if u_scale is not None:
                                dve.scalar_tensor_tensor(out=hb[0:r, b], in0=pU[b][0:r, :], scalar=u_scale[0:r, m:m + 1],
                                                         in1=sgb[0:r, b], op0=ALU.mult, op1=ALU.mult).then_inc(sem("v1"), 1)
                            else:
                                dve.tensor_tensor(hb[0:r, b], pU[b][0:r, :], sgb[0:r, b], ALU.mult).then_inc(sem("v1"), 1)
                            if routed(n):
                                dve.wait_ge(sem("v1"), n + 1)
                                dve.tensor_tensor(hb[0:r, b], pW[(n_scaled(n) - 1) % 2][0:r, :], hb[0:r, b], ALU.mult).then_inc(sem("v2"), 1)

                        def block_out(tb):
                            dve.wait_ge(sem("a3"), 2 * tb + 2)
                            for q in range(TPB):
                                add_normed(dve, ch, tb * TPB + q, y[:, q, :], tmp[:, q % 2], "v4", "v5")

                        hidden(0)
                        for n in range(N):
                            if n + 1 < N:
                                hidden(n + 1)
                            tb, m = divmod(n, n_m)
                            b, r = n % 2, rows[m]
                            dve.wait_ge(sem("a2"), n + 1)
                            if n >= 2:
                                dve.wait_ge(sem("p2"), n - 1)
                            dve.tensor_tensor(h_lo[0:r, b], hb[0:r, b], f(h_hi[0:r, b]), ALU.subtract).then_inc(sem("v3"), 1)
                            if m == 1 and tb:
                                block_out(tb - 1)
                        block_out(NB - 1)

                    if store:
                        @block.sync
                        def _(sp):
                            for tb in range(NB):
                                sp.wait_ge(sem("v6"), TPB * (tb + 1))
                                sp.dma_start(out[:, tb * TPB:(tb + 1) * TPB, :], X[:, tb * TPB:(tb + 1) * TPB, :]).then_inc(sem("dma_out"), 16)
                            sp.wait_ge(sem("dma_out"), 16 * NB)
                if not store:
                    phase_end()

        with ExitStack() as moe:
            xT = [sb(moe, f"xT{k}", [P, KD, T], F32R) for k in range(2)]
            wg_ = [sb(moe, f"wg_{k}", [P, KD, FM], F32R) for k in range(2)]
            wu_ = [sb(moe, f"wu_{k}", [P, KD, FM], F32R) for k in range(2)]
            wd_ = [sb(moe, f"wd_{k}", [P, NFM, D], F32R) for k in range(2)]
            gwr = sb(moe, "gwr", [P, KD, P])
            gw_ = [sb(moe, f"gw_{k}", [P, KD, P], F32R) for k in range(2)]
            selb = sb(moe, "selb", [3 * NE, FR], BF16)
            wT = sb(moe, "wT", [3 * NE, T], BF16)
            tri = sb(moe, "tri", [P, NE, NE])
            split_weights([(w[:, k, :], h_[0][:, k, :], h_[1][:, k, :]) for w, h_ in ((wg, wg_), (wu, wu_)) for k in range(KD)]
                          + [(wd[0:P, 0:6, :], wd_[0][:, 0:6], wd_[1][:, 0:6]), (wd[0:P, 6:12, :], wd_[0][:, 6:12], wd_[1][:, 6:12]),
                             (wd[0:P, 12:13, :], wd_[0][:, 12:13], wd_[1][:, 12:13]),
                             (wd[0:FM - 13 * P, 13:14, :], wd_[0][0:FM - 13 * P, 13:14], wd_[1][0:FM - 13 * P, 13:14])])
            turned_norm(*xT)
            with ExitStack() as c:
                self32 = sb(c, "self32", [3 * NE, FR])
                lgT = sb(c, "lgT", [NE, T])
                L = sb(c, "L", [P, NT, NE])
                S = sb(c, "S", [P, NT, NE])
                M = sb(c, "M", [P, NT, NE])
                R = sb(c, "R", [P, NT, NE])
                small = sb(c, "small", [P, 3, NT])
                G = sb(c, "G", [P, 2, NT, 4])
                cmp1 = sb(c, "cmp1", [P, NT, NE, NE])
                cmp2 = sb(c, "cmp2", [P, NT, NE, NE])
                w3 = sb(c, "w3", [P, NT, 3 * NE], BF16)
                pg = [ps(c, f"pg{b}", [P, BT]) for b in range(2)]
                pr_ = ps(c, "pr_", [P, 512])
                pw = [ps(c, f"pw{b}", [P, 1024], BF16) for b in range(2)]
                with nc.Block() as block:

                    @block.sync
                    def _(sp):
                        sp.dma_start(self32[:], sel).then_inc(sem("dma_w"), 16)
                        sp.wait_ge(sem("gp"), 1)
                        sp.dma_start(gwr[:, :, 0:NE], gw).then_inc(sem("dma_w2"), 16)

                    @block.gpsimd
                    def _(pool):
                        pool.memset(gwr[:], 0.0).then_inc(sem("gp"), 1)
                        pool.memset(tri[:], 1.0).then_inc(sem("gp"), 1)
                        pool.wait_ge(sem("gp"), 2)
                        pool.affine_select(out=tri[:], in_=tri[:], compare_op=ALU.is_gt, fill=0.0, base=0,
                                           pattern=[[1, NE], [-1, NE]], channel_multiplier=0).then_inc(sem("g1"), 1)
                        pool.wait_ge(sem("dma_w"), 16)
                        pool.tensor_copy(selb[:], self32[:]).then_inc(sem("g2"), 1)

                    @block.scalar
                    def _(act):
                        act.wait_ge(sem("dma_w2"), 16)
                        act.activation(gw_[0][:], gwr[:], ACT.Copy).then_inc(sem("a1"), 1)
                        for tb in range(NB):
                            act.wait_ge(sem("p1"), tb + 1)
                            act.activation(lgT[:, tb * BT:(tb + 1) * BT], pg[tb % 2][0:NE, :], ACT.Copy).then_inc(sem("a2"), 1)
                        act.wait_ge(sem("v2"), 1)
                        act.activation(S[:], S[:], ACT.Exp).then_inc(sem("a3"), 1)
                        for b in range(2):
                            act.wait_ge(sem("p3"), b + 1)
                            act.activation(wT[:, b * 1024:(b + 1) * 1024], pw[b][0:3 * NE, :], ACT.Copy).then_inc(sem("a4"), 1)

                    @block.tensor
                    def _(pe):
                        pe.wait_ge(sem("v1"), 1)
                        for tb in range(NB):
                            if tb >= 2:
                                pe.wait_ge(sem("a2"), tb - 1)
                            q = 0
                            for k in range(KD):
                                for i, j in ((0, 0), (0, 1), (1, 0)):
                                    mm = pe.matmul(pg[tb % 2][:], gw_[i][:, k, :], xT[j][:, k, tb * BT:(tb + 1) * BT], start=(q == 0), stop=(q == 5))
                                    q += 1
                            mm.then_inc(sem("p1"), 1)
                        pe.wait_ge(sem("a2"), NB)
                        for t in range(NT):
                            mm = pe.transpose(pr_[:, t * NE:(t + 1) * NE], lgT[:, t * P:(t + 1) * P], ident[0:NE, 0:NE])
                        mm.then_inc(sem("p2"), 1)
                        pe.wait_ge(sem("v3"), 1)
                        for b in range(2):
                            for t in range(8):
                                mm = pe.transpose(pw[b][0:3 * NE, t * P:(t + 1) * P], w3[:, 8 * b + t, :], identb[:])
                            mm.then_inc(sem("p3"), 1)

                    @block.vector
                    def _(dve):
                        ch = Chain(dve, sem("dv"))

                        def step(ins):
                            ch.inc(ins)
                            ch.wait()

                        def wide(ap, n):
                            return ap.unsqueeze(3).to_broadcast([P, NT, n, n])

                        def ranks(dst, src, n):
                            mine, other = wide(src, n), src.unsqueeze(2).to_broadcast([P, NT, n, n])
                            a, b = cmp1[:, :, 0:n, 0:n], cmp2[:, :, 0:n, 0:n]
                            ch.inc(dve.tensor_tensor(a, other, mine, ALU.is_gt))
                            step(dve.tensor_tensor(b, other, mine, ALU.is_equal))
                            step(dve.tensor_tensor(b, b, tri[:, 0:n, 0:n].unsqueeze(1).to_broadcast([P, NT, n, n]), ALU.mult))
                            step(dve.tensor_tensor(a, a, b, ALU.add))
                            step(dve.tensor_reduce(dst, a, AX.X, ALU.add))

                        def over(ap, n=NE):
                            return ap.unsqueeze(2).to_broadcast([P, NT, n])

                        dve.wait_ge(sem("a1"), 1)
                        dve.tensor_tensor(gw_[1][:], gwr[:], f(gw_[0][:]), ALU.subtract).then_inc(sem("v1"), 1)
                        dve.wait_ge(sem("p2"), 1)
                        step(dve.tensor_copy(L[:], pr_[:, 0:NT * NE].rearrange("p (t e) -> p t e", e=NE)))
                        step(dve.tensor_reduce(small[:, 0, :], L[:], AX.X, ALU.max))
                        dve.tensor_tensor(S[:], L[:], over(small[:, 0, :]), ALU.subtract).then_inc(sem("v2"), 1)
                        dve.wait_ge(sem("a3"), 1)
                        step(dve.tensor_reduce(small[:, 1, :], S[:], AX.X, ALU.add))
                        step(dve.reciprocal(small[:, 2, :], small[:, 1, :]))
                        step(dve.tensor_tensor(S[:], S[:], over(small[:, 2, :]), ALU.mult))
                        step(dve.tensor_reduce(G[:, 0], S[:].rearrange("p t (g e) -> p t g e", e=2), AX.X, ALU.max))
                        dve.wait_ge(sem("g1"), 1)
                        ranks(G[:, 1], G[:, 0], 4)
                        step(dve.tensor_scalar(G[:, 1], G[:, 1], 1.5, None, ALU.is_lt))
                        step(dve.tensor_tensor(M[:].rearrange("p t (g e) -> p t g e", e=2), S[:].rearrange("p t (g e) -> p t g e", e=2),
                                               G[:, 1].unsqueeze(3).to_broadcast([P, NT, 4, 2]), ALU.mult))
                        ranks(R[:], M[:], NE)
                        step(dve.tensor_scalar(R[:], R[:], 1.5, None, ALU.is_lt))
                        step(dve.tensor_tensor(M[:], M[:], R[:], ALU.mult))
                        step(dve.tensor_copy(w3[:, :, 0:NE], M[:]))
                        step(dve.tensor_tensor(M[:], M[:], w3[:, :, 0:NE], ALU.subtract))
                        step(dve.tensor_copy(w3[:, :, NE:2 * NE], M[:]))
                        step(dve.tensor_tensor(M[:], M[:], w3[:, :, NE:2 * NE], ALU.subtract))
                        dve.tensor_copy(w3[:, :, 2 * NE:3 * NE], M[:]).then_inc(sem("v3"), 1)
                phase_end()
            gated_ffn(xT, wg_, wu_, wd_, NFM, [P] * 13 + [FM - 13 * P], n_routed=FR // P, selb=selb, wT=wT)

        with ExitStack() as lru:
            xT = [sb(lru, f"xT{k}", [P, KD, T], F32R) for k in range(2)]
            wi_ = [sb(lru, f"wi_{k}", [P, KD, D], F32R) for k in range(2)]
            wr_ = [sb(lru, f"wr_{k}", [P, KD, D], F32R) for k in range(2)]
            split_weights([(l_in, wi_[0][:], wi_[1][:]), (l_gate, wr_[0][:], wr_[1][:])])
            turned_norm(*xT)
            with ExitStack() as c:
                si = sb(c, "si", [P, KD, T])
                al = sb(c, "al", [P, KD, T])
                be = sb(c, "be", [P, KD, T])
                xs = sb(c, "xs", [P, KD, T])
                lb = sb(c, "lb", [P, 2, KD])
                lam = sb(c, "lam", [P, KD])
                z = sb(c, "z", [P, 6, KD])
                tmp = sb(c, "tmp", [P, 2, D])
                eps = sb(c, "eps", [P, 1])
                pg = [ps(c, f"pg{b}", [P, BT]) for b in range(4)]
                py = [ps(c, f"py{b}", [P, 512]) for b in range(2)]
                gates = [(tb, e, w) for e in range(KD) for tb in range(NB) for w in range(2)]
                with nc.Block() as block:

                    @block.sync
                    def _(sp):
                        sp.dma_start(lb[:], l_b).then_inc(sem("dma_w"), 16)
                        sp.dma_start(lam[:], l_lam).then_inc(sem("dma_w"), 16)

                    @block.tensor
                    def _(pe):
                        for n, (tb, e, w) in enumerate(gates):
                            if n >= 4:
                                pe.wait_ge(sem("a1"), n - 3)
                            wts = (wi_, wr_)[w]
                            q = 0
                            for k in range(KD):
                                for i, j in ((0, 0), (0, 1), (1, 0)):
                                    mm = pe.matmul(pg[n % 4][:], wts[i][:, k, e * P:(e + 1) * P], xT[j][:, k, tb * BT:(tb + 1) * BT],
                                                   start=(q == 0), stop=(q == 5))
                                    q += 1
                            mm.then_inc(sem("p1"), 1)
                        for t in range(NT):
                            if t == 0:
                                pe.wait_ge(sem("v2"), KD)
                            if t >= 2:
                                pe.wait_ge(sem("v5"), t - 1)
                            for k in range(KD):
                                mm = pe.transpose(py[t % 2][:, k * P:(k + 1) * P], xs[:, k, t * P:(t + 1) * P], ident[:])
                            mm.then_inc(sem("p2"), 1)

                    @block.scalar
                    def _(act):
                        act.wait_ge(sem("dma_w"), 32)
                        act.wait_ge(sem("v3"), 1)
                        act.activation(z[:, 0, :], z[:, 1, :], ACT.Exp, scale=-1.0).then_inc(sem("a2"), 1)
                        for n, (tb, e, w) in enumerate(gates):
                            act.wait_ge(sem("p1"), n + 1)
                            dst = (si, al)[w][:, e, tb * BT:(tb + 1) * BT]
                            act.activation(dst, pg[n % 4][:], ACT.Sigmoid, bias=lb[:, w, e:e + 1]).then_inc(sem("a1"), 1)
                        act.wait_ge(sem("v3"), 2)
                        act.wait_ge(sem("a1"), len(gates))
                        for e in range(KD):
                            act.activation(al[:, e, :], al[:, e, :], ACT.Exp, scale=z[:, 5, e:e + 1]).then_inc(sem("a3"), 1)
                        for e in range(KD):
                            act.wait_ge(sem("v1"), e + 1)
                            act.activation(be[:, e, :], be[:, e, :], ACT.Sqrt, bias=eps[:]).then_inc(sem("a4"), 1)

                    @block.gpsimd
                    def _(pool):
                        pool.memset(eps[:], 1e-6).then_inc(sem("g2"), 1)
                        ch = Chain(pool, sem("gp"))
                        for t in range(NT):
                            pool.wait_ge(sem("v4"), t + 1)
                            pool_rsqrt(pool, ch, rs[:, t:t + 1], mv[:, t, 1:2], LN_EPS).then_inc(sem("g1"), 1)

                    @block.vector
                    def _(dve):
                        ch = Chain(dve, sem("dv"))

                        def step(ins):
                            ch.inc(ins)
                            ch.wait()

                        dve.wait_ge(sem("dma_w"), 32)
                        step(dve.tensor_scalar(z[:, 1, :], lam[:], -1.0, None, ALU.mult))
                        dve.tensor_tensor(z[:, 1, :], z[:, 1, :], lam[:], ALU.max).then_inc(sem("v3"), 1)
                        dve.wait_ge(sem("a2"), 1)
                        step(dve.tensor_scalar(z[:, 2, :], z[:, 0, :], 2.0, None, ALU.add))
                        step(dve.reciprocal(z[:, 2, :], z[:, 2, :]))
                        step(dve.tensor_tensor(z[:, 2, :], z[:, 2, :], z[:, 0, :], ALU.mult))
                        step(dve.tensor_tensor(z[:, 3, :], z[:, 2, :], z[:, 2, :], ALU.mult))
                        step(dve.tensor_scalar(z[:, 4, :], z[:, 3, :], 1.0 / (2 * LOG1P_TERMS + 1), None, ALU.mult))
                        for k in range(LOG1P_TERMS - 1, 0, -1):
                            step(dve.scalar_tensor_tensor(out=z[:, 4, :], in0=z[:, 4, :], scalar=1.0 / (2 * k + 1), in1=z[:, 3, :],
                                                          op0=ALU.add, op1=ALU.mult))
                        step(dve.scalar_tensor_tensor(out=z[:, 4, :], in0=z[:, 4, :], scalar=1.0, in1=z[:, 2, :],
                                                      op0=ALU.add, op1=ALU.mult))
                        step(dve.tensor_scalar(z[:, 0, :], lam[:], 0.0, -LRU_C, ALU.max, ALU.mult))
                        dve.scalar_tensor_tensor(out=z[:, 5, :], in0=z[:, 4, :], scalar=-2.0 * LRU_C, in1=z[:, 0, :],
                                                 op0=ALU.mult, op1=ALU.add).then_inc(sem("v3"), 1)
                        for e in range(KD):
                            step(dve.tensor_tensor(xs[:, e, :], f(xT[0][:, e, :]), f(xT[1][:, e, :]), ALU.add))
                        dve.wait_ge(sem("a1"), len(gates))
                        for e in range(KD):
                            step(dve.tensor_tensor(si[:, e, :], si[:, e, :], xs[:, e, :], ALU.mult))
                        for e in range(KD):
                            dve.wait_ge(sem("a3"), e + 1)
                            step(dve.tensor_tensor(be[:, e, :], al[:, e, :], al[:, e, :], ALU.mult))
                            if e == 0:
                                dve.wait_ge(sem("g2"), 1)
                            dve.tensor_scalar(be[:, e, :], be[:, e, :], -1.0, 1.0, ALU.mult, ALU.add).then_inc(sem("v1"), 1)
                        for e in range(KD):
                            dve.wait_ge(sem("a4"), e + 1)
                            step(dve.tensor_tensor(be[:, e, :], be[:, e, :], si[:, e, :], ALU.mult))
                            dve.tensor_tensor_scan(xs[:, e, :], al[:, e, :], be[:, e, :], 0.0, ALU.mult, ALU.add).then_inc(sem("v2"), 1)
                        for t in range(NT):
                            dve.wait_ge(sem("p2"), t + 1)
                            add_normed(dve, ch, t, py[t % 2][:, 0:D], tmp[:, t % 2], "v4", "v5")
                phase_end()

        with ExitStack() as ffn:
            xT = [sb(ffn, f"xT{k}", [P, KD, T], F32R) for k in range(2)]
            qg_ = [sb(ffn, f"qg_{k}", [P, KD, NFQ * P], F32R) for k in range(2)]
            qu_ = [sb(ffn, f"qu_{k}", [P, KD, NFQ * P], F32R) for k in range(2)]
            qd_ = [sb(ffn, f"qd_{k}", [P, NFQ, D], F32R) for k in range(2)]
            scg = sb(ffn, "scg", [P, NFQ])
            scu = sb(ffn, "scu", [P, NFQ])
            with ExitStack() as c:
                raws = [sb(c, "rawg", [P, KD, NFQ * P], I32), sb(c, "rawu", [P, KD, NFQ * P], I32), sb(c, "rawd", [P, NFQ, D], I32)]
                w32 = [sb(c, "w32g", [P, KD, NFQ * P]), sb(c, "w32u", [P, KD, NFQ * P]), sb(c, "w32d", [P, NFQ, D])]
                sdb = sb(c, "sdb", [P, D])
                with nc.Block() as block:

                    @block.sync
                    def _(sp):
                        for r_, s_ in zip(raws, (qg, qu, qd)):
                            sp.dma_start(r_[:], s_).then_inc(sem("dma_w"), 16)
                        sp.dma_start(sdb[:], sd.partition_broadcast(P)).then_inc(sem("dma_w2"), 16)
                        sp.dma_start(scg[:], sg).then_inc(sem("dma_w2"), 16)
                        sp.dma_start(scu[:], su).then_inc(sem("dma_w2"), 16)

                    @block.vector
                    def _(dve):
                        dve.wait_ge(sem("dma_w"), 48)
                        dve.wait_ge(sem("dma_w2"), 48)
                        for k in range(3):
                            dve.tensor_scalar(w32[k][:], raws[k][:], -ZERO_POINT, None, ALU.add).then_inc(sem("v1"), 1)
                        dve.wait_ge(sem("v1"), 3)
                        dve.tensor_tensor(w32[2][:], w32[2][:], sdb[:].unsqueeze(1).to_broadcast([P, NFQ, D]), ALU.mult).then_inc(sem("v1"), 1)
                        for k, w in enumerate((qg_, qu_, qd_)):
                            dve.wait_ge(sem("a1"), k + 1)
                            dve.tensor_tensor(w[1][:], w32[k][:], f(w[0][:]), ALU.subtract)

                    @block.scalar
                    def _(act):
                        for k, w in enumerate((qg_, qu_, qd_)):
                            act.wait_ge(sem("v1"), 4 if k == 2 else k + 1)
                            act.activation(w[0][:], w32[k][:], ACT.Copy).then_inc(sem("a1"), 1)
                phase_end()
            turned_norm(*xT)
            gated_ffn(xT, qg_, qu_, qd_, NFQ, [P] * NFQ, g_scale=scg, u_scale=scu, store=True)


def kernel(**inputs):
    import concourse.bacc as bacc
    from concourse.bass_utils import run_bass_kernel_spmd

    a = {k: np.asarray(v) for k, v in inputs.items()}

    def tiles(w, n=P):
        r = -w.shape[0] % n
        w = np.concatenate([w, np.zeros((r,) + w.shape[1:], w.dtype)]) if r else w
        return w.reshape(-1, n, *w.shape[1:]).swapaxes(0, 1)

    w_qb = a["L0_attn_w_qb"].reshape(H, DN + DR, QL)
    w_kvb = a["L0_attn_w_kvb"].reshape(H, DN + DV, KVL)
    inv = np.float32(1.0) / np.float32(10000.0) ** (np.arange(0, DR, 2, dtype=np.float32) / np.float32(DR))
    ang = np.outer(np.arange(T, dtype=np.float32), inv).astype(np.float32)
    cos, sin = np.cos(ang), np.sin(ang)
    unit = np.arange(FR)
    sel = np.tile((unit[None, :] // FE == np.arange(NE)[:, None]).astype(np.float32), (3, 1))
    up = lambda r, s: np.concatenate([r.reshape(FR, D), s]).T
    padded = lambda w: np.concatenate([w, np.zeros((NFQ * P - FQ,) + w.shape[1:], w.dtype)])
    arrays = {
        "x": tiles(a["L0_attn_hidden_states"].reshape(T, D)),
        "w_lat": tiles(np.concatenate([a["L0_attn_w_qa"], a["L0_attn_w_kva"]]).T),
        "w_qn": w_qb[:, :DN].swapaxes(0, 1),
        "w_qpe": w_qb[:, DN:].transpose(2, 0, 1),
        "w_kn": w_kvb[:, :DN].swapaxes(0, 1),
        "w_v": w_kvb[:, DN:].swapaxes(0, 1),
        "w_o": tiles(a["L0_attn_w_o"].T),
        "q_ln": a["L0_attn_q_a_ln_w"][:, None],
        "kv_ln": a["L0_attn_kv_a_ln_w"],
        "cos2": tiles(np.concatenate([cos, cos], 1)),
        "sin2": tiles(np.concatenate([-sin, sin], 1)),
        "gw": tiles(a["L0_ffn_gate_weight"].T),
        "wg": tiles(up(a["L0_ffn_gate_w"], a["L0_ffn_sh_gate_w"])),
        "wu": tiles(up(a["L0_ffn_up_w"], a["L0_ffn_sh_up_w"])),
        "wd": tiles(np.concatenate([a["L0_ffn_down_w"].transpose(0, 2, 1).reshape(FR, D), a["L0_ffn_sh_down_w"].T])),
        "sel": sel,
        "l_in": tiles(a["L1_attn_W_in"].T),
        "l_gate": tiles(a["L1_attn_W_gate"].T),
        "l_b": tiles(np.stack([a["L1_attn_b_in"], a["L1_attn_b_gate"]], 1)).swapaxes(1, 2),
        "l_lam": tiles(a["L1_attn_forget_lambda"]),
        "qg": tiles(padded(a["L1_ffn_wq_gate"]).T),
        "qu": tiles(padded(a["L1_ffn_wq_up"]).T),
        "qd": tiles(a["L1_ffn_wq_down"].T),
        "sg": tiles(a["L1_ffn_s_gate"]),
        "su": tiles(a["L1_ffn_s_up"]),
        "sd": a["L1_ffn_s_down"],
    }
    nc = bacc.Bacc("TRN2", target_bir_lowering=False, num_devices=1)
    arrays = {f"in_{k}": np.ascontiguousarray(v) for k, v in arrays.items()}
    aps = {k[3:]: nc.dram_tensor(k, v.shape, mybir.dt.from_np(v.dtype), kind="ExternalInput").ap() for k, v in arrays.items()}
    out = nc.dram_tensor("out", (P, NT, D), F32, kind="ExternalOutput").ap()
    build(nc, **aps, out=out)
    r = run_bass_kernel_spmd(nc, [arrays], core_ids=[0])
    return r.results[0]["out"].swapaxes(0, 1).reshape(1, T, D)
```

```python
from contextlib import ExitStack

import numpy as np
import concourse.bass as bass
from concourse import mybir

F32 = mybir.dt.float32
F32R = mybir.dt.float32r
BF16 = mybir.dt.bfloat16
F16 = mybir.dt.float16
I32 = mybir.dt.int32
ALU = mybir.AluOpType
ACT = mybir.ActivationFunctionType
AX = mybir.AxisListType

P = 128
T = 2048
D = 256
KD = D // P
NT = T // P
BT = 512
NB = T // BT
TPB = BT // P
H, QL, KVL, DN, DR, DV = 16, 192, 64, 128, 64, 128
DQ = KVL + DR
LAT = QL + KVL + DR
SCALE = float(DN + DR) ** -0.5
HG = 2
LN_EPS, RMS_EPS = 1e-5, 1e-6
MASKED = -1e30
NE, FE, FS = 8, 176, 352
FR = NE * FE
FM = FR + FS
NFM = -(-FM // P)
FQ = 704
NFQ = -(-FQ // P)
ZERO_POINT = 128.0
LRU_C = 8.0
LOG1P_TERMS = 9


class Chain:

    def __init__(self, eng, sem):
        self.eng, self.sem, self.n = eng, sem, 0

    def inc(self, ins):
        self.n += 1
        ins.then_inc(self.sem, 1)

    def wait(self):
        self.eng.wait_ge(self.sem, self.n)


def f(ap):
    return ap.bitcast(F32)


def build(nc, x, w_lat, w_qn, w_qpe, w_kn, w_v, w_o, q_ln, kv_ln, cos2, sin2, gw, wg, wu, wd, sel,
          l_in, l_gate, l_b, l_lam, qg, qu, qd, sg, su, sd, out):
    with ExitStack() as whole:
        sems = {}

        def sem(name):
            if name not in sems:
                sems[name] = whole.enter_context(nc.semaphore(name))
            return sems[name]

        used = {}

        def own(name):
            used[name] = used.get(name, 0) + 1
            return f"{name}_{used[name]}"

        def sb(ctx, name, shape, dt=F32):
            return ctx.enter_context(nc.sbuf_tensor(own(name), shape, dt))

        def ps(ctx, name, shape, dt=F32):
            return ctx.enter_context(nc.psum_tensor(own(name), shape, dt))

        def phase_end():
            nums = sorted(s.num for s in sems.values())
            nc.all_engine_barrier(sems_to_clear=range(nums[0], nums[-1] + 1))

        for name in ("dma_x0", "dma_x1", "dma_x2", "dma_x3", "dma_w", "dma_w2", "dma_w3", "dma_out", "gp", "dv", "ac", "a1", "a2", "a3", "a4", "p1", "p2", "p3", "p4", "p5",
                     "v1", "v2", "v3", "v4", "v5", "v6", "g1", "g2", "g3", "projected", "q_copied", "roped", "q_turned", "q_hi", "q_lo",
                     "scored", "maximum", "exped", "p_turned", "p_hi", "p_lo", "valued", "o_out"):
            sem(name)

        X = sb(whole, "X", [P, NT, D])
        ident = sb(whole, "ident", [P, P])
        identb = sb(whole, "identb", [P, P], BF16)
        maskb = sb(whole, "maskb", [P, P], BF16)
        mhalf = sb(whole, "mhalf", [P, NT * 2])
        stats = sb(whole, "stats", [P, NT, 6])
        mv = sb(whole, "mv", [P, NT, 2])
        rs = sb(whole, "rs", [P, NT])
        nmr = sb(whole, "nmr", [P, NT])

        def pool_rsqrt(pool, ch, dst, src, eps, scale=1.0):
            ch.inc(pool.tensor_scalar(dst, src, scale, eps, ALU.mult, ALU.add))
            ch.wait()
            return pool.tensor_tensor(dst, dst, mhalf[:, 0:dst.shape[1]], ALU.pow)

        def add_normed(dve, ch, t, y, tmp, varied="v2", read="v5"):
            ch.inc(dve.bn_stats(stats[:, t, :], y))
            ch.wait()
            dve.bn_aggr(mv[:, t, :], stats[:, t, :]).then_inc(sem(varied), 1)
            dve.wait_ge(sem("g1"), t + 1)
            ch.inc(dve.scalar_tensor_tensor(out=nmr[:, t:t + 1], in0=mv[:, t, 0:1], scalar=-1.0, in1=rs[:, t:t + 1],
                                            op0=ALU.mult, op1=ALU.mult))
            ch.wait()
            dve.tensor_scalar(tmp, y, rs[:, t:t + 1], nmr[:, t:t + 1], ALU.mult, ALU.add).then_inc(sem(read), 1)
            dve.wait_ge(sem(read), t + 1)
            dve.tensor_tensor(X[:, t, :], X[:, t, :], tmp, ALU.add).then_inc(sem("v6"), 1)

        with ExitStack() as att:
            kT_hi = sb(att, "kT_hi", [P, T], F32R)
            kT_lo = sb(att, "kT_lo", [P, T], F32R)
            c_hi = sb(att, "c_hi", [P, NT, 66], F16)
            c_lo = sb(att, "c_lo", [P, NT, 66], F16)
            cqT0 = sb(att, "cqT0", [P, T])
            cqT1 = sb(att, "cqT1", [QL - P, T])
            Wq0 = sb(att, "Wq0", [P, (H + 1) * DQ])
            Wq1 = sb(att, "Wq1", [QL - P, (H + 1) * DQ])
            Wvo_hi = sb(att, "Wvo_hi", [P, H // 2, D], F32R)
            Wvo_lo = sb(att, "Wvo_lo", [P, H // 2, D], F32R)
            cs = sb(att, "cs", [P, NT, DR])
            sn = sb(att, "sn", [P, NT, DR])
            with ExitStack() as pre:
                wl = sb(pre, "wl", [P, KD, LAT])
                wqn = sb(pre, "wqn", [P, H, QL])
                wqp0 = sb(pre, "wqp0", [P, H, DR])
                wqp1 = sb(pre, "wqp1", [QL - P, H, DR])
                wk = sb(pre, "wk", [P, H, KVL])
                wv = sb(pre, "wv", [P, H, KVL])
                wo = sb(pre, "wo", [P, H, D])
                qln0 = sb(pre, "qln0", [P, 1])
                qln1 = sb(pre, "qln1", [QL - P, 1])
                kln = sb(pre, "kln", [P, KVL])
                xn = sb(pre, "xn", [P, 3, D])
                xnT = sb(pre, "xnT", [P, 3, KD, P])
                kpe = sb(pre, "kpe", [P, 3, 2, DR])
                latn = sb(pre, "latn", [P, 3, LAT])
                junk = sb(pre, "junk", [P, 2, QL])
                ss = sb(pre, "ss", [P, NT, 2])
                rr = sb(pre, "rr", [P, NT, 2])
                rt = sb(pre, "rt", [P, 3, DR])
                pt = [ps(pre, f"pt{b}", [P, 512]) for b in range(2)]
                pl = [ps(pre, f"pl{b}", [P, 512]) for b in range(3)]
                pk = [ps(pre, f"pk{b}", [P, 512]) for b in range(3)]
                with nc.Block() as block:

                    @block.sync
                    def _(sp):
                        for g in range(4):
                            sp.dma_start(X[:, 4 * g:4 * g + 4, :], x[:, 4 * g:4 * g + 4, :]).then_inc(sem(f"dma_x{g}"), 16)
                        sp.dma_start(wl[:], w_lat).then_inc(sem("dma_w"), 16)
                        sp.dma_start(cs[:], cos2).then_inc(sem("dma_w2"), 16)
                        sp.dma_start(sn[:], sin2).then_inc(sem("dma_w2"), 16)

                    @block.scalar
                    def _(act):
                        w3 = sem("dma_w3")
                        act.dma_start(kln[:], kv_ln.partition_broadcast(P)).then_inc(w3, 16)
                        act.dma_start(qln0[:], q_ln[0:P, :]).then_inc(w3, 16)
                        act.dma_start(qln1[:], q_ln[P:QL, :]).then_inc(w3, 16)
                        act.dma_start(wk[:], w_kn).then_inc(w3, 16)
                        act.dma_start(wqn[:], w_qn).then_inc(w3, 16)
                        act.dma_start(wqp0[:], w_qpe[0:P]).then_inc(w3, 16)
                        act.dma_start(wqp1[:], w_qpe[P:QL]).then_inc(w3, 16)
                        act.dma_start(wv[:], w_v).then_inc(w3, 16)
                        act.dma_start(wo[:], w_o).then_inc(w3, 16)
                        for t in range(NT + 3):
                            if t < NT:
                                act.wait_ge(sem("p1"), t + 1)
                                if t >= 3:
                                    act.wait_ge(sem("p2"), t - 2)
                                act.activation(xnT[:, t % 3], pt[t % 2][:, 0:D].rearrange("p (k n) -> p k n", k=KD), ACT.Copy).then_inc(sem("a1"), 1)
                            if 1 <= t < NT + 1:
                                u = t - 1
                                act.wait_ge(sem("p2"), u + 1)
                                if u:
                                    act.wait_ge(sem("a2"), 2 * u)
                                act.activation(junk[:, 0], pl[u % 3][:, 0:QL], ACT.Square, accum_out=ss[:, u, 0:1]).then_inc(sem("a2"), 1)
                                act.activation(junk[:, 1, 0:KVL], pl[u % 3][:, QL:QL + KVL], ACT.Square,
                                               accum_out=ss[:, u, 1:2]).then_inc(sem("a2"), 1)
                            if t >= 3:
                                u = t - 3
                                sl = slice(u * P, (u + 1) * P)
                                act.wait_ge(sem("p3"), u + 1)
                                act.activation(kT_hi[:, sl], pk[u % 3][:, 2 * P:3 * P], ACT.Copy).then_inc(sem("a4"), 1)
                                act.activation(cqT0[:, sl], pk[u % 3][:, 0:P], ACT.Copy).then_inc(sem("a4"), 1)
                                act.activation(cqT1[:, sl], pk[u % 3][0:64, P:2 * P], ACT.Copy).then_inc(sem("a4"), 1)
                        for j in range(H // 2):
                            act.wait_ge(sem("p5"), j + 1)
                            act.activation(Wvo_hi[0:64, j], pk[j % 2][0:64, 0:D], ACT.Copy).then_inc(sem("a3"), 1)
                            act.activation(Wvo_hi[64:128, j], pk[j % 2][64:128, D:2 * D], ACT.Copy).then_inc(sem("a3"), 1)

                    @block.gpsimd
                    def _(pool):
                        ch = Chain(pool, sem("gp"))
                        pool.memset(mhalf[:], -0.5)
                        pool.memset(ident[:], 0.0)
                        ch.inc(pool.memset(identb[:], 0.0))
                        ch.inc(pool.memset(maskb[:], 0.0))
                        pool.memset(Wq0[:, H * DQ:], 0.0)
                        pool.memset(Wq1[:, H * DQ:], 0.0)
                        pool.memset(c_hi[:, :, 64:65], 1.0)
                        pool.memset(c_hi[:, :, 65:66], 0.0)
                        ch.inc(pool.memset(c_lo[:, :, 64:66], 0.0))
                        ch.wait()
                        ch.inc(pool.affine_select(out=ident[:], in_=ident[:], compare_op=ALU.not_equal, fill=1.0, base=0,
                                                  pattern=[[-1, P]], channel_multiplier=1))
                        ch.inc(pool.affine_select(out=identb[:], in_=identb[:], compare_op=ALU.not_equal, fill=1.0, base=0,
                                                  pattern=[[-1, P]], channel_multiplier=1))
                        ch.inc(pool.affine_select(out=maskb[:], in_=maskb[:], compare_op=ALU.is_ge, fill=MASKED, base=0,
                                                  pattern=[[-1, P]], channel_multiplier=1))
                        ch.wait()
                        pool.memset(rt[:], 0.0).then_inc(sem("g3"), 1)

                        def deviation(t):
                            pool.wait_ge(sem("v1"), t + 1)
                            pool_rsqrt(pool, ch, rs[:, t:t + 1], mv[:, t, 1:2], LN_EPS).then_inc(sem("g1"), 1)

                        deviation(0)
                        deviation(1)
                        for t in range(NT):
                            if t + 2 < NT:
                                deviation(t + 2)
                            pool.wait_ge(sem("a2"), 2 * t + 2)
                            ch.inc(pool.tensor_scalar(rr[:, t, 0:1], ss[:, t, 0:1], 1.0 / QL, RMS_EPS, ALU.mult, ALU.add))
                            ch.inc(pool.tensor_scalar(rr[:, t, 1:2], ss[:, t, 1:2], 1.0 / KVL, RMS_EPS, ALU.mult, ALU.add))
                            ch.wait()
                            pool.tensor_tensor(rr[:, t, :], rr[:, t, :], mhalf[:, 0:2], ALU.pow).then_inc(sem("g2"), 1)

                    @block.vector
                    def _(dve):
                        ch = Chain(dve, sem("dv"))

                        def variance(t):
                            if t % 4 == 0:
                                dve.wait_ge(sem(f"dma_x{t // 4}"), 16)
                            ch.inc(dve.bn_stats(stats[:, t, :], X[:, t, :]))
                            ch.wait()
                            dve.bn_aggr(mv[:, t, :], stats[:, t, :]).then_inc(sem("v1"), 1)

                        def normed(t):
                            dve.wait_ge(sem("g1"), t + 1)
                            if t >= 3:
                                dve.wait_ge(sem("p1"), t - 2)
                            dve.tensor_scalar(xn[:, t % 3, :], X[:, t, :], mv[:, t, 0:1], rs[:, t:t + 1],
                                              ALU.subtract, ALU.mult).then_inc(sem("v2"), 1)

                        def rope(t):
                            if t == 0:
                                dve.wait_ge(sem("dma_w2"), 32)
                                dve.wait_ge(sem("g3"), 1)
                            dve.wait_ge(sem("p2"), t + 1)
                            dve.wait_ge(sem("a2"), 2 * t + 2)
                            kp, r = kpe[:, t % 3], rt[:, t % 3]
                            ch.inc(dve.tensor_copy(kp[:, 0], pl[t % 3][:, QL + KVL:LAT]))
                            ch.wait()
                            dve.tensor_tensor(r[:, 0:32], kp[:, 0, 32:64], sn[:, t, 0:32], ALU.mult).then_inc(sem("dv"), 1)
                            dve.tensor_tensor(r[:, 32:64], kp[:, 0, 0:32], sn[:, t, 32:64], ALU.mult).then_inc(sem("dv"), 1)
                            dve.tensor_tensor(kp[:, 1], kp[:, 0], cs[:, t, :], ALU.mult).then_inc(sem("dv"), 1)
                            ch.n += 3

                        def latents(t):
                            dve.wait_ge(sem("g2"), t + 1)
                            if t >= 3:
                                dve.wait_ge(sem("p3"), t - 2)
                            ch.wait()
                            L, N = pl[t % 3], latn[:, t % 3]
                            ch.inc(dve.tensor_scalar(N[:, QL:QL + KVL], L[:, QL:QL + KVL], rr[:, t, 1:2], None, ALU.mult))
                            dve.tensor_tensor(N[:, QL + KVL:LAT], kpe[:, t % 3, 1], rt[:, t % 3], ALU.add)
                            dve.tensor_scalar(N[:, 0:QL], L[:, 0:QL], rr[:, t, 0:1], None, ALU.mult).then_inc(sem("v3"), 1)
                            ch.wait()
                            ch.inc(dve.tensor_copy(c_hi[:, t, 0:KVL], N[:, QL:QL + KVL]))
                            ch.wait()
                            ch.inc(dve.tensor_tensor(c_lo[:, t, 0:KVL], N[:, QL:QL + KVL], c_hi[:, t, 0:KVL], ALU.subtract))

                        def low(t):
                            dve.wait_ge(sem("a4"), 3 * t + 3)
                            sl = slice(t * P, (t + 1) * P)
                            dve.tensor_tensor(kT_lo[:, sl], pk[t % 3][:, 2 * P:3 * P], f(kT_hi[:, sl]), ALU.subtract).then_inc(sem("v4"), 1)

                        for t in range(-2, NT + 4):
                            if 0 <= t + 2 < NT:
                                variance(t + 2)
                            if 0 <= t + 1 < NT:
                                normed(t + 1)
                            if 1 <= t < NT + 1:
                                rope(t - 1)
                            if 2 <= t < NT + 2:
                                latents(t - 2)
                            if t >= 4:
                                low(t - 4)
                        dve.wait_ge(sem("dma_w3"), 16 * 9)
                        for w in (wk, wv):
                            dve.tensor_tensor(w[:], w[:], kln[:].unsqueeze(1).to_broadcast([P, H, KVL]), ALU.mult).then_inc(sem("v5"), 1)
                        q0 = Wq0[:, 0:H * DQ].rearrange("p (h d) -> p h d", h=H)
                        q1 = Wq1[:, 0:H * DQ].rearrange("p (h d) -> p h d", h=H)
                        dve.tensor_scalar(q0[:, :, KVL:DQ], wqp0[:], qln0[:], None, ALU.mult)
                        dve.tensor_scalar(q1[:, :, KVL:DQ], wqp1[:], qln1[:], None, ALU.mult)
                        for g in range(2):
                            dve.wait_ge(sem("p4"), g + 1)
                            h8 = slice(8 * g, 8 * g + 8)
                            dve.tensor_scalar(q0[:, h8, 0:KVL], pt[g][:].rearrange("p (h d) -> p h d", h=8), qln0[:], None, ALU.mult)
                            dve.tensor_scalar(q1[:, h8, 0:KVL], pl[g][0:64, :].rearrange("p (h d) -> p h d", h=8), qln1[:], None, ALU.mult)
                        for j in range(H // 2):
                            dve.wait_ge(sem("a3"), 2 * j + 2)
                            dve.tensor_tensor(Wvo_lo[0:64, j], pk[j % 2][0:64, 0:D], f(Wvo_hi[0:64, j]), ALU.subtract)
                            dve.tensor_tensor(Wvo_lo[64:128, j], pk[j % 2][64:128, D:2 * D], f(Wvo_hi[64:128, j]),
                                              ALU.subtract).then_inc(sem("v6"), 1)

                    @block.tensor
                    def _(pe):
                        def transposed(t):
                            if t == 0:
                                pe.wait_ge(sem("g3"), 1)
                            pe.wait_ge(sem("v2"), t + 1)
                            if t >= 2:
                                pe.wait_ge(sem("a1"), t - 1)
                            for k in range(KD):
                                m = pe.transpose(pt[t % 2][:, k * P:(k + 1) * P], xn[:, t % 3, k * P:(k + 1) * P], ident[:])
                            m.then_inc(sem("p1"), 1)

                        def latents(t):
                            pe.wait_ge(sem("a1"), t + 1)
                            if t >= 3:
                                pe.wait_ge(sem("v3"), t - 2)
                            for k in range(KD):
                                m = pe.matmul(pl[t % 3][:, 0:LAT], xnT[:, t % 3, k, :], wl[:, k, :], start=(k == 0), stop=(k == KD - 1))
                            m.then_inc(sem("p2"), 1)

                        def turned(t):
                            pe.wait_ge(sem("v3"), t + 1)
                            if t >= 3:
                                pe.wait_ge(sem("v4"), t - 2)
                            N, o = latn[:, t % 3], pk[t % 3]
                            pe.transpose(o[:, 0:P], N[:, 0:P], ident[:])
                            pe.transpose(o[0:64, P:2 * P], N[:, P:QL], ident[:])
                            pe.transpose(o[:, 2 * P:3 * P], N[:, QL:LAT], ident[:]).then_inc(sem("p3"), 1)

                        for t in range(NT + 3):
                            if t < NT:
                                transposed(t)
                            if t == 1:
                                pe.wait_ge(sem("dma_w"), 16)
                            if 1 <= t < NT + 1:
                                latents(t - 1)
                            if t >= 3:
                                turned(t - 3)
                        pe.wait_ge(sem("v5"), 2)
                        pe.wait_ge(sem("v4"), NT)
                        for g in range(2):
                            for j in range(8):
                                h = 8 * g + j
                                pe.matmul(pt[g][:, j * 64:(j + 1) * 64], wqn[:, h, 0:P], wk[:, h, :], start=True, stop=True)
                                m = pe.matmul(pl[g][0:64, j * 64:(j + 1) * 64], wqn[:, h, P:QL], wk[:, h, :], start=True, stop=True)
                            m.then_inc(sem("p4"), 1)
                        for j in range(H // 2):
                            if j >= 2:
                                pe.wait_ge(sem("v6"), j - 1)
                            pair = wv[:, 2 * j:2 * j + 2, :]
                            pe.matmul(pk[j % 2][:, 0:D], pair, wo[:, 2 * j, :], start=True, stop=True)
                            pe.matmul(pk[j % 2][:, D:2 * D], pair, wo[:, 2 * j + 1, :], start=True, stop=True).then_inc(sem("p5"), 1)

                phase_end()

            O = sb(att, "O", [P, NT, H * KVL])
            with ExitStack() as loop:
                qs = sb(loop, "qs", [P, 4, DQ])
                qt = sb(loop, "qt", [P, 2, DR])
                qT_hi = sb(loop, "qT_hi", [P, 2, P], F32R)
                qT_lo = sb(loop, "qT_lo", [P, 2, P], F32R)
                pr = sb(loop, "pr", [P, 3, T])
                pT_hi = sb(loop, "pT_hi", [P, 4, BT], F16)
                pT_lo = sb(loop, "pT_lo", [P, 4, BT], F16)
                cmx = sb(loop, "cmx", [P, 2, 4])
                nmx = sb(loop, "nmx", [P, 4])
                rl = sb(loop, "rl", [P, 2])
                pS = [ps(loop, f"pS{b}", [P, BT]) for b in range(4)]
                pT = [ps(loop, f"pT{b}", [P, BT]) for b in range(2)]
                pO = ps(loop, "pO", [P, BT])
                pQ = ps(loop, "pQ", [P, BT])
                NP = HG * NT
                order = [t for k in range(NT // 2) for t in (NT - 1 - k, k)]
                tile_at = lambda p: order[p % NT]
                chunk = [(p, c, min(4, tile_at(p) + 1 - 4 * c)) for p in range(NP + 1) for c in range(tile_at(p) // 4 + 1)]
                first = [next(n for n, k in enumerate(chunk) if k[0] == p) for p in range(NP + 1)] + [len(chunk)]
                n_chunks = first[NP]
                LEAD = first[1]
                LAG = 2
                QLEAD = 3
                plan = []
                behind = 0
                for p in range(1, NP + 1):
                    n = first[p + 1] - first[p]
                    placed = False
                    for k in range(n):
                        plan.append(("scores", first[p] + k))
                        last = k == n - 1
                        if k == 0:
                            plan.append(("turn", p + 1))
                        for _ in range(min(n, 2) if last else int(k < n - 2)):
                            plan.append(("probs", behind))
                            if behind >= LAG:
                                plan.append(("values", behind - LAG))
                            behind += 1
                            if last and not placed:
                                placed = True
                                plan.append(("project", p + QLEAD))
                assert behind == n_chunks
                plan += [("values", n_chunks - LAG + k) for k in range(LAG)]

                def heads(block, g, lead):
                    begun = {} if lead else {"projected": 1 + QLEAD, "q_copied": 1 + QLEAD, "roped": 1 + QLEAD, "q_turned": 2,
                                             "q_hi": 2, "q_lo": 2, "scored": LEAD, "maximum": 1}

                    def done(eng, name, item):
                        n = item + 1 - begun.get(name, 0)
                        if n > 0:
                            eng.wait_ge(sem(name), n)

                    @block.tensor
                    def _(pe):
                        def project(p):
                            turned = min(p - 1, max(1, p - QLEAD + 1))
                            if turned >= 0:
                                done(pe, "q_hi", turned)
                                done(pe, "q_lo", turned)
                            if p >= 1:
                                done(pe, "q_copied", p - 1)
                            t = tile_at(p)
                            sl = slice(t * P, (t + 1) * P)
                            ws = slice(0, DQ) if lead else bass.ds((g * HG + p // NT) * DQ, DQ)
                            pe.matmul(pQ[:, 0:DQ], cqT0[:, sl], Wq0[:, ws], start=True, stop=False)
                            pe.matmul(pQ[:, 0:DQ], cqT1[:, sl], Wq1[:, ws], start=False, stop=True).then_inc(sem("projected"), 1)

                        def turn(p):
                            done(pe, "roped", p)
                            if p >= 2:
                                done(pe, "q_copied", p + QLEAD - 2)
                            pe.transpose(pQ[:, P:2 * P], qs[:, p % 4, :], ident[:]).then_inc(sem("q_turned"), 1)

                        def scores(at):
                            p, c, n = chunk[at]
                            if c == 0:
                                done(pe, "q_hi", p)
                                done(pe, "q_lo", p)
                            if at >= 4:
                                done(pe, "exped", at - 4)
                            w = max(256, n * P)
                            o, ks = pS[at % 4][:, 0:w], slice(c * BT, c * BT + w)
                            pe.matmul(o, qT_hi[:, p % 2], kT_hi[:, ks], start=True, stop=False)
                            pe.matmul(o, qT_hi[:, p % 2], kT_lo[:, ks], start=False, stop=False)
                            if c == tile_at(p) // 4:
                                pe.matmul(pS[at % 4][:, (n - 1) * P:n * P], identb[:], maskb[:], start=False, stop=False,
                                          skip_group_check=True)
                            pe.matmul(o, qT_lo[:, p % 2], kT_hi[:, ks], start=False, stop=True).then_inc(sem("scored"), 1)

                        def probs(at):
                            p, c, n = chunk[at]
                            done(pe, "exped", at)
                            if at >= 2:
                                done(pe, "p_hi", at - 2)
                                done(pe, "p_lo", at - 2)
                            for k in range(n):
                                m = pe.transpose(pT[at % 2][:, k * P:(k + 1) * P],
                                                 pr[:, p % 3, (4 * c + k) * P:(4 * c + k + 1) * P], ident[:])
                            m.then_inc(sem("p_turned"), 1)

                        def values(at):
                            p, c, n = chunk[at]
                            done(pe, "p_hi", at)
                            done(pe, "p_lo", at)
                            if c == 0 and p >= 1:
                                done(pe, "o_out", p - 1)
                            o = pO[:, 0:KVL + 1]
                            for k in range(n):
                                ks = slice(k * P, (k + 1) * P)
                                j = 4 * c + k
                                hi, lo = pT_hi[:, at % 4, ks], pT_lo[:, at % 4, ks]
                                pe.matmul(o, hi, c_hi[:, j, 0:KVL + 1], start=(j == 0), stop=False)
                                pe.matmul(o, hi, c_lo[:, j, 0:KVL + 1], start=False, stop=False)
                                m = pe.matmul(o, lo, c_hi[:, j, 0:KVL + 1], start=False, stop=(j == tile_at(p)))
                            m.then_inc(sem("valued"), 1)

                        if lead:
                            project(0)
                            turn(0)
                            project(1)
                            turn(1)
                            project(2)
                            project(3)
                            for at in range(LEAD):
                                scores(at)
                            return
                        for step, at in plan:
                            {"project": project, "turn": turn, "scores": scores, "probs": probs, "values": values}[step](at)

                    @block.scalar
                    def _(act):
                        def q_out(p):
                            done(act, "projected", p)
                            if p >= 4:
                                done(act, "q_turned", p - 4)
                            act.activation(qs[:, p % 4], pQ[:, 0:DQ], ACT.Copy, scale=SCALE).then_inc(sem("q_copied"), 1)

                        def q_hi(p):
                            done(act, "q_turned", p)
                            act.activation(qT_hi[:, p % 2], pQ[:, P:2 * P], ACT.Copy).then_inc(sem("q_hi"), 1)

                        def exp(at):
                            p, c, n = chunk[at]
                            if c == 0:
                                done(act, "maximum", p)
                                if p >= 3:
                                    done(act, "p_turned", first[p - 2] - 1)
                            act.activation(pr[:, p % 3, c * BT:c * BT + n * P], pS[at % 4][:, 0:n * P], ACT.Exp,
                                           bias=nmx[:, p % 4:p % 4 + 1]).then_inc(sem("exped"), 1)

                        def p_hi(at):
                            n = chunk[at][2]
                            done(act, "p_turned", at)
                            if at >= 4:
                                done(act, "valued", at - 4)
                            act.activation(pT_hi[:, at % 4, 0:n * P], pT[at % 2][:, 0:n * P], ACT.Copy).then_inc(sem("p_hi"), 1)

                        if lead:
                            q_out(0)
                            q_hi(0)
                            q_out(1)
                            q_hi(1)
                            q_out(2)
                            q_out(3)
                            return
                        exped = 0
                        scored = LEAD
                        for step, at in plan:
                            if step == "scores":
                                while exped <= at - 4:
                                    exp(exped)
                                    exped += 1
                                if at + 1 in first and at + 1 > scored:
                                    scored = at + 1
                            elif step == "turn":
                                q_hi(at)
                            elif step == "probs":
                                while exped <= at:
                                    exp(exped)
                                    exped += 1
                                p_hi(at)
                                if exped < min(scored, n_chunks):
                                    exp(exped)
                                    exped += 1
                            elif step == "project":
                                q_out(at)

                    @block.gpsimd
                    def _(pool):
                        ch = Chain(pool, sem("gp"))
                        for p in range(0, 1 + QLEAD) if lead else range(1 + QLEAD, NP + 1 + QLEAD):
                            done(pool, "q_copied", p)
                            q, r, t = qs[:, p % 4, KVL:DQ], qt[:, p % 2], tile_at(p)
                            ch.inc(pool.tensor_tensor(r[:, 0:32], q[:, 32:64], sn[:, t, 0:32], ALU.mult))
                            ch.inc(pool.tensor_tensor(r[:, 32:64], q[:, 0:32], sn[:, t, 32:64], ALU.mult))
                            ch.wait()
                            ch.inc(pool.tensor_tensor(q, q, cs[:, t, :], ALU.mult))
                            ch.wait()
                            pool.tensor_tensor(q, q, r, ALU.add).then_inc(sem("roped"), 1)

                    @block.vector
                    def _(dve):
                        ch = Chain(dve, sem("dv"))

                        def q_lo(p):
                            done(dve, "q_hi", p)
                            dve.tensor_tensor(qT_lo[:, p % 2], pQ[:, P:2 * P], f(qT_hi[:, p % 2]), ALU.subtract).then_inc(sem("q_lo"), 1)

                        def maximum(at):
                            p, c, n = chunk[at]
                            n_c = tile_at(p) // 4 + 1
                            if c == 0 and p >= 4:
                                done(dve, "exped", first[p - 3] - 1)
                            done(dve, "scored", at)
                            whole_ = nmx[:, p % 4:p % 4 + 1]
                            if n_c == 1:
                                dve.tensor_reduce(whole_, pS[at % 4][:, 0:n * P], AX.X, ALU.max, negate=True).then_inc(sem("maximum"), 1)
                                return
                            ch.inc(dve.tensor_reduce(cmx[:, p % 2, c:c + 1], pS[at % 4][:, 0:n * P], AX.X, ALU.max))
                            if c == n_c - 1:
                                ch.wait()
                                dve.tensor_reduce(whole_, cmx[:, p % 2, 0:n_c], AX.X, ALU.max, negate=True).then_inc(sem("maximum"), 1)

                        def p_lo(at):
                            n = chunk[at][2]
                            done(dve, "p_hi", at)
                            dve.tensor_tensor(pT_lo[:, at % 4, 0:n * P], pT[at % 2][:, 0:n * P], pT_hi[:, at % 4, 0:n * P],
                                              ALU.subtract).then_inc(sem("p_lo"), 1)

                        def o_out(p):
                            done(dve, "valued", first[p + 1] - 1)
                            ch.inc(dve.reciprocal(rl[:, p % 2:p % 2 + 1], pO[:, KVL:KVL + 1]))
                            ch.wait()
                            dve.tensor_scalar(O[:, tile_at(p), bass.ds((g * HG + p // NT) * KVL, KVL)], pO[:, 0:KVL], rl[:, p % 2:p % 2 + 1], None,
                                              ALU.mult).then_inc(sem("o_out"), 1)

                        if lead:
                            q_lo(0)
                            q_lo(1)
                            for at in range(LEAD):
                                maximum(at)
                            return
                        turned = None
                        for step, at in plan:
                            if step != "values" and turned is not None:
                                p_lo(turned)
                                turned = None
                            if step == "scores":
                                maximum(at)
                            elif step == "turn":
                                q_lo(at)
                            elif step == "probs":
                                turned = at
                            elif step == "values" and at + 1 in first:
                                o_out(chunk[at][0])
                            if step == "values" and turned is not None:
                                p_lo(turned)
                                turned = None

                with nc.Block() as block:
                    heads(block, 0, True)
                phase_end()
                with nc.Fori(0, H // HG) as g:
                    with nc.Block() as block:
                        heads(block, g, False)
                    phase_end()

            with ExitStack() as op:
                OT_hi = sb(op, "OT_hi", [P, 2, 8, P], F32R)
                OT_lo = sb(op, "OT_lo", [P, 2, 8, P], F32R)
                tmp = sb(op, "tmp", [P, 2, D])
                pt = [[ps(op, f"po{b}{k}", [P, 512]) for k in range(2)] for b in range(2)]
                py = [ps(op, f"py{b}", [P, 512]) for b in range(2)]
                with nc.Block() as block:

                    @block.tensor
                    def _(pe):
                        def turn(t):
                            for k in range(2):
                                if t >= 2:
                                    pe.wait_ge(sem("v1"), 2 * (t - 2) + k + 1)
                                for j in range(4):
                                    m = pe.transpose(pt[t % 2][k][:, j * P:(j + 1) * P], O[:, t, (4 * k + j) * P:(4 * k + j + 1) * P], ident[:])
                                m.then_inc(sem("p1"), 1)

                        turn(0)
                        for t in range(NT):
                            if t + 1 < NT:
                                turn(t + 1)
                            pe.wait_ge(sem("v1"), 2 * t + 2)
                            if t >= 2:
                                pe.wait_ge(sem("v5"), t - 1)
                            y = py[t % 2][:, 0:D]
                            n = 0
                            for j in range(8):
                                for a, w in ((OT_hi, Wvo_hi), (OT_hi, Wvo_lo), (OT_lo, Wvo_hi)):
                                    m = pe.matmul(y, a[:, t % 2, j], w[:, j], start=(n == 0), stop=(n == 23))
                                    n += 1
                            m.then_inc(sem("p2"), 1)

                    @block.scalar
                    def _(act):
                        for t in range(NT):
                            for k in range(2):
                                act.wait_ge(sem("p1"), 2 * t + k + 1)
                                if t >= 2:
                                    act.wait_ge(sem("p2"), t - 1)
                                act.activation(OT_hi[:, t % 2, 4 * k:4 * k + 4], pt[t % 2][k][:].rearrange("p (j n) -> p j n", j=4),
                                               ACT.Copy).then_inc(sem("a1"), 1)

                    @block.gpsimd
                    def _(pool):
                        ch = Chain(pool, sem("gp"))
                        for t in range(NT):
                            pool.wait_ge(sem("v2"), t + 1)
                            pool_rsqrt(pool, ch, rs[:, t:t + 1], mv[:, t, 1:2], LN_EPS).then_inc(sem("g1"), 1)

                    @block.vector
                    def _(dve):
                        ch = Chain(dve, sem("dv"))

                        def split(t):
                            for k in range(2):
                                dve.wait_ge(sem("a1"), 2 * t + k + 1)
                                dve.tensor_tensor(OT_lo[:, t % 2, 4 * k:4 * k + 4], pt[t % 2][k][:].rearrange("p (j n) -> p j n", j=4),
                                                  f(OT_hi[:, t % 2, 4 * k:4 * k + 4]), ALU.subtract).then_inc(sem("v1"), 1)

                        split(0)
                        for t in range(NT):
                            if t + 1 < NT:
                                split(t + 1)
                            dve.wait_ge(sem("p2"), t + 1)
                            add_normed(dve, ch, t, py[t % 2][:, 0:D], tmp[:, t % 2])

                phase_end()

        def turned_norm(xT_hi, xT_lo):
            with ExitStack() as c:
                xn = sb(c, "xn", [P, 4, D])
                pt = [ps(c, f"pt{b}", [P, 512]) for b in range(4)]
                with nc.Block() as block:

                    @block.vector
                    def _(dve):
                        ch = Chain(dve, sem("dv"))

                        def centred(t):
                            dve.wait_ge(sem("g1"), t + 1)
                            if t >= 4:
                                dve.wait_ge(sem("p1"), t - 3)
                            dve.tensor_scalar(xn[:, t % 4, :], X[:, t, :], mv[:, t, 0:1], rs[:, t:t + 1],
                                              ALU.subtract, ALU.mult).then_inc(sem("v2"), 1)

                        def low(t):
                            dve.wait_ge(sem("a1"), t + 1)
                            sl = slice(t * P, (t + 1) * P)
                            dve.tensor_tensor(xT_lo[:, :, sl], pt[t % 4][:, 0:D].rearrange("p (k n) -> p k n", k=KD),
                                              f(xT_hi[:, :, sl]), ALU.subtract).then_inc(sem("v3"), 1)

                        for t in range(NT + 4):
                            if t < NT:
                                ch.inc(dve.bn_stats(stats[:, t, :], X[:, t, :]))
                                ch.wait()
                                dve.bn_aggr(mv[:, t, :], stats[:, t, :]).then_inc(sem("v1"), 1)
                            if 2 <= t < NT + 2:
                                centred(t - 2)
                            if 4 <= t:
                                low(t - 4)

                    @block.gpsimd
                    def _(pool):
                        ch = Chain(pool, sem("gp"))
                        for t in range(NT):
                            pool.wait_ge(sem("v1"), t + 1)
                            pool_rsqrt(pool, ch, rs[:, t:t + 1], mv[:, t, 1:2], LN_EPS).then_inc(sem("g1"), 1)

                    @block.tensor
                    def _(pe):
                        for t in range(NT):
                            pe.wait_ge(sem("v2"), t + 1)
                            if t >= 4:
                                pe.wait_ge(sem("v3"), t - 3)
                            for k in range(KD):
                                m = pe.transpose(pt[t % 4][:, k * P:(k + 1) * P], xn[:, t % 4, k * P:(k + 1) * P], ident[:])
                            m.then_inc(sem("p1"), 1)

                    @block.scalar
                    def _(act):
                        for t in range(NT):
                            act.wait_ge(sem("p1"), t + 1)
                            act.activation(xT_hi[:, :, t * P:(t + 1) * P], pt[t % 4][:, 0:D].rearrange("p (k n) -> p k n", k=KD),
                                           ACT.Copy).then_inc(sem("a1"), 1)
                phase_end()

        def split_weights(parts):
            with ExitStack() as c:
                width = 1760
                raw = sb(c, "raw", [P, 2, width])
                with nc.Block() as block:

                    @block.sync
                    def _(sp):
                        for n, (src, hi, lo) in enumerate(parts):
                            if n >= 2:
                                sp.wait_ge(sem("v1"), n - 1)
                            rows, cols = hi.shape[0], hi.free_size()
                            dst = raw[0:rows, n % 2, 0:cols]
                            if len(src.shape) == 3:
                                dst = dst.rearrange("p (a b) -> p a b", a=src.shape[1])
                            sp.dma_start(dst, src).then_inc(sem("dma_w" if n % 2 == 0 else "dma_w2"), 16)

                    @block.scalar
                    def _(act):
                        for n, (src, hi, lo) in enumerate(parts):
                            act.wait_ge(sem("dma_w" if n % 2 == 0 else "dma_w2"), 16 * (n // 2 + 1))
                            rows, cols = hi.shape[0], hi.free_size()
                            r = raw[0:rows, n % 2, 0:cols]
                            if len(hi.shape) == 3:
                                r = r.rearrange("p (a b) -> p a b", a=hi.shape[1])
                            act.activation(hi, r, ACT.Copy).then_inc(sem("a1"), 1)

                    @block.vector
                    def _(dve):
                        for n, (src, hi, lo) in enumerate(parts):
                            dve.wait_ge(sem("a1"), n + 1)
                            rows, cols = hi.shape[0], hi.free_size()
                            r = raw[0:rows, n % 2, 0:cols]
                            if len(hi.shape) == 3:
                                r = r.rearrange("p (a b) -> p a b", a=hi.shape[1])
                            dve.tensor_tensor(lo, r, f(hi), ALU.subtract).then_inc(sem("v1"), 1)
                phase_end()

        def gated_ffn(xT, wg_, wu_, wd_, n_m, rows, n_routed=0, selb=None, wT=None, g_scale=None, u_scale=None, store=False):
            with ExitStack() as c:
                sgb = sb(c, "sgb", [P, 2, BT])
                hb = sb(c, "hb", [P, 2, BT])
                h_hi = sb(c, "h_hi", [P, 3, BT], F32R)
                h_lo = sb(c, "h_lo", [P, 3, BT], F32R)
                y = sb(c, "y", [P, TPB, D])
                tmp = sb(c, "tmp", [P, 2, D])
                pG = [ps(c, f"pG{b}", [P, BT]) for b in range(2)]
                pU = [ps(c, f"pU{b}", [P, BT]) for b in range(2)]
                pW = [ps(c, f"pW{b}", [P, BT]) for b in range(2)]
                pY = [ps(c, f"pY{b}", [P, 2, D]) for b in range(2)]
                N = NB * n_m

                def routed(n):
                    return n % n_m < n_routed

                def n_scaled(n):
                    return (n // n_m) * n_routed + min(n % n_m + 1, n_routed)

                with nc.Block() as block:

                    @block.tensor
                    def _(pe):
                        def up(n):
                            tb, m = divmod(n, n_m)
                            b, r, ts = n % 2, rows[m], slice(tb * BT, (tb + 1) * BT)
                            fs = slice(m * P, m * P + r)
                            if n >= 2:
                                pe.wait_ge(sem("a1"), n - 1)
                                pe.wait_ge(sem("v1"), n - 1)
                            for out_, w in ((pG[b], wg_), (pU[b], wu_)):
                                q = 0
                                for k in range(KD):
                                    for i, j in ((0, 0), (0, 1), (1, 0)):
                                        mm = pe.matmul(out_[0:r, :], w[i][:, k, fs], xT[j][:, k, ts], start=(q == 0), stop=(q == 5))
                                        q += 1
                            if routed(n):
                                if n_scaled(n) > 2:
                                    pe.wait_ge(sem("v2"), n_scaled(n) - 2)
                                mm = pe.matmul(pW[(n_scaled(n) - 1) % 2][0:r, :], selb[:, fs], wT[:, ts], start=True, stop=True)
                            mm.then_inc(sem("p1"), 1)

                        def down(n):
                            tb, m = divmod(n, n_m)
                            b, r = n % 2, rows[m]
                            pe.wait_ge(sem("a2"), n + 1)
                            pe.wait_ge(sem("v3"), n + 1)
                            if m == 0 and tb:
                                pe.wait_ge(sem("a3"), 2 * tb)
                            for q in range(TPB):
                                qs_ = slice(q * P, (q + 1) * P)
                                for j, (a, w) in enumerate(((h_hi, wd_[0]), (h_hi, wd_[1]), (h_lo, wd_[0]))):
                                    mm = pe.matmul(pY[q // 2][:, q % 2, :], a[0:r, n % 3, qs_], w[0:r, m, :],
                                                   start=(m == 0 and q % 2 == 0 and j == 0), stop=(m == n_m - 1 and j == 2),
                                                   skip_group_check=True)
                            mm.then_inc(sem("p2"), 1)

                        up(0)
                        up(1)
                        for n in range(N):
                            if n + 2 < N:
                                up(n + 2)
                            down(n)

                    @block.scalar
                    def _(act):
                        def silu(n):
                            b, m = n % 2, n % n_m
                            r = rows[m]
                            act.wait_ge(sem("p1"), n + 1)
                            if n >= 2:
                                act.wait_ge(sem("v1"), n - 1)
                            kw = {"scale": g_scale[0:r, m:m + 1]} if g_scale is not None else {}
                            act.activation(sgb[0:r, b], pG[b][0:r, :], ACT.Silu, **kw).then_inc(sem("a1"), 1)

                        silu(0)
                        for n in range(N):
                            tb, m = divmod(n, n_m)
                            b, r = n % 2, rows[m]
                            if routed(n):
                                act.wait_ge(sem("v2"), n_scaled(n))
                            else:
                                act.wait_ge(sem("v1"), n + 1)
                            if n >= 3:
                                act.wait_ge(sem("p2"), n - 2)
                            act.activation(h_hi[0:r, n % 3], hb[0:r, b], ACT.Copy).then_inc(sem("a2"), 1)
                            if n + 1 < N:
                                silu(n + 1)
                            if m == n_m - 1:
                                act.wait_ge(sem("p2"), n + 1)
                                if tb:
                                    act.wait_ge(sem("v5"), TPB * tb)
                                for k in range(2):
                                    act.activation(y[:, 2 * k:2 * k + 2, :], pY[k][:], ACT.Copy).then_inc(sem("a3"), 1)

                    @block.gpsimd
                    def _(pool):
                        ch = Chain(pool, sem("gp"))
                        for t in range(NT):
                            pool.wait_ge(sem("v4"), t + 1)
                            pool_rsqrt(pool, ch, rs[:, t:t + 1], mv[:, t, 1:2], LN_EPS).then_inc(sem("g1"), 1)

                    @block.vector
                    def _(dve):
                        ch = Chain(dve, sem("dv"))

                        def hidden(n):
                            b, m = n % 2, n % n_m
                            r = rows[m]
                            dve.wait_ge(sem("a1"), n + 1)
                            if n >= 2:
                                dve.wait_ge(sem("a2"), n - 1)
                                dve.wait_ge(sem("v3"), n - 1)
                            if u_scale is not None:
                                dve.scalar_tensor_tensor(out=hb[0:r, b], in0=pU[b][0:r, :], scalar=u_scale[0:r, m:m + 1],
                                                         in1=sgb[0:r, b], op0=ALU.mult, op1=ALU.mult).then_inc(sem("v1"), 1)
                            else:
                                dve.tensor_tensor(hb[0:r, b], pU[b][0:r, :], sgb[0:r, b], ALU.mult).then_inc(sem("v1"), 1)
                            if routed(n):
                                dve.wait_ge(sem("v1"), n + 1)
                                dve.tensor_tensor(hb[0:r, b], pW[(n_scaled(n) - 1) % 2][0:r, :], hb[0:r, b], ALU.mult).then_inc(sem("v2"), 1)

                        def block_out(tb):
                            dve.wait_ge(sem("a3"), 2 * tb + 2)
                            for q in range(TPB):
                                add_normed(dve, ch, tb * TPB + q, y[:, q, :], tmp[:, q % 2], "v4", "v5")

                        hidden(0)
                        for n in range(N):
                            tb, m = divmod(n, n_m)
                            b, r = n % 2, rows[m]
                            dve.wait_ge(sem("a2"), n + 1)
                            if n >= 3:
                                dve.wait_ge(sem("p2"), n - 2)
                            dve.tensor_tensor(h_lo[0:r, n % 3], hb[0:r, b], f(h_hi[0:r, n % 3]), ALU.subtract).then_inc(sem("v3"), 1)
                            if n + 1 < N:
                                hidden(n + 1)
                            if m == 1 and tb:
                                block_out(tb - 1)
                        block_out(NB - 1)

                    if store:
                        @block.sync
                        def _(sp):
                            for tb in range(NB):
                                sp.wait_ge(sem("v6"), TPB * (tb + 1))
                                sp.dma_start(out[:, tb * TPB:(tb + 1) * TPB, :], X[:, tb * TPB:(tb + 1) * TPB, :]).then_inc(sem("dma_out"), 16)
                            sp.wait_ge(sem("dma_out"), 16 * NB)
                if not store:
                    phase_end()

        with ExitStack() as moe:
            xT = [sb(moe, f"xT{k}", [P, KD, T], F32R) for k in range(2)]
            wg_ = [sb(moe, f"wg_{k}", [P, KD, FM], F32R) for k in range(2)]
            wu_ = [sb(moe, f"wu_{k}", [P, KD, FM], F32R) for k in range(2)]
            wd_ = [sb(moe, f"wd_{k}", [P, NFM, D], F32R) for k in range(2)]
            gwr = sb(moe, "gwr", [P, KD, P])
            gw_ = [sb(moe, f"gw_{k}", [P, KD, P], F32R) for k in range(2)]
            selb = sb(moe, "selb", [3 * NE, FR], BF16)
            wT = sb(moe, "wT", [3 * NE, T], BF16)
            tri = sb(moe, "tri", [P, NE, NE])
            split_weights([(w[:, k, :], h_[0][:, k, :], h_[1][:, k, :]) for w, h_ in ((wg, wg_), (wu, wu_)) for k in range(KD)]
                          + [(wd[0:P, 0:6, :], wd_[0][:, 0:6], wd_[1][:, 0:6]), (wd[0:P, 6:12, :], wd_[0][:, 6:12], wd_[1][:, 6:12]),
                             (wd[0:P, 12:13, :], wd_[0][:, 12:13], wd_[1][:, 12:13]),
                             (wd[0:FM - 13 * P, 13:14, :], wd_[0][0:FM - 13 * P, 13:14], wd_[1][0:FM - 13 * P, 13:14])])
            turned_norm(*xT)
            with ExitStack() as c:
                self32 = sb(c, "self32", [3 * NE, FR])
                lgT = sb(c, "lgT", [NE, T])
                L = sb(c, "L", [P, NT, NE])
                S = sb(c, "S", [P, NT, NE])
                M = sb(c, "M", [P, NT, NE])
                R = sb(c, "R", [P, NT, NE])
                small = sb(c, "small", [P, 3, NT])
                G = sb(c, "G", [P, 2, NT, 4])
                cmp1 = sb(c, "cmp1", [P, NT, NE, NE])
                cmp2 = sb(c, "cmp2", [P, NT, NE, NE])
                w3 = sb(c, "w3", [P, NT, 3 * NE], BF16)
                pg = [ps(c, f"pg{b}", [P, BT]) for b in range(2)]
                pr_ = ps(c, "pr_", [P, 512])
                pw = [ps(c, f"pw{b}", [P, 1024], BF16) for b in range(2)]
                with nc.Block() as block:

                    @block.sync
                    def _(sp):
                        sp.dma_start(self32[:], sel).then_inc(sem("dma_w"), 16)
                        sp.wait_ge(sem("gp"), 1)
                        sp.dma_start(gwr[:, :, 0:NE], gw).then_inc(sem("dma_w2"), 16)

                    @block.gpsimd
                    def _(pool):
                        pool.memset(gwr[:], 0.0).then_inc(sem("gp"), 1)
                        pool.memset(tri[:], 1.0).then_inc(sem("gp"), 1)
                        pool.wait_ge(sem("gp"), 2)
                        pool.affine_select(out=tri[:], in_=tri[:], compare_op=ALU.is_gt, fill=0.0, base=0,
                                           pattern=[[1, NE], [-1, NE]], channel_multiplier=0).then_inc(sem("g1"), 1)
                        pool.wait_ge(sem("dma_w"), 16)
                        pool.tensor_copy(selb[:], self32[:]).then_inc(sem("g2"), 1)

                    @block.scalar
                    def _(act):
                        act.wait_ge(sem("dma_w2"), 16)
                        act.activation(gw_[0][:], gwr[:], ACT.Copy).then_inc(sem("a1"), 1)
                        for tb in range(NB):
                            act.wait_ge(sem("p1"), tb + 1)
                            act.activation(lgT[:, tb * BT:(tb + 1) * BT], pg[tb % 2][0:NE, :], ACT.Copy).then_inc(sem("a2"), 1)
                        act.wait_ge(sem("v2"), 1)
                        act.activation(S[:], S[:], ACT.Exp).then_inc(sem("a3"), 1)
                        for b in range(2):
                            act.wait_ge(sem("p3"), b + 1)
                            act.activation(wT[:, b * 1024:(b + 1) * 1024], pw[b][0:3 * NE, :], ACT.Copy).then_inc(sem("a4"), 1)

                    @block.tensor
                    def _(pe):
                        pe.wait_ge(sem("v1"), 1)
                        for tb in range(NB):
                            if tb >= 2:
                                pe.wait_ge(sem("a2"), tb - 1)
                            q = 0
                            for k in range(KD):
                                for i, j in ((0, 0), (0, 1), (1, 0)):
                                    mm = pe.matmul(pg[tb % 2][:], gw_[i][:, k, :], xT[j][:, k, tb * BT:(tb + 1) * BT], start=(q == 0), stop=(q == 5))
                                    q += 1
                            mm.then_inc(sem("p1"), 1)
                        pe.wait_ge(sem("a2"), NB)
                        for t in range(NT):
                            mm = pe.transpose(pr_[:, t * NE:(t + 1) * NE], lgT[:, t * P:(t + 1) * P], ident[0:NE, 0:NE])
                        mm.then_inc(sem("p2"), 1)
                        pe.wait_ge(sem("v3"), 1)
                        for b in range(2):
                            for t in range(8):
                                mm = pe.transpose(pw[b][0:3 * NE, t * P:(t + 1) * P], w3[:, 8 * b + t, :], identb[:])
                            mm.then_inc(sem("p3"), 1)

                    @block.vector
                    def _(dve):
                        ch = Chain(dve, sem("dv"))

                        def step(ins):
                            ch.inc(ins)
                            ch.wait()

                        def wide(ap, n):
                            return ap.unsqueeze(3).to_broadcast([P, NT, n, n])

                        def ranks(dst, src, n):
                            mine, other = wide(src, n), src.unsqueeze(2).to_broadcast([P, NT, n, n])
                            a, b = cmp1[:, :, 0:n, 0:n], cmp2[:, :, 0:n, 0:n]
                            ch.inc(dve.tensor_tensor(a, other, mine, ALU.is_gt))
                            step(dve.tensor_tensor(b, other, mine, ALU.is_equal))
                            step(dve.tensor_tensor(b, b, tri[:, 0:n, 0:n].unsqueeze(1).to_broadcast([P, NT, n, n]), ALU.mult))
                            step(dve.tensor_tensor(a, a, b, ALU.add))
                            step(dve.tensor_reduce(dst, a, AX.X, ALU.add))

                        def over(ap, n=NE):
                            return ap.unsqueeze(2).to_broadcast([P, NT, n])

                        dve.wait_ge(sem("a1"), 1)
                        dve.tensor_tensor(gw_[1][:], gwr[:], f(gw_[0][:]), ALU.subtract).then_inc(sem("v1"), 1)
                        dve.wait_ge(sem("p2"), 1)
                        step(dve.tensor_copy(L[:], pr_[:, 0:NT * NE].rearrange("p (t e) -> p t e", e=NE)))
                        step(dve.tensor_reduce(small[:, 0, :], L[:], AX.X, ALU.max))
                        dve.tensor_tensor(S[:], L[:], over(small[:, 0, :]), ALU.subtract).then_inc(sem("v2"), 1)
                        dve.wait_ge(sem("a3"), 1)
                        step(dve.tensor_reduce(small[:, 1, :], S[:], AX.X, ALU.add))
                        step(dve.reciprocal(small[:, 2, :], small[:, 1, :]))
                        step(dve.tensor_tensor(S[:], S[:], over(small[:, 2, :]), ALU.mult))
                        step(dve.tensor_reduce(G[:, 0], S[:].rearrange("p t (g e) -> p t g e", e=2), AX.X, ALU.max))
                        dve.wait_ge(sem("g1"), 1)
                        ranks(G[:, 1], G[:, 0], 4)
                        step(dve.tensor_scalar(G[:, 1], G[:, 1], 1.5, None, ALU.is_lt))
                        step(dve.tensor_tensor(M[:].rearrange("p t (g e) -> p t g e", e=2), S[:].rearrange("p t (g e) -> p t g e", e=2),
                                               G[:, 1].unsqueeze(3).to_broadcast([P, NT, 4, 2]), ALU.mult))
                        ranks(R[:], M[:], NE)
                        step(dve.tensor_scalar(R[:], R[:], 1.5, None, ALU.is_lt))
                        step(dve.tensor_tensor(M[:], M[:], R[:], ALU.mult))
                        step(dve.tensor_copy(w3[:, :, 0:NE], M[:]))
                        step(dve.tensor_tensor(M[:], M[:], w3[:, :, 0:NE], ALU.subtract))
                        step(dve.tensor_copy(w3[:, :, NE:2 * NE], M[:]))
                        step(dve.tensor_tensor(M[:], M[:], w3[:, :, NE:2 * NE], ALU.subtract))
                        dve.tensor_copy(w3[:, :, 2 * NE:3 * NE], M[:]).then_inc(sem("v3"), 1)
                phase_end()
            gated_ffn(xT, wg_, wu_, wd_, NFM, [P] * 13 + [FM - 13 * P], n_routed=FR // P, selb=selb, wT=wT)

        with ExitStack() as lru:
            xT = [sb(lru, f"xT{k}", [P, KD, T], F32R) for k in range(2)]
            wi_ = [sb(lru, f"wi_{k}", [P, KD, D], F32R) for k in range(2)]
            wr_ = [sb(lru, f"wr_{k}", [P, KD, D], F32R) for k in range(2)]
            split_weights([(l_in, wi_[0][:], wi_[1][:]), (l_gate, wr_[0][:], wr_[1][:])])
            turned_norm(*xT)
            with ExitStack() as c:
                si = sb(c, "si", [P, KD, T])
                al = sb(c, "al", [P, KD, T])
                be = sb(c, "be", [P, KD, T])
                xs = sb(c, "xs", [P, KD, T])
                lb = sb(c, "lb", [P, 2, KD])
                lam = sb(c, "lam", [P, KD])
                z = sb(c, "z", [P, 6, KD])
                tmp = sb(c, "tmp", [P, 2, D])
                eps = sb(c, "eps", [P, 1])
                pg = [ps(c, f"pg{b}", [P, BT]) for b in range(4)]
                py = [ps(c, f"py{b}", [P, 512]) for b in range(2)]
                gates = [(tb, e, w) for e in range(KD) for tb in range(NB) for w in range(2)]
                with nc.Block() as block:

                    @block.sync
                    def _(sp):
                        sp.dma_start(lb[:], l_b).then_inc(sem("dma_w"), 16)
                        sp.dma_start(lam[:], l_lam).then_inc(sem("dma_w"), 16)

                    @block.tensor
                    def _(pe):
                        for n, (tb, e, w) in enumerate(gates):
                            if n >= 4:
                                pe.wait_ge(sem("a1"), n - 3)
                            wts = (wi_, wr_)[w]
                            q = 0
                            for k in range(KD):
                                for i, j in ((0, 0), (0, 1), (1, 0)):
                                    mm = pe.matmul(pg[n % 4][:], wts[i][:, k, e * P:(e + 1) * P], xT[j][:, k, tb * BT:(tb + 1) * BT],
                                                   start=(q == 0), stop=(q == 5))
                                    q += 1
                            mm.then_inc(sem("p1"), 1)
                        for t in range(NT):
                            if t == 0:
                                pe.wait_ge(sem("v2"), KD)
                            if t >= 2:
                                pe.wait_ge(sem("v5"), t - 1)
                            for k in range(KD):
                                mm = pe.transpose(py[t % 2][:, k * P:(k + 1) * P], xs[:, k, t * P:(t + 1) * P], ident[:])
                            mm.then_inc(sem("p2"), 1)

                    @block.scalar
                    def _(act):
                        act.wait_ge(sem("dma_w"), 32)
                        act.wait_ge(sem("v3"), 1)
                        act.activation(z[:, 0, :], z[:, 1, :], ACT.Exp, scale=-1.0).then_inc(sem("a2"), 1)
                        for n, (tb, e, w) in enumerate(gates):
                            act.wait_ge(sem("p1"), n + 1)
                            dst = (si, al)[w][:, e, tb * BT:(tb + 1) * BT]
                            act.activation(dst, pg[n % 4][:], ACT.Sigmoid, bias=lb[:, w, e:e + 1]).then_inc(sem("a1"), 1)
                        act.wait_ge(sem("v3"), 2)
                        act.wait_ge(sem("a1"), len(gates))
                        for e in range(KD):
                            act.activation(al[:, e, :], al[:, e, :], ACT.Exp, scale=z[:, 5, e:e + 1]).then_inc(sem("a3"), 1)
                        for e in range(KD):
                            act.wait_ge(sem("v1"), e + 1)
                            act.activation(be[:, e, :], be[:, e, :], ACT.Sqrt, bias=eps[:]).then_inc(sem("a4"), 1)

                    @block.gpsimd
                    def _(pool):
                        pool.memset(eps[:], 1e-6).then_inc(sem("g2"), 1)
                        ch = Chain(pool, sem("gp"))
                        for t in range(NT):
                            pool.wait_ge(sem("v4"), t + 1)
                            pool_rsqrt(pool, ch, rs[:, t:t + 1], mv[:, t, 1:2], LN_EPS).then_inc(sem("g1"), 1)

                    @block.vector
                    def _(dve):
                        ch = Chain(dve, sem("dv"))

                        def step(ins):
                            ch.inc(ins)
                            ch.wait()

                        dve.wait_ge(sem("dma_w"), 32)
                        step(dve.tensor_scalar(z[:, 1, :], lam[:], -1.0, None, ALU.mult))
                        dve.tensor_tensor(z[:, 1, :], z[:, 1, :], lam[:], ALU.max).then_inc(sem("v3"), 1)
                        dve.wait_ge(sem("a2"), 1)
                        step(dve.tensor_scalar(z[:, 2, :], z[:, 0, :], 2.0, None, ALU.add))
                        step(dve.reciprocal(z[:, 2, :], z[:, 2, :]))
                        step(dve.tensor_tensor(z[:, 2, :], z[:, 2, :], z[:, 0, :], ALU.mult))
                        step(dve.tensor_tensor(z[:, 3, :], z[:, 2, :], z[:, 2, :], ALU.mult))
                        step(dve.tensor_scalar(z[:, 4, :], z[:, 3, :], 1.0 / (2 * LOG1P_TERMS + 1), None, ALU.mult))
                        for k in range(LOG1P_TERMS - 1, 0, -1):
                            step(dve.scalar_tensor_tensor(out=z[:, 4, :], in0=z[:, 4, :], scalar=1.0 / (2 * k + 1), in1=z[:, 3, :],
                                                          op0=ALU.add, op1=ALU.mult))
                        step(dve.scalar_tensor_tensor(out=z[:, 4, :], in0=z[:, 4, :], scalar=1.0, in1=z[:, 2, :],
                                                      op0=ALU.add, op1=ALU.mult))
                        step(dve.tensor_scalar(z[:, 0, :], lam[:], 0.0, -LRU_C, ALU.max, ALU.mult))
                        dve.scalar_tensor_tensor(out=z[:, 5, :], in0=z[:, 4, :], scalar=-2.0 * LRU_C, in1=z[:, 0, :],
                                                 op0=ALU.mult, op1=ALU.add).then_inc(sem("v3"), 1)
                        for e in range(KD):
                            step(dve.tensor_tensor(xs[:, e, :], f(xT[0][:, e, :]), f(xT[1][:, e, :]), ALU.add))
                        dve.wait_ge(sem("a1"), len(gates))
                        for e in range(KD):
                            step(dve.tensor_tensor(si[:, e, :], si[:, e, :], xs[:, e, :], ALU.mult))
                        for e in range(KD):
                            dve.wait_ge(sem("a3"), e + 1)
                            step(dve.tensor_tensor(be[:, e, :], al[:, e, :], al[:, e, :], ALU.mult))
                            if e == 0:
                                dve.wait_ge(sem("g2"), 1)
                            dve.tensor_scalar(be[:, e, :], be[:, e, :], -1.0, 1.0, ALU.mult, ALU.add).then_inc(sem("v1"), 1)
                        for e in range(KD):
                            dve.wait_ge(sem("a4"), e + 1)
                            step(dve.tensor_tensor(be[:, e, :], be[:, e, :], si[:, e, :], ALU.mult))
                            dve.tensor_tensor_scan(xs[:, e, :], al[:, e, :], be[:, e, :], 0.0, ALU.mult, ALU.add).then_inc(sem("v2"), 1)
                        for t in range(NT):
                            dve.wait_ge(sem("p2"), t + 1)
                            add_normed(dve, ch, t, py[t % 2][:, 0:D], tmp[:, t % 2], "v4", "v5")
                phase_end()

        with ExitStack() as ffn:
            xT = [sb(ffn, f"xT{k}", [P, KD, T], F32R) for k in range(2)]
            qg_ = [sb(ffn, f"qg_{k}", [P, KD, NFQ * P], F32R) for k in range(2)]
            qu_ = [sb(ffn, f"qu_{k}", [P, KD, NFQ * P], F32R) for k in range(2)]
            qd_ = [sb(ffn, f"qd_{k}", [P, NFQ, D], F32R) for k in range(2)]
            scg = sb(ffn, "scg", [P, NFQ])
            scu = sb(ffn, "scu", [P, NFQ])
            with ExitStack() as c:
                raws = [sb(c, "rawg", [P, KD, NFQ * P], I32), sb(c, "rawu", [P, KD, NFQ * P], I32), sb(c, "rawd", [P, NFQ, D], I32)]
                w32 = [sb(c, "w32g", [P, KD, NFQ * P]), sb(c, "w32u", [P, KD, NFQ * P]), sb(c, "w32d", [P, NFQ, D])]
                sdb = sb(c, "sdb", [P, D])
                with nc.Block() as block:

                    @block.sync
                    def _(sp):
                        for r_, s_ in zip(raws, (qg, qu, qd)):
                            sp.dma_start(r_[:], s_).then_inc(sem("dma_w"), 16)
                        sp.dma_start(sdb[:], sd.partition_broadcast(P)).then_inc(sem("dma_w2"), 16)
                        sp.dma_start(scg[:], sg).then_inc(sem("dma_w2"), 16)
                        sp.dma_start(scu[:], su).then_inc(sem("dma_w2"), 16)

                    @block.vector
                    def _(dve):
                        dve.wait_ge(sem("dma_w"), 48)
                        dve.wait_ge(sem("dma_w2"), 48)
                        for k in range(3):
                            dve.tensor_scalar(w32[k][:], raws[k][:], -ZERO_POINT, None, ALU.add).then_inc(sem("v1"), 1)
                        dve.wait_ge(sem("v1"), 3)
                        dve.tensor_tensor(w32[2][:], w32[2][:], sdb[:].unsqueeze(1).to_broadcast([P, NFQ, D]), ALU.mult).then_inc(sem("v1"), 1)
                        for k, w in enumerate((qg_, qu_, qd_)):
                            dve.wait_ge(sem("a1"), k + 1)
                            dve.tensor_tensor(w[1][:], w32[k][:], f(w[0][:]), ALU.subtract)

                    @block.scalar
                    def _(act):
                        for k, w in enumerate((qg_, qu_, qd_)):
                            act.wait_ge(sem("v1"), 4 if k == 2 else k + 1)
                            act.activation(w[0][:], w32[k][:], ACT.Copy).then_inc(sem("a1"), 1)
                phase_end()
            turned_norm(*xT)
            gated_ffn(xT, qg_, qu_, qd_, NFQ, [P] * NFQ, g_scale=scg, u_scale=scu, store=True)


def kernel(**inputs):
    import concourse.bacc as bacc
    from concourse.bass_utils import run_bass_kernel_spmd

    a = {k: np.asarray(v) for k, v in inputs.items()}

    def tiles(w, n=P):
        r = -w.shape[0] % n
        w = np.concatenate([w, np.zeros((r,) + w.shape[1:], w.dtype)]) if r else w
        return w.reshape(-1, n, *w.shape[1:]).swapaxes(0, 1)

    w_qb = a["L0_attn_w_qb"].reshape(H, DN + DR, QL)
    w_kvb = a["L0_attn_w_kvb"].reshape(H, DN + DV, KVL)
    inv = np.float32(1.0) / np.float32(10000.0) ** (np.arange(0, DR, 2, dtype=np.float32) / np.float32(DR))
    ang = np.outer(np.arange(T, dtype=np.float32), inv).astype(np.float32)
    cos, sin = np.cos(ang), np.sin(ang)
    unit = np.arange(FR)
    sel = np.tile((unit[None, :] // FE == np.arange(NE)[:, None]).astype(np.float32), (3, 1))
    up = lambda r, s: np.concatenate([r.reshape(FR, D), s]).T
    padded = lambda w: np.concatenate([w, np.zeros((NFQ * P - FQ,) + w.shape[1:], w.dtype)])
    arrays = {
        "x": tiles(a["L0_attn_hidden_states"].reshape(T, D)),
        "w_lat": tiles(np.concatenate([a["L0_attn_w_qa"], a["L0_attn_w_kva"]]).T),
        "w_qn": w_qb[:, :DN].swapaxes(0, 1),
        "w_qpe": w_qb[:, DN:].transpose(2, 0, 1),
        "w_kn": w_kvb[:, :DN].swapaxes(0, 1),
        "w_v": w_kvb[:, DN:].swapaxes(0, 1),
        "w_o": tiles(a["L0_attn_w_o"].T),
        "q_ln": a["L0_attn_q_a_ln_w"][:, None],
        "kv_ln": a["L0_attn_kv_a_ln_w"],
        "cos2": tiles(np.concatenate([cos, cos], 1)),
        "sin2": tiles(np.concatenate([-sin, sin], 1)),
        "gw": tiles(a["L0_ffn_gate_weight"].T),
        "wg": tiles(up(a["L0_ffn_gate_w"], a["L0_ffn_sh_gate_w"])),
        "wu": tiles(up(a["L0_ffn_up_w"], a["L0_ffn_sh_up_w"])),
        "wd": tiles(np.concatenate([a["L0_ffn_down_w"].transpose(0, 2, 1).reshape(FR, D), a["L0_ffn_sh_down_w"].T])),
        "sel": sel,
        "l_in": tiles(a["L1_attn_W_in"].T),
        "l_gate": tiles(a["L1_attn_W_gate"].T),
        "l_b": tiles(np.stack([a["L1_attn_b_in"], a["L1_attn_b_gate"]], 1)).swapaxes(1, 2),
        "l_lam": tiles(a["L1_attn_forget_lambda"]),
        "qg": tiles(padded(a["L1_ffn_wq_gate"]).T),
        "qu": tiles(padded(a["L1_ffn_wq_up"]).T),
        "qd": tiles(a["L1_ffn_wq_down"].T),
        "sg": tiles(a["L1_ffn_s_gate"]),
        "su": tiles(a["L1_ffn_s_up"]),
        "sd": a["L1_ffn_s_down"],
    }
    nc = bacc.Bacc("TRN2", target_bir_lowering=False, num_devices=1)
    arrays = {f"in_{k}": np.ascontiguousarray(v) for k, v in arrays.items()}
    aps = {k[3:]: nc.dram_tensor(k, v.shape, mybir.dt.from_np(v.dtype), kind="ExternalInput").ap() for k, v in arrays.items()}
    out = nc.dram_tensor("out", (P, NT, D), F32, kind="ExternalOutput").ap()
    build(nc, **aps, out=out)
    r = run_bass_kernel_spmd(nc, [arrays], core_ids=[0])
    return r.results[0]["out"].swapaxes(0, 1).reshape(1, T, D)
```

```python
from contextlib import ExitStack

import numpy as np
import concourse.bass as bass
from concourse import mybir

F32 = mybir.dt.float32
F32R = mybir.dt.float32r
BF16 = mybir.dt.bfloat16
F16 = mybir.dt.float16
I32 = mybir.dt.int32
ALU = mybir.AluOpType
ACT = mybir.ActivationFunctionType
AX = mybir.AxisListType

P = 128
T = 2048
D = 256
KD = D // P
NT = T // P
BT = 512
NB = T // BT
TPB = BT // P
H, QL, KVL, DN, DR, DV = 16, 192, 64, 128, 64, 128
DQ = KVL + DR
LAT = QL + KVL + DR
SCALE = float(DN + DR) ** -0.5
SLOTS = 5
HG = 4
LN_EPS, RMS_EPS = 1e-5, 1e-6
MASKED = -1e30
NE, FE, FS = 8, 176, 352
FR = NE * FE
FM = FR + FS
NFM = -(-FM // P)
FQ = 704
NFQ = -(-FQ // P)
ZERO_POINT = 128.0
LRU_C = 8.0
LOG1P_TERMS = 9


class Chain:

    def __init__(self, eng, sem):
        self.eng, self.sem, self.n = eng, sem, 0

    def inc(self, ins):
        self.n += 1
        ins.then_inc(self.sem, 1)

    def wait(self):
        self.eng.wait_ge(self.sem, self.n)


def f(ap):
    return ap.bitcast(F32)


def build(nc, x, w_lat, w_qn, w_qpe, w_kn, w_v, w_o, q_ln, kv_ln, cos2, sin2, gw, wg, wu, wd, sel,
          l_in, l_gate, l_b, l_lam, qg, qu, qd, sg, su, sd, out):
    with ExitStack() as whole:
        sems = {}

        def sem(name):
            if name not in sems:
                sems[name] = whole.enter_context(nc.semaphore(name))
            return sems[name]

        used = {}

        def own(name):
            used[name] = used.get(name, 0) + 1
            return f"{name}_{used[name]}"

        def sb(ctx, name, shape, dt=F32, side="left"):
            return ctx.enter_context(nc.sbuf_tensor(own(name), shape, dt, side=side))

        def sbr(ctx, name, shape, dt=F32):
            return sb(ctx, name, shape, dt, "right")

        def ps(ctx, name, shape, dt=F32):
            return ctx.enter_context(nc.psum_tensor(own(name), shape, dt))

        def phase_end():
            nums = sorted(s.num for s in sems.values())
            nc.all_engine_barrier(sems_to_clear=range(nums[0], nums[-1] + 1))

        for name in ("dma_x0", "dma_x1", "dma_x2", "dma_x3", "dma_w", "dma_w2", "dma_w3", "dma_out", "gp", "dv", "ac", "a1", "a2", "a3", "a4", "p1", "p2", "p3", "p4", "p5",
                     "v1", "v2", "v3", "v4", "v5", "v6", "g1", "g2", "g3", "projected", "q_copied", "w_in0", "w_in1", "w_in2", "w_in3", "w_in4", "w_float", "w_hi", "w_lo", "roped", "q_turned", "q_hi", "q_lo",
                     "scored", "maximum", "exped", "p_turned", "p_hi", "p_lo", "valued", "o_out"):
            sem(name)

        X = sb(whole, "X", [P, NT, D])
        ident = sb(whole, "ident", [P, P])
        identb = sb(whole, "identb", [P, P], BF16)
        maskb = sb(whole, "maskb", [P, P], BF16)
        mhalf = sb(whole, "mhalf", [P, NT * 2])
        stats = sb(whole, "stats", [P, NT, 6])
        mv = sb(whole, "mv", [P, NT, 2])
        rs = sb(whole, "rs", [P, NT])
        nmr = sb(whole, "nmr", [P, NT])

        def pool_rsqrt(pool, ch, dst, src, eps, scale=1.0):
            ch.inc(pool.tensor_scalar(dst, src, scale, eps, ALU.mult, ALU.add))
            ch.wait()
            return pool.tensor_tensor(dst, dst, mhalf[:, 0:dst.shape[1]], ALU.pow)

        def measure(dve, ch, t, y, varied="v2"):
            ch.inc(dve.bn_stats(stats[:, t, :], y))
            ch.wait()
            dve.bn_aggr(mv[:, t, :], stats[:, t, :]).then_inc(sem(varied), 1)

        def add_normed(dve, ch, t, y, tmp, read="v5"):
            dve.wait_ge(sem("g1"), t + 1)
            ch.inc(dve.scalar_tensor_tensor(out=nmr[:, t:t + 1], in0=mv[:, t, 0:1], scalar=-1.0, in1=rs[:, t:t + 1],
                                            op0=ALU.mult, op1=ALU.mult))
            ch.wait()
            dve.tensor_scalar(tmp, y, rs[:, t:t + 1], nmr[:, t:t + 1], ALU.mult, ALU.add).then_inc(sem(read), 1)
            dve.wait_ge(sem(read), t + 1)
            dve.tensor_tensor(X[:, t, :], X[:, t, :], tmp, ALU.add).then_inc(sem("v6"), 1)

        def slot_of(raw, piece, n):
            return raw[:, n % SLOTS, 0:piece[0].shape[1]]

        def pieces_of(arrays, n):
            flat = [[a.rearrange("p k n -> p (k n)") for a in array] for array in arrays]
            cut = lambda a, i: a[:, i * (a.shape[1] // n):(i + 1) * (a.shape[1] // n)]
            return [tuple(cut(a, i) for a in array) for array in flat for i in range(n)]

        def load_pieces(sp, raw, pieces):
            for n, piece in enumerate(pieces):
                if n >= SLOTS:
                    sp.wait_ge(sem("w_lo"), n - SLOTS + 1)
                sp.dma_start(slot_of(raw, piece, n), piece[0]).then_inc(sem(f"w_in{n % SLOTS}"), 16)

        def piece_hi(act, raw, pieces, n):
            act.wait_ge(sem(f"w_in{n % SLOTS}"), 16 * (n // SLOTS + 1))
            act.activation(pieces[n][1], slot_of(raw, pieces[n], n), ACT.Copy).then_inc(sem("w_hi"), 1)

        def piece_lo(dve, raw, pieces, n):
            dve.wait_ge(sem("w_hi"), n + 1)
            dve.tensor_tensor(pieces[n][2], slot_of(raw, pieces[n], n), f(pieces[n][1]), ALU.subtract).then_inc(sem("w_lo"), 1)

        weights = whole.enter_context(ExitStack())
        with ExitStack() as att:
            Wvo_hi = sb(att, "Wvo_hi", [P, H // 2, D], F32R)
            Wvo_lo = sb(att, "Wvo_lo", [P, H // 2, D], F32R)
            heads_in = att.enter_context(ExitStack())
            kT_hi = sbr(heads_in, "kT_hi", [P, T], F32R)
            kT_lo = sbr(heads_in, "kT_lo", [P, T], F32R)
            c_hi = sbr(heads_in, "c_hi", [P, NT, 66], F16)
            c_lo = sbr(heads_in, "c_lo", [P, NT, 66], F16)
            cqT0 = sbr(heads_in, "cqT0", [P, T])
            cqT1 = sbr(heads_in, "cqT1", [QL - P, T])
            Wq0 = sbr(heads_in, "Wq0", [P, (H + 1) * DQ])
            Wq1 = sbr(heads_in, "Wq1", [QL - P, (H + 1) * DQ])
            cs = sbr(heads_in, "cs", [P, NT, DR])
            sn = sbr(heads_in, "sn", [P, NT, DR])
            with ExitStack() as pre:
                wl = sbr(pre, "wl", [P, KD, LAT])
                wqn = sbr(pre, "wqn", [P, H, QL])
                wqp0 = sbr(pre, "wqp0", [P, H, DR])
                wqp1 = sbr(pre, "wqp1", [QL - P, H, DR])
                wk = sbr(pre, "wk", [P, H, KVL])
                wv = sbr(pre, "wv", [P, H, KVL])
                wo = sbr(pre, "wo", [P, H, D])
                qln0 = sbr(pre, "qln0", [P, 1])
                qln1 = sbr(pre, "qln1", [QL - P, 1])
                kln = sbr(pre, "kln", [P, KVL])
                xn = sbr(pre, "xn", [P, 3, D])
                xnT = sbr(pre, "xnT", [P, 3, KD, P])
                kpe = sbr(pre, "kpe", [P, 3, 2, DR])
                latn = sbr(pre, "latn", [P, 3, LAT])
                junk = sbr(pre, "junk", [P, 2, QL])
                ss = sbr(pre, "ss", [P, NT, 2])
                rr = sbr(pre, "rr", [P, NT, 2])
                rt = sbr(pre, "rt", [P, 3, DR])
                pt = [ps(pre, f"pt{b}", [P, 512]) for b in range(2)]
                pl = [ps(pre, f"pl{b}", [P, 512]) for b in range(3)]
                pk = [ps(pre, f"pk{b}", [P, 512]) for b in range(3)]
                with nc.Block() as block:

                    @block.sync
                    def _(sp):
                        for g in range(4):
                            sp.dma_start(X[:, 4 * g:4 * g + 4, :], x[:, 4 * g:4 * g + 4, :]).then_inc(sem(f"dma_x{g}"), 16)
                        sp.dma_start(wl[:], w_lat).then_inc(sem("dma_w"), 16)
                        sp.dma_start(cs[:], cos2).then_inc(sem("dma_w2"), 16)
                        sp.dma_start(sn[:], sin2).then_inc(sem("dma_w2"), 16)

                    @block.scalar
                    def _(act):
                        w3 = sem("dma_w3")
                        act.dma_start(kln[:], kv_ln.partition_broadcast(P)).then_inc(w3, 16)
                        act.dma_start(qln0[:], q_ln[0:P, :]).then_inc(w3, 16)
                        act.dma_start(qln1[:], q_ln[P:QL, :]).then_inc(w3, 16)
                        act.dma_start(wk[:], w_kn).then_inc(w3, 16)
                        act.dma_start(wqn[:], w_qn).then_inc(w3, 16)
                        act.dma_start(wqp0[:], w_qpe[0:P]).then_inc(w3, 16)
                        act.dma_start(wqp1[:], w_qpe[P:QL]).then_inc(w3, 16)
                        act.dma_start(wv[:], w_v).then_inc(w3, 16)
                        act.dma_start(wo[:], w_o).then_inc(w3, 16)
                        for t in range(NT + 3):
                            if t < NT:
                                act.wait_ge(sem("p1"), t + 1)
                                if t >= 3:
                                    act.wait_ge(sem("p2"), t - 2)
                                act.activation(xnT[:, t % 3], pt[t % 2][:, 0:D].rearrange("p (k n) -> p k n", k=KD), ACT.Copy).then_inc(sem("a1"), 1)
                            if 1 <= t < NT + 1:
                                u = t - 1
                                act.wait_ge(sem("p2"), u + 1)
                                if u:
                                    act.wait_ge(sem("a2"), 2 * u)
                                act.activation(junk[:, 0], pl[u % 3][:, 0:QL], ACT.Square, accum_out=ss[:, u, 0:1]).then_inc(sem("a2"), 1)
                                act.activation(junk[:, 1, 0:KVL], pl[u % 3][:, QL:QL + KVL], ACT.Square,
                                               accum_out=ss[:, u, 1:2]).then_inc(sem("a2"), 1)
                            if t >= 3:
                                u = t - 3
                                sl = slice(u * P, (u + 1) * P)
                                act.wait_ge(sem("p3"), u + 1)
                                act.activation(kT_hi[:, sl], pk[u % 3][:, 2 * P:3 * P], ACT.Copy).then_inc(sem("a4"), 1)
                                act.activation(cqT0[:, sl], pk[u % 3][:, 0:P], ACT.Copy).then_inc(sem("a4"), 1)
                                act.activation(cqT1[:, sl], pk[u % 3][0:64, P:2 * P], ACT.Copy).then_inc(sem("a4"), 1)
                        for j in range(H // 2):
                            act.wait_ge(sem("p5"), j + 1)
                            act.activation(Wvo_hi[0:64, j], pk[j % 3][0:64, 0:D], ACT.Copy).then_inc(sem("a3"), 1)
                            act.activation(Wvo_hi[64:128, j], pk[j % 3][64:128, D:2 * D], ACT.Copy).then_inc(sem("a3"), 1)

                    @block.gpsimd
                    def _(pool):
                        ch = Chain(pool, sem("gp"))
                        pool.memset(mhalf[:], -0.5)
                        pool.memset(ident[:], 0.0)
                        ch.inc(pool.memset(identb[:], 0.0))
                        ch.inc(pool.memset(maskb[:], 0.0))
                        pool.memset(Wq0[:, H * DQ:], 0.0)
                        pool.memset(Wq1[:, H * DQ:], 0.0)
                        pool.memset(c_hi[:, :, 64:65], 1.0)
                        pool.memset(c_hi[:, :, 65:66], 0.0)
                        ch.inc(pool.memset(c_lo[:, :, 64:66], 0.0))
                        ch.wait()
                        ch.inc(pool.affine_select(out=ident[:], in_=ident[:], compare_op=ALU.not_equal, fill=1.0, base=0,
                                                  pattern=[[-1, P]], channel_multiplier=1))
                        ch.inc(pool.affine_select(out=identb[:], in_=identb[:], compare_op=ALU.not_equal, fill=1.0, base=0,
                                                  pattern=[[-1, P]], channel_multiplier=1))
                        ch.inc(pool.affine_select(out=maskb[:], in_=maskb[:], compare_op=ALU.is_ge, fill=MASKED, base=0,
                                                  pattern=[[-1, P]], channel_multiplier=1))
                        ch.wait()
                        pool.memset(rt[:], 0.0).then_inc(sem("g3"), 1)

                        def deviation(t):
                            pool.wait_ge(sem("v1"), t + 1)
                            pool_rsqrt(pool, ch, rs[:, t:t + 1], mv[:, t, 1:2], LN_EPS).then_inc(sem("g1"), 1)

                        deviation(0)
                        deviation(1)
                        for t in range(NT):
                            if t + 2 < NT:
                                deviation(t + 2)
                            pool.wait_ge(sem("a2"), 2 * t + 2)
                            ch.inc(pool.tensor_scalar(rr[:, t, 0:1], ss[:, t, 0:1], 1.0 / QL, RMS_EPS, ALU.mult, ALU.add))
                            ch.inc(pool.tensor_scalar(rr[:, t, 1:2], ss[:, t, 1:2], 1.0 / KVL, RMS_EPS, ALU.mult, ALU.add))
                            ch.wait()
                            pool.tensor_tensor(rr[:, t, :], rr[:, t, :], mhalf[:, 0:2], ALU.pow).then_inc(sem("g2"), 1)
                            if t in (9, 11):
                                w = wv if t == 9 else wk
                                pool.wait_ge(sem("dma_w3"), 16 * 9)
                                pool.tensor_tensor(w[:], w[:], kln[:].unsqueeze(1).to_broadcast([P, H, KVL]), ALU.mult).then_inc(sem("v5"), 1)

                    @block.vector
                    def _(dve):
                        ch = Chain(dve, sem("dv"))

                        def variance(t):
                            if t % 4 == 0:
                                dve.wait_ge(sem(f"dma_x{t // 4}"), 16)
                            ch.inc(dve.bn_stats(stats[:, t, :], X[:, t, :]))
                            ch.wait()
                            dve.bn_aggr(mv[:, t, :], stats[:, t, :]).then_inc(sem("v1"), 1)

                        def normed(t):
                            dve.wait_ge(sem("g1"), t + 1)
                            if t >= 3:
                                dve.wait_ge(sem("p1"), t - 2)
                            dve.tensor_scalar(xn[:, t % 3, :], X[:, t, :], mv[:, t, 0:1], rs[:, t:t + 1],
                                              ALU.subtract, ALU.mult).then_inc(sem("v2"), 1)

                        def rope(t):
                            if t == 0:
                                dve.wait_ge(sem("dma_w2"), 32)
                                dve.wait_ge(sem("g3"), 1)
                            dve.wait_ge(sem("p2"), t + 1)
                            dve.wait_ge(sem("a2"), 2 * t + 2)
                            kp, r = kpe[:, t % 3], rt[:, t % 3]
                            ch.inc(dve.tensor_copy(kp[:, 0], pl[t % 3][:, QL + KVL:LAT]))
                            ch.wait()
                            dve.tensor_tensor(r[:, 0:32], kp[:, 0, 32:64], sn[:, t, 0:32], ALU.mult).then_inc(sem("dv"), 1)
                            dve.tensor_tensor(r[:, 32:64], kp[:, 0, 0:32], sn[:, t, 32:64], ALU.mult).then_inc(sem("dv"), 1)
                            dve.tensor_tensor(kp[:, 1], kp[:, 0], cs[:, t, :], ALU.mult).then_inc(sem("dv"), 1)
                            ch.n += 3

                        def latents(t):
                            dve.wait_ge(sem("g2"), t + 1)
                            if t >= 3:
                                dve.wait_ge(sem("p3"), t - 2)
                            ch.wait()
                            L, N = pl[t % 3], latn[:, t % 3]
                            ch.inc(dve.tensor_scalar(N[:, QL:QL + KVL], L[:, QL:QL + KVL], rr[:, t, 1:2], None, ALU.mult))
                            dve.tensor_tensor(N[:, QL + KVL:LAT], kpe[:, t % 3, 1], rt[:, t % 3], ALU.add)
                            dve.tensor_scalar(N[:, 0:QL], L[:, 0:QL], rr[:, t, 0:1], None, ALU.mult).then_inc(sem("v3"), 1)
                            ch.wait()
                            ch.inc(dve.tensor_copy(c_hi[:, t, 0:KVL], N[:, QL:QL + KVL]))
                            ch.wait()
                            ch.inc(dve.tensor_tensor(c_lo[:, t, 0:KVL], N[:, QL:QL + KVL], c_hi[:, t, 0:KVL], ALU.subtract))

                        def low(t):
                            dve.wait_ge(sem("a4"), 3 * t + 3)
                            sl = slice(t * P, (t + 1) * P)
                            dve.tensor_tensor(kT_lo[:, sl], pk[t % 3][:, 2 * P:3 * P], f(kT_hi[:, sl]), ALU.subtract).then_inc(sem("v4"), 1)

                        for t in range(-2, NT + 4):
                            if 0 <= t + 2 < NT:
                                variance(t + 2)
                            if 0 <= t + 1 < NT:
                                normed(t + 1)
                            if 1 <= t < NT + 1:
                                rope(t - 1)
                            if 2 <= t < NT + 2:
                                latents(t - 2)
                            if t >= 4:
                                low(t - 4)
                        dve.wait_ge(sem("dma_w3"), 16 * 9)
                        q0 = Wq0[:, 0:H * DQ].rearrange("p (h d) -> p h d", h=H)
                        q1 = Wq1[:, 0:H * DQ].rearrange("p (h d) -> p h d", h=H)
                        dve.tensor_scalar(q0[:, :, KVL:DQ], wqp0[:], qln0[:], None, ALU.mult)
                        dve.tensor_scalar(q1[:, :, KVL:DQ], wqp1[:], qln1[:], None, ALU.mult)
                        for j in range(H // 2):
                            dve.wait_ge(sem("a3"), 2 * j + 2)
                            dve.tensor_tensor(Wvo_lo[0:64, j], pk[j % 3][0:64, 0:D], f(Wvo_hi[0:64, j]), ALU.subtract)
                            dve.tensor_tensor(Wvo_lo[64:128, j], pk[j % 3][64:128, D:2 * D], f(Wvo_hi[64:128, j]),
                                              ALU.subtract).then_inc(sem("v6"), 1)
                        for g in range(2):
                            dve.wait_ge(sem("p4"), g + 1)
                            h8 = slice(8 * g, 8 * g + 8)
                            dve.tensor_scalar(q0[:, h8, 0:KVL], pt[g][:].rearrange("p (h d) -> p h d", h=8), qln0[:], None, ALU.mult)
                            dve.tensor_scalar(q1[:, h8, 0:KVL], pl[g][0:64, :].rearrange("p (h d) -> p h d", h=8), qln1[:], None, ALU.mult)

                    @block.tensor
                    def _(pe):
                        def transposed(t):
                            if t == 0:
                                pe.wait_ge(sem("g3"), 1)
                            pe.wait_ge(sem("v2"), t + 1)
                            if t >= 2:
                                pe.wait_ge(sem("a1"), t - 1)
                            for k in range(KD):
                                m = pe.transpose(pt[t % 2][:, k * P:(k + 1) * P], xn[:, t % 3, k * P:(k + 1) * P], ident[:])
                            m.then_inc(sem("p1"), 1)

                        def latents(t):
                            pe.wait_ge(sem("a1"), t + 1)
                            if t >= 3:
                                pe.wait_ge(sem("v3"), t - 2)
                            for k in range(KD):
                                m = pe.matmul(pl[t % 3][:, 0:LAT], xnT[:, t % 3, k, :], wl[:, k, :], start=(k == 0), stop=(k == KD - 1))
                            m.then_inc(sem("p2"), 1)

                        def turned(t):
                            pe.wait_ge(sem("v3"), t + 1)
                            if t >= 3:
                                pe.wait_ge(sem("v4"), t - 2)
                            N, o = latn[:, t % 3], pk[t % 3]
                            pe.transpose(o[:, 0:P], N[:, 0:P], ident[:])
                            pe.transpose(o[0:64, P:2 * P], N[:, P:QL], ident[:])
                            pe.transpose(o[:, 2 * P:3 * P], N[:, QL:LAT], ident[:]).then_inc(sem("p3"), 1)

                        for t in range(NT + 3):
                            if t < NT:
                                transposed(t)
                            if t == 1:
                                pe.wait_ge(sem("dma_w"), 16)
                            if 1 <= t < NT + 1:
                                latents(t - 1)
                            if t >= 3:
                                turned(t - 3)
                        pe.wait_ge(sem("v5"), 2)
                        pe.wait_ge(sem("v4"), NT)
                        for j in range(H // 2):
                            if j >= 3:
                                pe.wait_ge(sem("v6"), j - 2)
                            pair = wv[:, 2 * j:2 * j + 2, :]
                            pe.matmul(pk[j % 3][:, 0:D], pair, wo[:, 2 * j, :], start=True, stop=True)
                            pe.matmul(pk[j % 3][:, D:2 * D], pair, wo[:, 2 * j + 1, :], start=True, stop=True).then_inc(sem("p5"), 1)
                        for g in range(2):
                            for j in range(8):
                                h = 8 * g + j
                                pe.matmul(pt[g][:, j * 64:(j + 1) * 64], wqn[:, h, 0:P], wk[:, h, :], start=True, stop=True)
                                m = pe.matmul(pl[g][0:64, j * 64:(j + 1) * 64], wqn[:, h, P:QL], wk[:, h, :], start=True, stop=True)
                            m.then_inc(sem("p4"), 1)

                phase_end()

            O = sb(att, "O", [P, NT, H * KVL])
            with ExitStack() as loop:
                qs = sbr(loop, "qs", [P, 4, DQ])
                qt = sbr(loop, "qt", [P, 2, DR])
                qT_hi = sbr(loop, "qT_hi", [P, 2, P], F32R)
                qT_lo = sbr(loop, "qT_lo", [P, 2, P], F32R)
                pr = sbr(loop, "pr", [P, 3, T])
                pT_hi = sbr(loop, "pT_hi", [P, 4, BT], F16)
                pT_lo = sbr(loop, "pT_lo", [P, 4, BT], F16)
                cmx = sbr(loop, "cmx", [P, 2, 4])
                nmx = sbr(loop, "nmx", [P, 4])
                rl = sbr(loop, "rl", [P, 2])
                pS = [ps(loop, f"pS{b}", [P, BT]) for b in range(4)]
                pT = [ps(loop, f"pT{b}", [P, BT]) for b in range(2)]
                pO = ps(loop, "pO", [P, BT])
                pQ = ps(loop, "pQ", [P, BT])
                NP = HG * NT
                order = [t for k in range(NT // 2) for t in (NT - 1 - k, k)]
                tile_at = lambda p: order[p % NT]
                chunk = [(p, c, min(4, tile_at(p) + 1 - 4 * c)) for p in range(NP + 1) for c in range(tile_at(p) // 4 + 1)]
                first = [next(n for n, k in enumerate(chunk) if k[0] == p) for p in range(NP + 1)] + [len(chunk)]
                n_chunks = first[NP]
                LEAD = first[1]
                LAG = 2
                QLEAD = 3
                plan = []
                behind = 0
                for p in range(1, NP + 1):
                    n = first[p + 1] - first[p]
                    placed = False
                    for k in range(n):
                        plan.append(("scores", first[p] + k))
                        last = k == n - 1
                        if k == 0:
                            plan.append(("turn", p + 1))
                        for _ in range(min(n, 2) if last else int(k < n - 2)):
                            plan.append(("probs", behind))
                            if behind >= LAG:
                                plan.append(("values", behind - LAG))
                            behind += 1
                            if last and not placed:
                                placed = True
                                plan.append(("project", p + QLEAD))
                assert behind == n_chunks
                plan += [("values", n_chunks - LAG + k) for k in range(LAG)]

                def heads(block, g, lead):
                    begun = {} if lead else {"projected": 1 + QLEAD, "q_copied": 1 + QLEAD, "roped": 1 + QLEAD, "q_turned": 2,
                                             "q_hi": 2, "q_lo": 2, "scored": LEAD, "maximum": 1}

                    def done(eng, name, item):
                        n = item + 1 - begun.get(name, 0)
                        if n > 0:
                            eng.wait_ge(sem(name), n)

                    @block.tensor
                    def _(pe):
                        def project(p):
                            turned = min(p - 1, max(1, p - QLEAD + 1))
                            if turned >= 0:
                                done(pe, "q_hi", turned)
                                done(pe, "q_lo", turned)
                            if p >= 1:
                                done(pe, "q_copied", p - 1)
                            t = tile_at(p)
                            sl = slice(t * P, (t + 1) * P)
                            ws = slice(0, DQ) if lead else bass.ds((g * HG + p // NT) * DQ, DQ)
                            pe.matmul(pQ[:, 0:DQ], cqT0[:, sl], Wq0[:, ws], start=True, stop=False)
                            pe.matmul(pQ[:, 0:DQ], cqT1[:, sl], Wq1[:, ws], start=False, stop=True).then_inc(sem("projected"), 1)

                        def turn(p):
                            done(pe, "roped", p)
                            if p >= 2:
                                done(pe, "q_copied", p + QLEAD - 2)
                            pe.transpose(pQ[:, P:2 * P], qs[:, p % 4, :], ident[:]).then_inc(sem("q_turned"), 1)

                        def scores(at):
                            p, c, n = chunk[at]
                            if c == 0:
                                done(pe, "q_hi", p)
                                done(pe, "q_lo", p)
                            if at >= 4:
                                done(pe, "exped", at - 4)
                            w = max(256, n * P)
                            o, ks = pS[at % 4][:, 0:w], slice(c * BT, c * BT + w)
                            pe.matmul(o, qT_hi[:, p % 2], kT_hi[:, ks], start=True, stop=False)
                            pe.matmul(o, qT_hi[:, p % 2], kT_lo[:, ks], start=False, stop=False)
                            if c == tile_at(p) // 4:
                                pe.matmul(pS[at % 4][:, (n - 1) * P:n * P], identb[:], maskb[:], start=False, stop=False,
                                          skip_group_check=True)
                            pe.matmul(o, qT_lo[:, p % 2], kT_hi[:, ks], start=False, stop=True).then_inc(sem("scored"), 1)

                        def probs(at):
                            p, c, n = chunk[at]
                            done(pe, "exped", at)
                            if at >= 2:
                                done(pe, "p_hi", at - 2)
                                done(pe, "p_lo", at - 2)
                            for k in range(n):
                                m = pe.transpose(pT[at % 2][:, k * P:(k + 1) * P],
                                                 pr[:, p % 3, (4 * c + k) * P:(4 * c + k + 1) * P], ident[:])
                            m.then_inc(sem("p_turned"), 1)

                        def values(at):
                            p, c, n = chunk[at]
                            done(pe, "p_hi", at)
                            done(pe, "p_lo", at)
                            if c == 0 and p >= 1:
                                done(pe, "o_out", p - 1)
                            o = pO[:, 0:KVL + 1]
                            for k in range(n):
                                ks = slice(k * P, (k + 1) * P)
                                j = 4 * c + k
                                hi, lo = pT_hi[:, at % 4, ks], pT_lo[:, at % 4, ks]
                                pe.matmul(o, hi, c_hi[:, j, 0:KVL + 1], start=(j == 0), stop=False)
                                pe.matmul(o, hi, c_lo[:, j, 0:KVL + 1], start=False, stop=False)
                                m = pe.matmul(o, lo, c_hi[:, j, 0:KVL + 1], start=False, stop=(j == tile_at(p)))
                            m.then_inc(sem("valued"), 1)

                        if lead:
                            project(0)
                            turn(0)
                            project(1)
                            turn(1)
                            project(2)
                            project(3)
                            for at in range(LEAD):
                                scores(at)
                            return
                        for step, at in plan:
                            {"project": project, "turn": turn, "scores": scores, "probs": probs, "values": values}[step](at)

                    @block.scalar
                    def _(act):
                        def q_out(p):
                            done(act, "projected", p)
                            if p >= 4:
                                done(act, "q_turned", p - 4)
                            act.activation(qs[:, p % 4], pQ[:, 0:DQ], ACT.Copy, scale=SCALE).then_inc(sem("q_copied"), 1)

                        def q_hi(p):
                            done(act, "q_turned", p)
                            act.activation(qT_hi[:, p % 2], pQ[:, P:2 * P], ACT.Copy).then_inc(sem("q_hi"), 1)

                        def exp(at):
                            p, c, n = chunk[at]
                            if c == 0:
                                done(act, "maximum", p)
                                if p >= 3:
                                    done(act, "p_turned", first[p - 2] - 1)
                            act.activation(pr[:, p % 3, c * BT:c * BT + n * P], pS[at % 4][:, 0:n * P], ACT.Exp,
                                           bias=nmx[:, p % 4:p % 4 + 1]).then_inc(sem("exped"), 1)

                        def p_hi(at):
                            n = chunk[at][2]
                            done(act, "p_turned", at)
                            if at >= 4:
                                done(act, "valued", at - 4)
                            act.activation(pT_hi[:, at % 4, 0:n * P], pT[at % 2][:, 0:n * P], ACT.Copy).then_inc(sem("p_hi"), 1)

                        if lead:
                            q_out(0)
                            q_hi(0)
                            q_out(1)
                            q_hi(1)
                            q_out(2)
                            q_out(3)
                            return
                        exped = 0
                        scored = LEAD
                        for step, at in plan:
                            if step == "scores":
                                while exped <= at - 4:
                                    exp(exped)
                                    exped += 1
                                if at + 1 in first and at + 1 > scored:
                                    scored = at + 1
                            elif step == "turn":
                                q_hi(at)
                            elif step == "probs":
                                while exped <= at:
                                    exp(exped)
                                    exped += 1
                                p_hi(at)
                                if exped < min(scored, n_chunks):
                                    exp(exped)
                                    exped += 1
                            elif step == "project":
                                q_out(at)

                    @block.gpsimd
                    def _(pool):
                        ch = Chain(pool, sem("gp"))
                        for p in range(0, 1 + QLEAD) if lead else range(1 + QLEAD, NP + 1 + QLEAD):
                            done(pool, "q_copied", p)
                            q, r, t = qs[:, p % 4, KVL:DQ], qt[:, p % 2], tile_at(p)
                            ch.inc(pool.tensor_tensor(r[:, 0:32], q[:, 32:64], sn[:, t, 0:32], ALU.mult))
                            ch.inc(pool.tensor_tensor(r[:, 32:64], q[:, 0:32], sn[:, t, 32:64], ALU.mult))
                            ch.wait()
                            ch.inc(pool.tensor_tensor(q, q, cs[:, t, :], ALU.mult))
                            ch.wait()
                            pool.tensor_tensor(q, q, r, ALU.add).then_inc(sem("roped"), 1)

                    @block.vector
                    def _(dve):
                        ch = Chain(dve, sem("dv"))

                        def q_lo(p):
                            done(dve, "q_hi", p)
                            dve.tensor_tensor(qT_lo[:, p % 2], pQ[:, P:2 * P], f(qT_hi[:, p % 2]), ALU.subtract).then_inc(sem("q_lo"), 1)

                        def maximum(at):
                            p, c, n = chunk[at]
                            n_c = tile_at(p) // 4 + 1
                            if c == 0 and p >= 4:
                                done(dve, "exped", first[p - 3] - 1)
                            done(dve, "scored", at)
                            whole_ = nmx[:, p % 4:p % 4 + 1]
                            if n_c == 1:
                                dve.tensor_reduce(whole_, pS[at % 4][:, 0:n * P], AX.X, ALU.max, negate=True).then_inc(sem("maximum"), 1)
                                return
                            ch.inc(dve.tensor_reduce(cmx[:, p % 2, c:c + 1], pS[at % 4][:, 0:n * P], AX.X, ALU.max))
                            if c == n_c - 1:
                                ch.wait()
                                dve.tensor_reduce(whole_, cmx[:, p % 2, 0:n_c], AX.X, ALU.max, negate=True).then_inc(sem("maximum"), 1)

                        def p_lo(at):
                            n = chunk[at][2]
                            done(dve, "p_hi", at)
                            dve.tensor_tensor(pT_lo[:, at % 4, 0:n * P], pT[at % 2][:, 0:n * P], pT_hi[:, at % 4, 0:n * P],
                                              ALU.subtract).then_inc(sem("p_lo"), 1)

                        def o_out(p):
                            done(dve, "valued", first[p + 1] - 1)
                            ch.inc(dve.reciprocal(rl[:, p % 2:p % 2 + 1], pO[:, KVL:KVL + 1]))
                            ch.wait()
                            dve.tensor_scalar(O[:, tile_at(p), bass.ds((g * HG + p // NT) * KVL, KVL)], pO[:, 0:KVL], rl[:, p % 2:p % 2 + 1], None,
                                              ALU.mult).then_inc(sem("o_out"), 1)

                        if lead:
                            q_lo(0)
                            q_lo(1)
                            for at in range(LEAD):
                                maximum(at)
                            return
                        turned = None
                        for step, at in plan:
                            if step != "values" and turned is not None:
                                p_lo(turned)
                                turned = None
                            if step == "scores":
                                maximum(at)
                            elif step == "turn":
                                q_lo(at)
                            elif step == "probs":
                                turned = at
                            elif step == "values" and at + 1 in first:
                                o_out(chunk[at][0])
                            if step == "values" and turned is not None:
                                p_lo(turned)
                                turned = None

                with nc.Block() as block:
                    heads(block, 0, True)
                phase_end()
                with nc.Fori(0, H // HG) as g:
                    with nc.Block() as block:
                        heads(block, g, False)
                    phase_end()

            heads_in.close()

            wg_ = [sbr(weights, f"wg_{k}", [P, KD, FM], F32R) for k in range(2)]
            wu_ = [sbr(weights, f"wu_{k}", [P, KD, FM], F32R) for k in range(2)]
            wd_ = [sbr(weights, f"wd_{k}", [P, NFM, D], F32R) for k in range(2)]
            expert_pieces = pieces_of(((src, w[0][:], w[1][:]) for src, w in ((wg, wg_), (wu, wu_), (wd, wd_))), 8)
            pieces_at = lambda t: range(len(expert_pieces) * t // NT, len(expert_pieces) * (t + 1) // NT)

            with ExitStack() as op:
                OT_hi = sb(op, "OT_hi", [P, 2, 8, P], F32R)
                OT_lo = sb(op, "OT_lo", [P, 2, 8, P], F32R)
                tmp = sb(op, "tmp", [P, 2, D])
                raw = sb(op, "raw", [P, SLOTS, max(p_[0].shape[1] for p_ in expert_pieces)])
                pt = [[ps(op, f"po{b}{k}", [P, 512]) for k in range(2)] for b in range(2)]
                py = [ps(op, f"py{b}", [P, 512]) for b in range(2)]
                with nc.Block() as block:

                    @block.sync
                    def _(sp):
                        load_pieces(sp, raw, expert_pieces)

                    @block.tensor
                    def _(pe):
                        def turn(t):
                            for k in range(2):
                                if t >= 2:
                                    pe.wait_ge(sem("v1"), 2 * (t - 2) + k + 1)
                                for j in range(4):
                                    m = pe.transpose(pt[t % 2][k][:, j * P:(j + 1) * P], O[:, t, (4 * k + j) * P:(4 * k + j + 1) * P], ident[:])
                                m.then_inc(sem("p1"), 1)

                        turn(0)
                        for t in range(NT):
                            if t + 1 < NT:
                                turn(t + 1)
                            pe.wait_ge(sem("v1"), 2 * t + 2)
                            if t >= 2:
                                pe.wait_ge(sem("v5"), t - 1)
                            y = py[t % 2][:, 0:D]
                            n = 0
                            for j in range(8):
                                for a, w in ((OT_hi, Wvo_hi), (OT_hi, Wvo_lo), (OT_lo, Wvo_hi)):
                                    m = pe.matmul(y, a[:, t % 2, j], w[:, j], start=(n == 0), stop=(n == 23))
                                    n += 1
                            m.then_inc(sem("p2"), 1)

                    @block.scalar
                    def _(act):
                        for t in range(NT):
                            for k in range(2):
                                act.wait_ge(sem("p1"), 2 * t + k + 1)
                                if t >= 2:
                                    act.wait_ge(sem("p2"), t - 1)
                                act.activation(OT_hi[:, t % 2, 4 * k:4 * k + 4], pt[t % 2][k][:].rearrange("p (j n) -> p j n", j=4),
                                               ACT.Copy).then_inc(sem("a1"), 1)
                            for n in pieces_at(t):
                                piece_hi(act, raw, expert_pieces, n)

                    @block.gpsimd
                    def _(pool):
                        ch = Chain(pool, sem("gp"))
                        for t in range(NT):
                            pool.wait_ge(sem("v2"), t + 1)
                            pool_rsqrt(pool, ch, rs[:, t:t + 1], mv[:, t, 1:2], LN_EPS).then_inc(sem("g1"), 1)

                    @block.vector
                    def _(dve):
                        ch = Chain(dve, sem("dv"))

                        def split(t):
                            for k in range(2):
                                dve.wait_ge(sem("a1"), 2 * t + k + 1)
                                dve.tensor_tensor(OT_lo[:, t % 2, 4 * k:4 * k + 4], pt[t % 2][k][:].rearrange("p (j n) -> p j n", j=4),
                                                  f(OT_hi[:, t % 2, 4 * k:4 * k + 4]), ALU.subtract).then_inc(sem("v1"), 1)

                        split(0)
                        for t in range(NT):
                            if t + 1 < NT:
                                split(t + 1)
                            dve.wait_ge(sem("p2"), t + 1)
                            measure(dve, ch, t, py[t % 2][:, 0:D])
                            for n in pieces_at(t - 1) if t else ():
                                piece_lo(dve, raw, expert_pieces, n)
                            add_normed(dve, ch, t, py[t % 2][:, 0:D], tmp[:, t % 2])
                        for n in pieces_at(NT - 1):
                            piece_lo(dve, raw, expert_pieces, n)

                phase_end()

        def turned_norm(xT_hi, xT_lo):
            with ExitStack() as c:
                xn = sb(c, "xn", [P, 4, D])
                pt = [ps(c, f"pt{b}", [P, 2, KD, P]) for b in range(NT // 2)]
                pair = lambda xT_, g: xT_[:, :, 2 * g * P:2 * (g + 1) * P].rearrange("p k (t n) -> p k t n", t=2)
                with nc.Block() as block:

                    @block.vector
                    def _(dve):
                        ch = Chain(dve, sem("dv"))
                        for t in range(NT):
                            ch.inc(dve.bn_stats(stats[:, t, :], X[:, t, :]))
                            if t:
                                dve.bn_aggr(mv[:, t - 1, :], stats[:, t - 1, :]).then_inc(sem("v1"), 1)
                            ch.wait()
                        dve.bn_aggr(mv[:, NT - 1, :], stats[:, NT - 1, :]).then_inc(sem("v1"), 1)
                        for g in range(NT // 2):
                            dve.wait_ge(sem("a1"), g + 1)
                            dve.tensor_tensor(pair(xT_lo, g), pt[g][:].rearrange("p t k n -> p k t n"), pair(f(xT_hi[:]), g), ALU.subtract)

                    @block.gpsimd
                    def _(pool):
                        ch = Chain(pool, sem("gp"))
                        for g in range(NT // 2):
                            ts = slice(2 * g, 2 * g + 2)
                            pool.wait_ge(sem("v1"), 2 * g + 2)
                            ch.inc(pool_rsqrt(pool, ch, rs[:, ts], mv[:, ts, 1], LN_EPS))
                            ch.wait()
                            ch.inc(pool.tensor_tensor(nmr[:, ts], mv[:, ts, 0], rs[:, ts], ALU.mult))
                            ch.wait()
                            pool.tensor_scalar(nmr[:, ts], nmr[:, ts], -1.0, None, ALU.mult).then_inc(sem("g1"), 1)

                    @block.tensor
                    def _(pe):
                        for t in range(NT):
                            pe.wait_ge(sem("a2"), t + 1)
                            for k in range(KD):
                                m = pe.transpose(pt[t // 2][:, t % 2, k], xn[:, t % 4, k * P:(k + 1) * P], ident[:])
                            m.then_inc(sem("p1"), 1)

                    @block.scalar
                    def _(act):
                        def normed(t):
                            act.wait_ge(sem("g1"), t // 2 + 1)
                            if t >= 4:
                                act.wait_ge(sem("p1"), t - 3)
                            act.activation(xn[:, t % 4, :], X[:, t, :], ACT.Identity, bias=nmr[:, t:t + 1],
                                           scale=rs[:, t:t + 1]).then_inc(sem("a2"), 1)

                        normed(0)
                        normed(1)
                        for g in range(NT // 2):
                            if g + 1 < NT // 2:
                                normed(2 * g + 2)
                                normed(2 * g + 3)
                            act.wait_ge(sem("p1"), 2 * g + 2)
                            act.activation(pair(xT_hi, g), pt[g][:].rearrange("p t k n -> p k t n"), ACT.Copy).then_inc(sem("a1"), 1)
                phase_end()

        def gated_ffn(xT, wg_, wu_, wd_, n_m, rows, n_routed=0, selb=None, wT=None, g_scale=None, u_scale=None, store=False,
                      pieces=()):
            with ExitStack() as c:
                sgb = sb(c, "sgb", [P, 2, BT])
                hb = sb(c, "hb", [P, 2, BT])
                h_hi = sb(c, "h_hi", [P, 3, BT], F32R)
                h_lo = sb(c, "h_lo", [P, 3, BT], F32R)
                y = sb(c, "y", [P, TPB, D])
                raw = sb(c, "raw", [P, SLOTS, BT]) if pieces else None
                tmp = sb(c, "tmp", [P, 2, D])
                pG = [ps(c, f"pG{b}", [P, BT]) for b in range(2)]
                pU = [ps(c, f"pU{b}", [P, BT]) for b in range(2)]
                pW = [ps(c, f"pW{b}", [P, BT]) for b in range(2)]
                pY = [ps(c, f"pY{b}", [P, 2, D]) for b in range(2)]
                N = NB * n_m

                def routed(n):
                    return n % n_m < n_routed

                def n_scaled(n):
                    return (n // n_m) * n_routed + min(n % n_m + 1, n_routed)

                with nc.Block() as block:

                    @block.tensor
                    def _(pe):
                        def up(n):
                            tb, m = divmod(n, n_m)
                            b, r, ts = n % 2, rows[m], slice(tb * BT, (tb + 1) * BT)
                            fs = slice(m * P, m * P + r)
                            if n >= 2:
                                pe.wait_ge(sem("a1"), n - 1)
                                pe.wait_ge(sem("v1"), n - 1)
                            for out_, w in ((pG[b], wg_), (pU[b], wu_)):
                                q = 0
                                for k in range(KD):
                                    for i, j in ((0, 0), (0, 1), (1, 0)):
                                        mm = pe.matmul(out_[0:r, :], w[i][:, k, fs], xT[j][:, k, ts], start=(q == 0), stop=(q == 5))
                                        q += 1
                            if routed(n):
                                if n_scaled(n) > 2:
                                    pe.wait_ge(sem("v2"), n_scaled(n) - 2)
                                mm = pe.matmul(pW[(n_scaled(n) - 1) % 2][0:r, :], selb[:, fs], wT[:, ts], start=True, stop=True)
                            mm.then_inc(sem("p1"), 1)

                        def down(n):
                            tb, m = divmod(n, n_m)
                            b, r = n % 2, rows[m]
                            pe.wait_ge(sem("a2"), n + 1)
                            pe.wait_ge(sem("v3"), n + 1)
                            if m == 0 and tb:
                                pe.wait_ge(sem("a3"), 2 * tb)
                            for q in range(TPB):
                                qs_ = slice(q * P, (q + 1) * P)
                                for j, (a, w) in enumerate(((h_hi, wd_[0]), (h_hi, wd_[1]), (h_lo, wd_[0]))):
                                    mm = pe.matmul(pY[q // 2][:, q % 2, :], a[0:r, n % 3, qs_], w[0:r, m, :],
                                                   start=(m == 0 and q % 2 == 0 and j == 0), stop=(m == n_m - 1 and j == 2),
                                                   skip_group_check=True)
                            mm.then_inc(sem("p2"), 1)

                        up(0)
                        up(1)
                        for n in range(N):
                            if n + 2 < N:
                                up(n + 2)
                            down(n)

                    @block.scalar
                    def _(act):
                        def silu(n):
                            b, m = n % 2, n % n_m
                            r = rows[m]
                            act.wait_ge(sem("p1"), n + 1)
                            if n >= 2:
                                act.wait_ge(sem("v1"), n - 1)
                            kw = {"scale": g_scale[0:r, m:m + 1]} if g_scale is not None else {}
                            act.activation(sgb[0:r, b], pG[b][0:r, :], ACT.Silu, **kw).then_inc(sem("a1"), 1)

                        silu(0)
                        for n in range(N):
                            tb, m = divmod(n, n_m)
                            b, r = n % 2, rows[m]
                            if routed(n):
                                act.wait_ge(sem("v2"), n_scaled(n))
                            else:
                                act.wait_ge(sem("v1"), n + 1)
                            if n >= 3:
                                act.wait_ge(sem("p2"), n - 2)
                            act.activation(h_hi[0:r, n % 3], hb[0:r, b], ACT.Copy).then_inc(sem("a2"), 1)
                            if n + 1 < N:
                                silu(n + 1)
                            if 0 <= n - n_m < len(pieces):
                                piece_hi(act, raw, pieces, n - n_m)
                            if m == n_m - 1:
                                act.wait_ge(sem("p2"), n + 1)
                                if tb:
                                    act.wait_ge(sem("v5"), TPB * tb)
                                for k in range(2):
                                    act.activation(y[:, 2 * k:2 * k + 2, :], pY[k][:], ACT.Copy).then_inc(sem("a3"), 1)

                    @block.gpsimd
                    def _(pool):
                        ch = Chain(pool, sem("gp"))
                        for t in range(NT):
                            pool.wait_ge(sem("v4"), t + 1)
                            pool_rsqrt(pool, ch, rs[:, t:t + 1], mv[:, t, 1:2], LN_EPS).then_inc(sem("g1"), 1)

                    @block.vector
                    def _(dve):
                        ch = Chain(dve, sem("dv"))

                        def hidden(n):
                            b, m = n % 2, n % n_m
                            r = rows[m]
                            dve.wait_ge(sem("a1"), n + 1)
                            if n >= 2:
                                dve.wait_ge(sem("a2"), n - 1)
                                dve.wait_ge(sem("v3"), n - 1)
                            if u_scale is not None:
                                dve.scalar_tensor_tensor(out=hb[0:r, b], in0=pU[b][0:r, :], scalar=u_scale[0:r, m:m + 1],
                                                         in1=sgb[0:r, b], op0=ALU.mult, op1=ALU.mult).then_inc(sem("v1"), 1)
                            else:
                                dve.tensor_tensor(hb[0:r, b], pU[b][0:r, :], sgb[0:r, b], ALU.mult).then_inc(sem("v1"), 1)
                            if routed(n):
                                dve.wait_ge(sem("v1"), n + 1)
                                dve.tensor_tensor(hb[0:r, b], pW[(n_scaled(n) - 1) % 2][0:r, :], hb[0:r, b], ALU.mult).then_inc(sem("v2"), 1)

                        def block_out(tb):
                            dve.wait_ge(sem("a3"), 2 * tb + 2)
                            for q in range(TPB + 2):
                                if q < TPB:
                                    measure(dve, ch, tb * TPB + q, y[:, q, :], "v4")
                                if q >= 2:
                                    add_normed(dve, ch, tb * TPB + q - 2, y[:, q - 2, :], tmp[:, q % 2])

                        hidden(0)
                        for n in range(N):
                            tb, m = divmod(n, n_m)
                            b, r = n % 2, rows[m]
                            dve.wait_ge(sem("a2"), n + 1)
                            if n >= 3:
                                dve.wait_ge(sem("p2"), n - 2)
                            dve.tensor_tensor(h_lo[0:r, n % 3], hb[0:r, b], f(h_hi[0:r, n % 3]), ALU.subtract).then_inc(sem("v3"), 1)
                            if n + 1 < N:
                                hidden(n + 1)
                            if 0 <= n - n_m < len(pieces):
                                piece_lo(dve, raw, pieces, n - n_m)
                            if m == 1 and tb:
                                block_out(tb - 1)
                        block_out(NB - 1)

                    @block.sync
                    def _(sp):
                        load_pieces(sp, raw, pieces)
                        if store:
                            for tb in range(NB):
                                sp.wait_ge(sem("v6"), TPB * (tb + 1))
                                sp.dma_start(out[:, tb * TPB:(tb + 1) * TPB, :], X[:, tb * TPB:(tb + 1) * TPB, :]).then_inc(sem("dma_out"), 16)
                            sp.wait_ge(sem("dma_out"), 16 * NB)
                if not store:
                    phase_end()

        lru_w = whole.enter_context(ExitStack())
        wi_ = [sb(lru_w, f"wi_{k}", [P, KD, D], F32R) for k in range(2)]
        wr_ = [sb(lru_w, f"wr_{k}", [P, KD, D], F32R) for k in range(2)]
        xT = [sb(lru_w, f"xT{k}", [P, KD, T], F32R) for k in range(2)]
        with ExitStack() as moe:
            gwr = sb(moe, "gwr", [P, KD, P])
            gw_ = [sb(moe, f"gw_{k}", [P, KD, P], F32R) for k in range(2)]
            selb = sb(moe, "selb", [3 * NE, FR], BF16)
            wT = sb(moe, "wT", [3 * NE, T], BF16)
            tri = sb(moe, "tri", [P, NE, NE])
            turned_norm(*xT)
            with ExitStack() as c:
                self32 = sb(c, "self32", [3 * NE, FR])
                lgT = sb(c, "lgT", [NE, T])
                L = sb(c, "L", [P, NT, NE])
                S = sb(c, "S", [P, NT, NE])
                M = sb(c, "M", [P, NT, NE])
                R = sb(c, "R", [P, NT, NE])
                small = sb(c, "small", [P, 3, NT])
                G = sb(c, "G", [P, 2, NT, 4])
                cmp1 = sb(c, "cmp1", [P, NT, NE, NE])
                cmp2 = sb(c, "cmp2", [P, NT, NE, NE])
                w3 = sb(c, "w3", [P, NT, 3 * NE], BF16)
                pg = [ps(c, f"pg{b}", [P, BT]) for b in range(2)]
                pr_ = ps(c, "pr_", [P, 512])
                pw = [ps(c, f"pw{b}", [P, 1024], BF16) for b in range(2)]
                with nc.Block() as block:

                    @block.sync
                    def _(sp):
                        sp.dma_start(self32[:], sel).then_inc(sem("dma_w"), 16)
                        sp.wait_ge(sem("gp"), 1)
                        sp.dma_start(gwr[:, :, 0:NE], gw).then_inc(sem("dma_w2"), 16)

                    @block.gpsimd
                    def _(pool):
                        pool.memset(gwr[:], 0.0).then_inc(sem("gp"), 1)
                        pool.memset(tri[:], 1.0).then_inc(sem("gp"), 1)
                        pool.wait_ge(sem("gp"), 2)
                        pool.affine_select(out=tri[:], in_=tri[:], compare_op=ALU.is_gt, fill=0.0, base=0,
                                           pattern=[[1, NE], [-1, NE]], channel_multiplier=0).then_inc(sem("g1"), 1)
                        pool.wait_ge(sem("dma_w"), 16)
                        pool.tensor_copy(selb[:], self32[:]).then_inc(sem("g2"), 1)

                    @block.scalar
                    def _(act):
                        act.wait_ge(sem("dma_w2"), 16)
                        act.activation(gw_[0][:], gwr[:], ACT.Copy).then_inc(sem("a1"), 1)
                        for tb in range(NB):
                            act.wait_ge(sem("p1"), tb + 1)
                            act.activation(lgT[:, tb * BT:(tb + 1) * BT], pg[tb % 2][0:NE, :], ACT.Copy).then_inc(sem("a2"), 1)
                        act.wait_ge(sem("v2"), 1)
                        act.activation(S[:], S[:], ACT.Exp).then_inc(sem("a3"), 1)
                        for b in range(2):
                            act.wait_ge(sem("p3"), b + 1)
                            act.activation(wT[:, b * 1024:(b + 1) * 1024], pw[b][0:3 * NE, :], ACT.Copy).then_inc(sem("a4"), 1)

                    @block.tensor
                    def _(pe):
                        pe.wait_ge(sem("v1"), 1)
                        for tb in range(NB):
                            if tb >= 2:
                                pe.wait_ge(sem("a2"), tb - 1)
                            q = 0
                            for k in range(KD):
                                for i, j in ((0, 0), (0, 1), (1, 0)):
                                    mm = pe.matmul(pg[tb % 2][:], gw_[i][:, k, :], xT[j][:, k, tb * BT:(tb + 1) * BT], start=(q == 0), stop=(q == 5))
                                    q += 1
                            mm.then_inc(sem("p1"), 1)
                        pe.wait_ge(sem("a2"), NB)
                        for t in range(NT):
                            mm = pe.transpose(pr_[:, t * NE:(t + 1) * NE], lgT[:, t * P:(t + 1) * P], ident[0:NE, 0:NE])
                        mm.then_inc(sem("p2"), 1)
                        pe.wait_ge(sem("v3"), 1)
                        for b in range(2):
                            for t in range(8):
                                mm = pe.transpose(pw[b][0:3 * NE, t * P:(t + 1) * P], w3[:, 8 * b + t, :], identb[:])
                            mm.then_inc(sem("p3"), 1)

                    @block.vector
                    def _(dve):
                        ch = Chain(dve, sem("dv"))

                        def step(ins):
                            ch.inc(ins)
                            ch.wait()

                        def wide(ap, n):
                            return ap.unsqueeze(3).to_broadcast([P, NT, n, n])

                        def ranks(dst, src, n):
                            mine, other = wide(src, n), src.unsqueeze(2).to_broadcast([P, NT, n, n])
                            a, b = cmp1[:, :, 0:n, 0:n], cmp2[:, :, 0:n, 0:n]
                            ch.inc(dve.tensor_tensor(a, other, mine, ALU.is_gt))
                            step(dve.tensor_tensor(b, other, mine, ALU.is_equal))
                            step(dve.tensor_tensor(b, b, tri[:, 0:n, 0:n].unsqueeze(1).to_broadcast([P, NT, n, n]), ALU.mult))
                            step(dve.tensor_tensor(a, a, b, ALU.add))
                            step(dve.tensor_reduce(dst, a, AX.X, ALU.add))

                        def over(ap, n=NE):
                            return ap.unsqueeze(2).to_broadcast([P, NT, n])

                        dve.wait_ge(sem("a1"), 1)
                        dve.tensor_tensor(gw_[1][:], gwr[:], f(gw_[0][:]), ALU.subtract).then_inc(sem("v1"), 1)
                        dve.wait_ge(sem("p2"), 1)
                        step(dve.tensor_copy(L[:], pr_[:, 0:NT * NE].rearrange("p (t e) -> p t e", e=NE)))
                        step(dve.tensor_reduce(small[:, 0, :], L[:], AX.X, ALU.max))
                        dve.tensor_tensor(S[:], L[:], over(small[:, 0, :]), ALU.subtract).then_inc(sem("v2"), 1)
                        dve.wait_ge(sem("a3"), 1)
                        step(dve.tensor_reduce(small[:, 1, :], S[:], AX.X, ALU.add))
                        step(dve.reciprocal(small[:, 2, :], small[:, 1, :]))
                        step(dve.tensor_tensor(S[:], S[:], over(small[:, 2, :]), ALU.mult))
                        step(dve.tensor_reduce(G[:, 0], S[:].rearrange("p t (g e) -> p t g e", e=2), AX.X, ALU.max))
                        dve.wait_ge(sem("g1"), 1)
                        ranks(G[:, 1], G[:, 0], 4)
                        step(dve.tensor_scalar(G[:, 1], G[:, 1], 1.5, None, ALU.is_lt))
                        step(dve.tensor_tensor(M[:].rearrange("p t (g e) -> p t g e", e=2), S[:].rearrange("p t (g e) -> p t g e", e=2),
                                               G[:, 1].unsqueeze(3).to_broadcast([P, NT, 4, 2]), ALU.mult))
                        ranks(R[:], M[:], NE)
                        step(dve.tensor_scalar(R[:], R[:], 1.5, None, ALU.is_lt))
                        step(dve.tensor_tensor(M[:], M[:], R[:], ALU.mult))
                        step(dve.tensor_copy(w3[:, :, 0:NE], M[:]))
                        step(dve.tensor_tensor(M[:], M[:], w3[:, :, 0:NE], ALU.subtract))
                        step(dve.tensor_copy(w3[:, :, NE:2 * NE], M[:]))
                        step(dve.tensor_tensor(M[:], M[:], w3[:, :, NE:2 * NE], ALU.subtract))
                        dve.tensor_copy(w3[:, :, 2 * NE:3 * NE], M[:]).then_inc(sem("v3"), 1)
                phase_end()
            gated_ffn(xT, wg_, wu_, wd_, NFM, [P] * 13 + [FM - 13 * P], n_routed=FR // P, selb=selb, wT=wT,
                      pieces=pieces_of(((l_in, wi_[0][:], wi_[1][:]), (l_gate, wr_[0][:], wr_[1][:])), 1))

        weights.close()
        qg_ = [sbr(weights, f"qg_{k}", [P, KD, NFQ * P], F32R) for k in range(2)]
        qu_ = [sbr(weights, f"qu_{k}", [P, KD, NFQ * P], F32R) for k in range(2)]
        qd_ = [sbr(weights, f"qd_{k}", [P, NFQ, D], F32R) for k in range(2)]
        scg = sbr(weights, "scg", [P, NFQ])
        scu = sbr(weights, "scu", [P, NFQ])
        sdb = sbr(weights, "sdb", [P, D])
        quant = (qg_, qu_, qd_)
        turned_norm(*xT)
        with ExitStack() as lru:
            with ExitStack() as c:
                si = sb(c, "si", [P, KD, T])
                al = sb(c, "al", [P, KD, T])
                be = sb(c, "be", [P, KD, T])
                xs = sb(c, "xs", [P, KD, T])
                lb = sb(c, "lb", [P, 2, KD])
                lam = sb(c, "lam", [P, KD])
                z = sb(c, "z", [P, 6, KD])
                tmp = sb(c, "tmp", [P, 4, D])
                eps = sb(c, "eps", [P, 1])
                integers = [sb(c, "intg", [P, KD, NFQ * P], I32), sb(c, "intu", [P, KD, NFQ * P], I32), sb(c, "intd", [P, NFQ, D], I32)]
                pg = [ps(c, f"pg{b}", [P, BT]) for b in range(4)]
                py = [ps(c, f"py{b}", [P, 512]) for b in range(4)]
                gates = [(tb, e, w) for e in range(KD) for tb in range(NB) for w in range(2)]
                with nc.Block() as block:

                    @block.sync
                    def _(sp):
                        sp.dma_start(lb[:], l_b).then_inc(sem("dma_w"), 16)
                        sp.dma_start(lam[:], l_lam).then_inc(sem("dma_w"), 16)
                        for i, (src, dst) in enumerate(zip((qg, qu, qd), integers)):
                            sp.dma_start(dst[:], src).then_inc(sem(f"w_in{i}"), 16)
                        sp.dma_start(sdb[:], sd.partition_broadcast(P)).then_inc(sem("w_in3"), 16)
                        sp.dma_start(scg[:], sg).then_inc(sem("dma_w2"), 16)
                        sp.dma_start(scu[:], su).then_inc(sem("dma_w2"), 16)
                        sp.wait_ge(sem("dma_w2"), 32)

                    @block.tensor
                    def _(pe):
                        for n, (tb, e, w) in enumerate(gates):
                            if n >= 4:
                                pe.wait_ge(sem("a1"), n - 3)
                            wts = (wi_, wr_)[w]
                            q = 0
                            for k in range(KD):
                                for i, j in ((0, 0), (0, 1), (1, 0)):
                                    mm = pe.matmul(pg[n % 4][:], wts[i][:, k, e * P:(e + 1) * P], xT[j][:, k, tb * BT:(tb + 1) * BT],
                                                   start=(q == 0), stop=(q == 5))
                                    q += 1
                            mm.then_inc(sem("p1"), 1)
                        for t in range(NT):
                            if t == 0:
                                pe.wait_ge(sem("v2"), KD)
                            if t >= 4:
                                pe.wait_ge(sem("v5"), t - 3)
                            for k in range(KD):
                                mm = pe.transpose(py[t % 4][:, k * P:(k + 1) * P], xs[:, k, t * P:(t + 1) * P], ident[:])
                            mm.then_inc(sem("p2"), 1)

                    @block.scalar
                    def _(act):
                        act.wait_ge(sem("dma_w"), 32)
                        act.wait_ge(sem("v3"), 1)
                        act.activation(z[:, 0, :], z[:, 1, :], ACT.Exp, scale=-1.0).then_inc(sem("a2"), 1)
                        for n, (tb, e, w) in enumerate(gates):
                            act.wait_ge(sem("p1"), n + 1)
                            dst = (si, al)[w][:, e, tb * BT:(tb + 1) * BT]
                            act.activation(dst, pg[n % 4][:], ACT.Sigmoid, bias=lb[:, w, e:e + 1]).then_inc(sem("a1"), 1)
                            if n in (11, 13, 15):
                                k = (n - 11) // 2
                                act.wait_ge(sem("w_float"), k + 1)
                                act.activation(quant[k][0][:], f(integers[k][:]), ACT.Copy).then_inc(sem("w_hi"), 1)
                        act.wait_ge(sem("v3"), 2)
                        act.wait_ge(sem("a1"), len(gates))
                        for e in range(KD):
                            act.activation(al[:, e, :], al[:, e, :], ACT.Exp, scale=z[:, 5, e:e + 1]).then_inc(sem("a3"), 1)
                        for e in range(KD):
                            act.wait_ge(sem("v1"), e + 1)
                            act.activation(be[:, e, :], be[:, e, :], ACT.Sqrt, bias=eps[:]).then_inc(sem("a4"), 1)
                        for t in range(NT):
                            act.wait_ge(sem("g1"), t + 1)
                            if t >= 4:
                                act.wait_ge(sem("v6"), t - 3)
                            act.activation(tmp[:, t % 4], py[t % 4][:, 0:D], ACT.Identity, bias=nmr[:, t:t + 1],
                                           scale=rs[:, t:t + 1]).then_inc(sem("v5"), 1)

                    @block.gpsimd
                    def _(pool):
                        pool.memset(eps[:], 1e-6).then_inc(sem("g2"), 1)
                        ch = Chain(pool, sem("gp"))
                        for k, raw in enumerate(integers):
                            pool.wait_ge(sem(f"w_in{k}"), 16)
                            less = pool.tensor_scalar(f(raw[:]), raw[:], -ZERO_POINT, None, ALU.add)
                            if k == 2:
                                ch.inc(less)
                                ch.wait()
                                pool.wait_ge(sem("w_in3"), 16)
                                less = pool.tensor_tensor(f(raw[:]), f(raw[:]), sdb[:].unsqueeze(1).to_broadcast([P, NFQ, D]), ALU.mult)
                            less.then_inc(sem("w_float"), 1)
                        for k, (raw, w) in enumerate(zip(integers, quant)):
                            pool.wait_ge(sem("w_hi"), k + 1)
                            pool.tensor_tensor(w[1][:], f(raw[:]), f(w[0][:]), ALU.subtract).then_inc(sem("w_lo"), 1)
                        for t in range(NT):
                            pool.wait_ge(sem("v4"), t + 1)
                            ch.inc(pool_rsqrt(pool, ch, rs[:, t:t + 1], mv[:, t, 1:2], LN_EPS))
                            ch.wait()
                            pool.tensor_scalar(nmr[:, t:t + 1], mv[:, t, 0:1], rs[:, t:t + 1], -1.0, ALU.mult, ALU.mult).then_inc(sem("g1"), 1)

                    @block.vector
                    def _(dve):
                        ch = Chain(dve, sem("dv"))

                        def step(ins):
                            ch.inc(ins)
                            ch.wait()

                        dve.wait_ge(sem("dma_w"), 32)
                        step(dve.tensor_scalar(z[:, 1, :], lam[:], -1.0, None, ALU.mult))
                        dve.tensor_tensor(z[:, 1, :], z[:, 1, :], lam[:], ALU.max).then_inc(sem("v3"), 1)
                        dve.wait_ge(sem("a2"), 1)
                        step(dve.tensor_scalar(z[:, 2, :], z[:, 0, :], 2.0, None, ALU.add))
                        step(dve.reciprocal(z[:, 2, :], z[:, 2, :]))
                        step(dve.tensor_tensor(z[:, 2, :], z[:, 2, :], z[:, 0, :], ALU.mult))
                        step(dve.tensor_tensor(z[:, 3, :], z[:, 2, :], z[:, 2, :], ALU.mult))
                        step(dve.tensor_scalar(z[:, 4, :], z[:, 3, :], 1.0 / (2 * LOG1P_TERMS + 1), None, ALU.mult))
                        for k in range(LOG1P_TERMS - 1, 0, -1):
                            step(dve.scalar_tensor_tensor(out=z[:, 4, :], in0=z[:, 4, :], scalar=1.0 / (2 * k + 1), in1=z[:, 3, :],
                                                          op0=ALU.add, op1=ALU.mult))
                        step(dve.scalar_tensor_tensor(out=z[:, 4, :], in0=z[:, 4, :], scalar=1.0, in1=z[:, 2, :],
                                                      op0=ALU.add, op1=ALU.mult))
                        step(dve.tensor_scalar(z[:, 0, :], lam[:], 0.0, -LRU_C, ALU.max, ALU.mult))
                        dve.scalar_tensor_tensor(out=z[:, 5, :], in0=z[:, 4, :], scalar=-2.0 * LRU_C, in1=z[:, 0, :],
                                                 op0=ALU.mult, op1=ALU.add).then_inc(sem("v3"), 1)
                        for e in range(KD):
                            step(dve.tensor_tensor(xs[:, e, :], f(xT[0][:, e, :]), f(xT[1][:, e, :]), ALU.add))
                        for n, (tb, e, w) in enumerate(gates):
                            if w == 0:
                                ts = slice(tb * BT, (tb + 1) * BT)
                                dve.wait_ge(sem("a1"), n + 1)
                                ch.inc(dve.tensor_tensor(si[:, e, ts], si[:, e, ts], xs[:, e, ts], ALU.mult))
                        for e in range(KD):
                            dve.wait_ge(sem("a3"), e + 1)
                            step(dve.tensor_tensor(be[:, e, :], al[:, e, :], al[:, e, :], ALU.mult))
                            if e == 0:
                                dve.wait_ge(sem("g2"), 1)
                            dve.tensor_scalar(be[:, e, :], be[:, e, :], -1.0, 1.0, ALU.mult, ALU.add).then_inc(sem("v1"), 1)
                        for e in range(KD):
                            dve.wait_ge(sem("a4"), e + 1)
                            step(dve.tensor_tensor(be[:, e, :], be[:, e, :], si[:, e, :], ALU.mult))
                            dve.tensor_tensor_scan(xs[:, e, :], al[:, e, :], be[:, e, :], 0.0, ALU.mult, ALU.add).then_inc(sem("v2"), 1)
                        for t in range(NT + 3):
                            if t < NT:
                                dve.wait_ge(sem("p2"), t + 1)
                                measure(dve, ch, t, py[t % 4][:, 0:D], "v4")
                            if t >= 3:
                                u = t - 3
                                dve.wait_ge(sem("v5"), u + 1)
                                dve.tensor_tensor(X[:, u, :], X[:, u, :], tmp[:, u % 4], ALU.add).then_inc(sem("v6"), 1)
                phase_end()

        turned_norm(*xT)
        gated_ffn(xT, qg_, qu_, qd_, NFQ, [P] * NFQ, g_scale=scg, u_scale=scu, store=True)


def kernel(**inputs):
    import concourse.bacc as bacc
    from concourse.bass_utils import run_bass_kernel_spmd

    a = {k: np.asarray(v) for k, v in inputs.items()}

    def tiles(w, n=P):
        r = -w.shape[0] % n
        w = np.concatenate([w, np.zeros((r,) + w.shape[1:], w.dtype)]) if r else w
        return w.reshape(-1, n, *w.shape[1:]).swapaxes(0, 1)

    w_qb = a["L0_attn_w_qb"].reshape(H, DN + DR, QL)
    w_kvb = a["L0_attn_w_kvb"].reshape(H, DN + DV, KVL)
    inv = np.float32(1.0) / np.float32(10000.0) ** (np.arange(0, DR, 2, dtype=np.float32) / np.float32(DR))
    ang = np.outer(np.arange(T, dtype=np.float32), inv).astype(np.float32)
    cos, sin = np.cos(ang), np.sin(ang)
    unit = np.arange(FR)
    sel = np.tile((unit[None, :] // FE == np.arange(NE)[:, None]).astype(np.float32), (3, 1))
    up = lambda r, s: np.concatenate([r.reshape(FR, D), s]).T
    padded = lambda w: np.concatenate([w, np.zeros((NFQ * P - FQ,) + w.shape[1:], w.dtype)])
    arrays = {
        "x": tiles(a["L0_attn_hidden_states"].reshape(T, D)),
        "w_lat": tiles(np.concatenate([a["L0_attn_w_qa"], a["L0_attn_w_kva"]]).T),
        "w_qn": w_qb[:, :DN].swapaxes(0, 1),
        "w_qpe": w_qb[:, DN:].transpose(2, 0, 1),
        "w_kn": w_kvb[:, :DN].swapaxes(0, 1),
        "w_v": w_kvb[:, DN:].swapaxes(0, 1),
        "w_o": tiles(a["L0_attn_w_o"].T),
        "q_ln": a["L0_attn_q_a_ln_w"][:, None],
        "kv_ln": a["L0_attn_kv_a_ln_w"],
        "cos2": tiles(np.concatenate([cos, cos], 1)),
        "sin2": tiles(np.concatenate([-sin, sin], 1)),
        "gw": tiles(a["L0_ffn_gate_weight"].T),
        "wg": tiles(up(a["L0_ffn_gate_w"], a["L0_ffn_sh_gate_w"])),
        "wu": tiles(up(a["L0_ffn_up_w"], a["L0_ffn_sh_up_w"])),
        "wd": tiles(np.concatenate([a["L0_ffn_down_w"].transpose(0, 2, 1).reshape(FR, D), a["L0_ffn_sh_down_w"].T])),
        "sel": sel,
        "l_in": tiles(a["L1_attn_W_in"].T),
        "l_gate": tiles(a["L1_attn_W_gate"].T),
        "l_b": tiles(np.stack([a["L1_attn_b_in"], a["L1_attn_b_gate"]], 1)).swapaxes(1, 2),
        "l_lam": tiles(a["L1_attn_forget_lambda"]),
        "qg": tiles(padded(a["L1_ffn_wq_gate"]).T),
        "qu": tiles(padded(a["L1_ffn_wq_up"]).T),
        "qd": tiles(a["L1_ffn_wq_down"].T),
        "sg": tiles(a["L1_ffn_s_gate"]),
        "su": tiles(a["L1_ffn_s_up"]),
        "sd": a["L1_ffn_s_down"],
    }
    nc = bacc.Bacc("TRN2", target_bir_lowering=False, num_devices=1)
    arrays = {f"in_{k}": np.ascontiguousarray(v) for k, v in arrays.items()}
    aps = {k[3:]: nc.dram_tensor(k, v.shape, mybir.dt.from_np(v.dtype), kind="ExternalInput").ap() for k, v in arrays.items()}
    out = nc.dram_tensor("out", (P, NT, D), F32, kind="ExternalOutput").ap()
    build(nc, **aps, out=out)
    r = run_bass_kernel_spmd(nc, [arrays], core_ids=[0])
    return r.results[0]["out"].swapaxes(0, 1).reshape(1, T, D)
```
